# Optimizing a Trainium2 kernel written in Bass

```python
import numpy as np
import jax
import jax.numpy as jnp

def _softmax(x, axis=-1):
    return jax.nn.softmax(x, axis=axis)

def _gelu(x):
    return jax.nn.gelu(x, approximate=True)

def _silu(x):
    return jax.nn.silu(x)

def _sigmoid(x):
    return jax.nn.sigmoid(x)

def _layernorm(x, axis=-1, eps=1e-05):
    m = jnp.mean(x, axis=axis, keepdims=True)
    v = jnp.var(x, axis=axis, keepdims=True)
    return (x - m) / jnp.sqrt(v + eps)

def _scatter_add(tgt, idx, src, axis=0):
    return tgt.at[idx].add(src)

def _segment_sum(src, seg, n):
    return jax.ops.segment_sum(src, seg, n)
kernel_name = 'mk_macaron_d1_jaxref_r8_862635'

def setup_inputs(seed: int=0):
    np.random.seed(seed)
    _w = jnp.asarray

    def _L0_attn_setup():
        import jax, jax.numpy as jnp
        import numpy as np
        HIDDEN = 128
        HEADS = 16
        HEAD_DIM = HIDDEN // HEADS
        SCALE = HEAD_DIM ** (-0.5)
        EPS = 1e-06
        key = jax.random.key(seed)
        k1, k2, k3, k4, k5 = jax.random.split(key, 5)
        B, S = (2, 256)
        std = HIDDEN ** (-0.5)
        return {'x': jax.random.normal(k1, (B, S, HIDDEN), dtype=jnp.float32), 'Wq': jax.random.normal(k2, (HIDDEN, HIDDEN), dtype=jnp.float32) * std, 'Wk': jax.random.normal(k3, (HIDDEN, HIDDEN), dtype=jnp.float32) * std, 'Wv': jax.random.normal(k4, (HIDDEN, HIDDEN), dtype=jnp.float32) * std, 'Wo': jax.random.normal(k5, (HIDDEN, HIDDEN), dtype=jnp.float32) * std}
    _L0_attn_in = _L0_attn_setup()

    def _L0_ffn_setup():
        import jax, jax.numpy as jnp
        import numpy as np
        DIM = 128
        DEPTH = 6
        HEADS = 16
        DIM_HEAD = 64
        WINDOW = 32
        INNER = HEADS * DIM_HEAD
        DIM_INNER = int(DIM * 4 * 2 / 3)
        QK_SCALE = 8.0

        def shift_tokens(t):
            a, s = jnp.split(t, 2, -1)
            s = jnp.pad(s, ((0, 0), (1, 0), (0, 0)))[:, :-1]
            return jnp.concatenate([a, s], -1)

        def l2norm(t):
            return t / jnp.maximum(jnp.linalg.norm(t, axis=-1, keepdims=True), 1e-12)

        def rotate_half(x):
            x1, x2 = jnp.split(x, 2, -1)
            return jnp.concatenate([-x2, x1], -1)

        def rotary_tables(n):
            half = jnp.arange(0, DIM_HEAD, 2, dtype=jnp.float32)
            inv_freq = 1.0 / 10000.0 ** (half / DIM_HEAD)
            t = jnp.arange(n, dtype=jnp.float32)
            freqs = t[:, None] * inv_freq[None, :]
            freqs = jnp.concatenate([freqs, freqs], -1)
            base_scale = (half + 0.4 * DIM_HEAD) / (1.4 * DIM_HEAD)
            power = (t - n // 2) / (WINDOW // 2)
            scale = base_scale[None, :] ** power[:, None]
            scale = jnp.concatenate([scale, scale], -1)
            return (freqs, scale)

        def local_attention(q, k, v):
            b, h, n, d = q.shape
            w = WINDOW
            nw = n // w
            bq = q.reshape(b, h, nw, w, d)
            bk = k.reshape(b, h, nw, w, d)
            bv = v.reshape(b, h, nw, w, d)

            def look(t):
                p = jnp.pad(t, ((0, 0), (0, 0), (1, 0), (0, 0), (0, 0)))
                return jnp.concatenate([p[:, :, :nw], p[:, :, 1:]], axis=3)
            bk2, bv2 = (look(bk), look(bv))
            seq = jnp.arange(n).reshape(nw, w)
            seq_p = jnp.pad(seq, ((1, 0), (0, 0)), constant_values=-1)
            jt = jnp.concatenate([seq_p[:nw], seq_p[1:]], axis=1)
            it = seq[:, :, None]
            jb = jt[:, None, :]
            mask = (it < jb) | (it > jb + w) | (jb == -1)
            sim = jnp.einsum('bhwie,bhwje->bhwij', bq, bk2) * QK_SCALE
            sim = jnp.where(mask, -jnp.finfo(sim.dtype).max, sim)
            attn = jax.nn.softmax(sim, -1)
            out = jnp.einsum('bhwij,bhwje->bhwie', attn, bv2)
            return out.reshape(b, h, n, d)

        def attn_layer(x, Wqkv, qs, ksc, Wo):
            b, n, _ = x.shape
            qkv = x @ Wqkv
            q, k, v = jnp.split(qkv, 3, -1)
            sh = lambda t: t.reshape(b, n, HEADS, DIM_HEAD).transpose(0, 2, 1, 3)
            q, k, v = (sh(q), sh(k), sh(v))
            q = l2norm(q) * qs
            k = l2norm(k) * ksc
            freqs, scale = rotary_tables(n)
            cos, sin = (jnp.cos(freqs), jnp.sin(freqs))
            q = q * cos * scale + rotate_half(q) * sin * scale
            inv = 1.0 / scale
            k = k * cos * inv + rotate_half(k) * sin * inv
            out = local_attention(q, k, v)
            out = out.transpose(0, 2, 1, 3).reshape(b, n, INNER)
            return out @ Wo

        def ffn_layer(x, g, bln, W1, b1, W2, b2):
            mu = x.mean(-1, keepdims=True)
            var = ((x - mu) ** 2).mean(-1, keepdims=True)
            xn = (x - mu) / jnp.sqrt(var + 1e-05) * g + bln
            hg = xn @ W1 + b1
            a, gate = jnp.split(hg, 2, -1)
            return a * jax.nn.gelu(gate, approximate=False) @ W2 + b2
        key = jax.random.key(seed)
        ks = jax.random.split(key, 8)
        B, N = (2, 256)
        init = lambda k, shape: jax.random.normal(k, shape, jnp.float32) * 0.02
        return {'x': jax.random.normal(ks[0], (B, N, DIM), jnp.float32), 'Wqkv': init(ks[1], (DEPTH, DIM, 3 * INNER)), 'q_scale': jnp.ones((DEPTH, DIM_HEAD), jnp.float32), 'k_scale': jnp.ones((DEPTH, DIM_HEAD), jnp.float32), 'Wo': init(ks[2], (DEPTH, INNER, DIM)), 'ln_g': jnp.ones((DEPTH, DIM), jnp.float32), 'ln_b': jnp.zeros((DEPTH, DIM), jnp.float32), 'W1': init(ks[3], (DEPTH, DIM, 2 * DIM_INNER)), 'b1': jnp.zeros((DEPTH, 2 * DIM_INNER), jnp.float32), 'W2': init(ks[4], (DEPTH, DIM_INNER, DIM)), 'b2': jnp.zeros((DEPTH, DIM), jnp.float32)}
    _L0_ffn_in = _L0_ffn_setup()
    _d = {'L0_attn_x': _L0_attn_in['x'], 'L0_attn_Wq': _L0_attn_in['Wq'], 'L0_attn_Wk': _L0_attn_in['Wk'], 'L0_attn_Wv': _L0_attn_in['Wv'], 'L0_attn_Wo': _L0_attn_in['Wo'], 'L0_ffn_Wqkv': _L0_ffn_in['Wqkv'], 'L0_ffn_q_scale': _L0_ffn_in['q_scale'], 'L0_ffn_k_scale': _L0_ffn_in['k_scale'], 'L0_ffn_Wo': _L0_ffn_in['Wo'], 'L0_ffn_ln_g': _L0_ffn_in['ln_g'], 'L0_ffn_ln_b': _L0_ffn_in['ln_b'], 'L0_ffn_W1': _L0_ffn_in['W1'], 'L0_ffn_b1': _L0_ffn_in['b1'], 'L0_ffn_W2': _L0_ffn_in['W2'], 'L0_ffn_b2': _L0_ffn_in['b2']}
    _x0 = _d['L0_attn_x']
    _d['L0_attn_x'] = jax.random.normal(jax.random.fold_in(jax.random.key(seed), 1), (4, 512, 128), dtype=_x0.dtype)
    del _x0
    return _d

def reference(L0_attn_x, L0_attn_Wq, L0_attn_Wk, L0_attn_Wv, L0_attn_Wo, L0_ffn_Wqkv, L0_ffn_q_scale, L0_ffn_k_scale, L0_ffn_Wo, L0_ffn_ln_g, L0_ffn_ln_b, L0_ffn_W1, L0_ffn_b1, L0_ffn_W2, L0_ffn_b2):

    def _L0_attn_ref(x, Wq, Wk, Wv, Wo):
        import jax, jax.numpy as jnp
        import numpy as np
        HIDDEN = 128
        HEADS = 16
        HEAD_DIM = HIDDEN // HEADS
        SCALE = HEAD_DIM ** (-0.5)
        EPS = 1e-06
        B, S, H = x.shape

        def proj(W):
            y = jnp.einsum('bsh,oh->bso', x, W)
            return y.reshape(B, S, HEADS, HEAD_DIM).transpose(0, 2, 1, 3)
        q, k, v = (proj(Wq), proj(Wk), proj(Wv))
        scores = jnp.einsum('bhqd,bhkd->bhqk', q, k) * SCALE
        w = jax.nn.sigmoid(scores)
        w = w / (w.sum(axis=-1, keepdims=True) + EPS)
        out = jnp.einsum('bhqk,bhkd->bhqd', w, v)
        out = out.transpose(0, 2, 1, 3).reshape(B, S, H)
        return jnp.einsum('bsh,oh->bso', out, Wo)

    def _L0_ffn_ref(x, Wqkv, q_scale, k_scale, Wo, ln_g, ln_b, W1, b1, W2, b2):
        import jax, jax.numpy as jnp
        import numpy as np
        DIM = 128
        DEPTH = 6
        HEADS = 16
        DIM_HEAD = 64
        WINDOW = 32
        INNER = HEADS * DIM_HEAD
        DIM_INNER = int(DIM * 4 * 2 / 3)
        QK_SCALE = 8.0

        def shift_tokens(t):
            a, s = jnp.split(t, 2, -1)
            s = jnp.pad(s, ((0, 0), (1, 0), (0, 0)))[:, :-1]
            return jnp.concatenate([a, s], -1)

        def l2norm(t):
            return t / jnp.maximum(jnp.linalg.norm(t, axis=-1, keepdims=True), 1e-12)

        def rotate_half(x):
            x1, x2 = jnp.split(x, 2, -1)
            return jnp.concatenate([-x2, x1], -1)

        def rotary_tables(n):
            half = jnp.arange(0, DIM_HEAD, 2, dtype=jnp.float32)
            inv_freq = 1.0 / 10000.0 ** (half / DIM_HEAD)
            t = jnp.arange(n, dtype=jnp.float32)
            freqs = t[:, None] * inv_freq[None, :]
            freqs = jnp.concatenate([freqs, freqs], -1)
            base_scale = (half + 0.4 * DIM_HEAD) / (1.4 * DIM_HEAD)
            power = (t - n // 2) / (WINDOW // 2)
            scale = base_scale[None, :] ** power[:, None]
            scale = jnp.concatenate([scale, scale], -1)
            return (freqs, scale)

        def local_attention(q, k, v):
            b, h, n, d = q.shape
            w = WINDOW
            nw = n // w
            bq = q.reshape(b, h, nw, w, d)
            bk = k.reshape(b, h, nw, w, d)
            bv = v.reshape(b, h, nw, w, d)

            def look(t):
                p = jnp.pad(t, ((0, 0), (0, 0), (1, 0), (0, 0), (0, 0)))
                return jnp.concatenate([p[:, :, :nw], p[:, :, 1:]], axis=3)
            bk2, bv2 = (look(bk), look(bv))
            seq = jnp.arange(n).reshape(nw, w)
            seq_p = jnp.pad(seq, ((1, 0), (0, 0)), constant_values=-1)
            jt = jnp.concatenate([seq_p[:nw], seq_p[1:]], axis=1)
            it = seq[:, :, None]
            jb = jt[:, None, :]
            mask = (it < jb) | (it > jb + w) | (jb == -1)
            sim = jnp.einsum('bhwie,bhwje->bhwij', bq, bk2) * QK_SCALE
            sim = jnp.where(mask, -jnp.finfo(sim.dtype).max, sim)
            attn = jax.nn.softmax(sim, -1)
            out = jnp.einsum('bhwij,bhwje->bhwie', attn, bv2)
            return out.reshape(b, h, n, d)

        def attn_layer(x, Wqkv, qs, ksc, Wo):
            b, n, _ = x.shape
            qkv = x @ Wqkv
            q, k, v = jnp.split(qkv, 3, -1)
            sh = lambda t: t.reshape(b, n, HEADS, DIM_HEAD).transpose(0, 2, 1, 3)
            q, k, v = (sh(q), sh(k), sh(v))
            q = l2norm(q) * qs
            k = l2norm(k) * ksc
            freqs, scale = rotary_tables(n)
            cos, sin = (jnp.cos(freqs), jnp.sin(freqs))
            q = q * cos * scale + rotate_half(q) * sin * scale
            inv = 1.0 / scale
            k = k * cos * inv + rotate_half(k) * sin * inv
            out = local_attention(q, k, v)
            out = out.transpose(0, 2, 1, 3).reshape(b, n, INNER)
            return out @ Wo

        def ffn_layer(x, g, bln, W1, b1, W2, b2):
            mu = x.mean(-1, keepdims=True)
            var = ((x - mu) ** 2).mean(-1, keepdims=True)
            xn = (x - mu) / jnp.sqrt(var + 1e-05) * g + bln
            hg = xn @ W1 + b1
            a, gate = jnp.split(hg, 2, -1)
            return a * jax.nn.gelu(gate, approximate=False) @ W2 + b2
        for i in range(DEPTH):
            x = attn_layer(shift_tokens(x), Wqkv[i], q_scale[i], k_scale[i], Wo[i]) + x
            x = ffn_layer(shift_tokens(x), ln_g[i], ln_b[i], W1[i], b1[i], W2[i], b2[i]) + x
        return x
    x = L0_attn_x
    x = x + 0.5 * _L0_ffn_ref(_layernorm(x, axis=-1), L0_ffn_Wqkv, L0_ffn_q_scale, L0_ffn_k_scale, L0_ffn_Wo, L0_ffn_ln_g, L0_ffn_ln_b, L0_ffn_W1, L0_ffn_b1, L0_ffn_W2, L0_ffn_b2)
    x = x + _L0_attn_ref(_layernorm(x, axis=-1), L0_attn_Wq, L0_attn_Wk, L0_attn_Wv, L0_attn_Wo)
    x = x + 0.5 * _L0_ffn_ref(_layernorm(x, axis=-1), L0_ffn_Wqkv, L0_ffn_q_scale, L0_ffn_k_scale, L0_ffn_Wo, L0_ffn_ln_g, L0_ffn_ln_b, L0_ffn_W1, L0_ffn_b1, L0_ffn_W2, L0_ffn_b2)
    return x

_drawn_inputs = setup_inputs


def setup_inputs(seed=0):
    import zlib

    import numpy as np

    out = dict(_drawn_inputs(seed))
    spreads = {'L0_ffn_q_scale': (1.0, 0.6),
     'L0_ffn_k_scale': (1.0, 0.6),
     'L0_ffn_ln_g': (1.0, 0.6),
     'L0_ffn_ln_b': (0.0, 0.8),
     'L0_ffn_b1': (0.0, 0.8),
     'L0_ffn_b2': (0.0, 0.1)}
    factors = {'L0_ffn_W1': 3.143, 'L0_ffn_W2': 3.073, 'L0_attn_Wq': 4.68, 'L0_attn_Wk': 4.857}
    for name, (base, spread) in spreads.items():
        noise = np.random.default_rng([zlib.crc32(name.encode()), seed]).standard_normal(out[name].shape)
        drawn = base * np.exp(spread * noise) if base else spread * noise
        out[name] = jnp.asarray(drawn.astype(out[name].dtype))
    for name, factor in factors.items():
        out[name] = (out[name] * factor).astype(out[name].dtype)
    return out
```

```python
import numpy as np
import concourse.bass as bass
from concourse import mybir
from contextlib import ExitStack

F32 = mybir.dt.float32
F16 = mybir.dt.float16
BF16 = mybir.dt.bfloat16
ALU = mybir.AluOpType
ACT = mybir.ActivationFunctionType
AX = mybir.AxisListType

P = 128
DIM = 128
BATCHES, SEQ = 4, 512
TOKENS = BATCHES * SEQ
DEPTH = 6
HEADS, DH, WIN = 16, 64, 32
INNER = HEADS * DH
PAIRS = HEADS // 2
TILES = SEQ // P
WPT = P // WIN
KEYS = 2 * WIN
CH = 512
HPC = CH // DH
W_SCALE = 64.0
NORM_FLOOR = (1e-12 * W_SCALE) ** 2
MASKED = -1e30
HID = int(DIM * 4 * 2 / 3)
FCH = [(0, 128), (128, 128), (256, HID - 256)]
LN_EPS = 1e-5
GH, GD = 16, 8
HPG = 4
GROUPS = GH // HPG
SIG_EPS = 1e-6

LAYER_TILES = BATCHES * TILES
TILE_LEAD, BATCH_LEAD, LAYER_LEAD = 4, 4, 1
TR_LEAD = 2


def tile_done(T, j=0, per=1):
    return (T + TILE_LEAD) * per + (j + 1)


def batch_done(B, j=0, per=1):
    return (B + BATCH_LEAD) * per + (j + 1)


def layer_done(L, j=0, per=1):
    return (L + LAYER_LEAD) * per + (j + 1)


def build(nc, x_in, gWq, gWk, gWv, gWo, Wqkv, q_scale, k_scale, Wo, ln_g, ln_b, W1, b1, W2, b2,
          rope_in, ident_in, mask_in, slot_in, sel_in, out):
    ctx = ExitStack()
    with ctx:
        def sb(name, shape, dt=F32):
            return ctx.enter_context(nc.sbuf_tensor(name, shape, dt))

        ident = sb("ident", [P, P])
        identb = sb("identb", [P, P], BF16)
        maskf = sb("maskf", [P, 2, KEYS])
        maskb = sb("maskb", [P, 2, KEYS], BF16)
        mean_w = sb("mean_w", [P, P])
        ones_w = sb("ones_w", [P, P])
        half_neg = sb("half_neg", [P, HPC])
        rope = sb("rope", [P, TILES, 4, DH])
        slot = sb("slot", [P, 2])
        sel = sb("sel", [P, 2, GROUPS, P])
        resid = sb("resid", [P, BATCHES, SEQ])
        xs = sb("xs", [P, BATCHES, SEQ])
        w_stage = sb("w_stage", [P, 3 * INNER])
        w_hi = sb("w_hi", [P, 3 * INNER], F16)
        w_lo = sb("w_lo", [P, 3 * INNER], F16)
        wo_sb = sb("wo_sb", [P, PAIRS, DIM])
        w1_sb = sb("w1_sb", [P, 2 * HID])
        w2_sb = sb("w2_sb", [P, 3, DIM])
        b1_sb = sb("b1_sb", [P, 2, 3])
        vec = sb("vec", [P, 3])
        qks = sb("qks", [P, 4, DH])
        table = sb("table", [P, TILES, 4, DH])
        in_hi = sb("in_hi", [P, WIN + SEQ], F16)
        in_lo = sb("in_lo", [P, WIN + SEQ], F16)
        sq = sb("sq", [P, 2, CH])
        n2 = sb("n2", [P, 2, HPC])
        n2f = sb("n2f", [P, 2, HPC])
        rn = sb("rn", [P, 2, HPC])
        t1 = sb("t1", [P, 2, CH])
        t2 = sb("t2", [P, 2, CH])
        rot = sb("rot", [P, 2, CH])
        qkn = sb("qkn", [P, 2, 4, CH])
        qT = sb("qT", [P, 2, PAIRS, P])
        kT = sb("kT", [P, 2, PAIRS, WIN + P])
        vw = sb("vw", [P, 2, WPT, CH])
        smax = sb("smax", [P, 2, HPC])
        prob = sb("prob", [P, 2, PAIRS, 2, KEYS])
        psumr = sb("psumr", [P, 2, HEADS])
        rsum = sb("rsum", [P, 2, HEADS])
        pT = sb("pT", [P, PAIRS, P])
        on = sb("on", [P, PAIRS, 2, DH])
        oT = sb("oT", [P, PAIRS, SEQ])
        f_in = sb("f_in", [P, SEQ])
        xc = sb("xc", [P, SEQ])
        sqd = sb("sqd", [P, SEQ])
        veps = sb("veps", [P, TILES])
        rstd = sb("rstd", [P, TILES])
        diag = sb("diag", [P, TILES, P])
        xn = sb("xn", [P, SEQ])
        xg = sb("xg", [P, SEQ])
        gel = sb("gel", [P, 2, SEQ])
        hid = sb("hid", [P, 3, SEQ])

        ps = [ctx.enter_context(nc.psum_tensor(f"ps{i}", [P, 512], F32)) for i in range(8)]
        proj, tr, sc, ov = ps[0:2], ps[2:4], ps[4:6], ps[6:8]

        def sem(name):
            return ctx.enter_context(nc.semaphore(name))

        loaded = sem("loaded")
        const_ready = sem("const_ready")
        tile_sems = {}

        def tsem(name, per):
            s = sem(name)
            tile_sems[name] = (s, per * TILE_LEAD)
            return s

        def bsem(name, per=1):
            s = sem(name)
            tile_sems[name] = (s, per * BATCH_LEAD)
            return s

        def lsem(name, credit):
            s = sem(name)
            tile_sems[name] = (s, credit)
            return s

        pe_qk = tsem("pe_qk", 4)
        pe_v = tsem("pe_v", 4)
        pe_tqk = tsem("pe_tqk", 4)
        pe_s = tsem("pe_s", 1)
        pe_tp = tsem("pe_tp", 2)
        pe_pv = tsem("pe_pv", 2)
        pe_to = tsem("pe_to", 2)
        act_sq = tsem("act_sq", 4)
        act_v = tsem("act_v", 4)
        act_tr = lsem("act_tr", TR_LEAD)
        act_exp = tsem("act_exp", 1)
        dve_n2 = tsem("dve_n2", 4)
        dve_rot = tsem("dve_rot", 4)
        dve_qkn = tsem("dve_qkn", 4)
        dve_max = tsem("dve_max", 2)
        dve_sub = tsem("dve_sub", 2)
        dve_sum = tsem("dve_sum", 1)
        dve_rs = tsem("dve_rs", 1)
        dve_on = tsem("dve_on", 2)
        pool_r = tsem("pool_r", 8)
        pool_add = tsem("pool_add", 4)
        pool_carry = tsem("pool_carry", 1)
        act_in = bsem("act_in", 2)
        dve_in = bsem("dve_in", 2)
        pe_wo = bsem("pe_wo")
        dve_x1 = bsem("dve_x1")
        act_fin = bsem("act_fin", 2)
        pe_mean = bsem("pe_mean")
        dve_xc = bsem("dve_xc")
        act_sqd = bsem("act_sqd")
        pe_var = bsem("pe_var")
        dve_veps = bsem("dve_veps")
        pool_rstd = bsem("pool_rstd")
        dve_diag = bsem("dve_diag")
        pe_rep = bsem("pe_rep")
        dve_xn = bsem("dve_xn")
        act_xg = bsem("act_xg")
        pe_gate = bsem("pe_gate", 3)
        pe_up = bsem("pe_up", 3)
        act_gelu = bsem("act_gelu", 3)
        dve_hid = bsem("dve_hid", 3)
        pe_w2 = bsem("pe_w2")
        dve_x2 = bsem("dve_x2")
        w_loaded = lsem("w_loaded", 16)
        f_loaded = lsem("f_loaded", 0)
        t_loaded = lsem("t_loaded", 0)
        act_whi = lsem("act_whi", 6)
        dve_wlo = lsem("dve_wlo", 6)
        dve_tab = lsem("dve_tab", TILES)

        passed = {}

        def wait_apart(eng, semaphore, value):
            eng.wait_ge(semaphore, value)
            eng.sem_inc(passed[eng], 1)

        x_flat = x_in.rearrange("b (t p) d -> p (b t) d", p=P)
        n_x = BATCHES * TILES
        xtok = vw[:, :, :, :].rearrange("p a w c -> p (a w c)")[:, 0:n_x * DIM].rearrange("p (t d) -> p t d", d=DIM)
        gw_in = rope_tmp = w_stage[:, 0:4 * P].rearrange("p (k c) -> p k c", k=4)
        gwT = sb("gwT", [P, 4, P])
        gw_qk = sb("gw_qk", [P, 2, GROUPS, HPG, 4, GD])
        passed_pe, passed_pool = sem("passed_pe"), sem("passed_pool")
        init_pe, init_act = sem("init_pe"), sem("init_act")

        with nc.Block() as block:
            @block.sync
            def _(sp):
                for s, credit in tile_sems.values():
                    if credit:
                        sp.sem_inc(s, credit)
                sp.dma_start(ident[:, :], ident_in).then_inc(loaded, 16)
                sp.dma_start(xtok, x_flat).then_inc(loaded, 16)
                for i, w in enumerate((gWq, gWk, gWv, gWo)):
                    sp.dma_start(gw_in[:, i, :], w).then_inc(loaded, 16)
                sp.dma_start(maskf[:, :, :], mask_in).then_inc(loaded, 16)
                sp.dma_start(rope[:, :, :, :], rope_in.rearrange("(t p) k d -> p t k d", p=P)).then_inc(loaded, 16)
                sp.dma_start(slot[:, :], slot_in).then_inc(loaded, 16)
                sp.dma_start(sel[:, :, :, :], sel_in).then_inc(loaded, 16)

            @block.gpsimd
            def _(pool):
                pool.memset(mean_w[:, :], 1.0 / DIM)
                pool.memset(ones_w[:, :], 1.0)
                pool.memset(half_neg[:, :], -0.5)
                pool.memset(in_hi[:, 0:WIN + 1], 0.0)
                pool.memset(in_lo[:, 0:WIN + 1], 0.0)
                pool.memset(f_in[:, 0:1], 0.0).then_inc(const_ready, 1)

            @block.vector
            def _(dve):
                dve.wait_ge(loaded, 160)
                dve.tensor_copy(identb[:, :], ident[:, :])
                dve.tensor_copy(maskb[:, :, :], maskf[:, :, :]).then_inc(const_ready, 1)

            @block.tensor
            def _(pe):
                pe.wait_ge(loaded, 160)
                for g in range(4):
                    if g >= 2:
                        pe.wait_ge(init_act, g - 1)
                    for i in range(4):
                        last = pe.transpose(tr[g % 2][:, i * P:(i + 1) * P], xtok[:, 4 * g + i, :], ident[:, :])
                    last.then_inc(init_pe, 1)
                pe.wait_ge(init_act, 3)
                for i in range(4):
                    last = pe.transpose(tr[0][:, i * P:(i + 1) * P], gw_in[:, i, :], ident[:, :])
                last.then_inc(init_pe, 1)

            @block.scalar
            def _(act):
                for g in range(4):
                    act.wait_ge(init_pe, g + 1)
                    act.activation(resid[:, g, :], tr[g % 2][:, :], ACT.Copy).then_inc(init_act, 1)
                act.wait_ge(init_pe, 5)
                act.activation(gwT[:, :, :], tr[0][:, :].rearrange("p (k c) -> p k c", k=4), ACT.Copy)
                for k in range(2):
                    for r in range(4):
                        act.activation(gw_qk[:, k, :, :, r, :],
                                       tr[0][:, k * P:(k + 1) * P].rearrange("p (g i d) -> p g i d", g=GROUPS, i=HPG),
                                       ACT.Copy)
                act.activation(veps[:, 0:1], ident[:, 0:1], ACT.Copy).then_inc(init_act, 1)

        ln_pe, ln_dve, ln_act, ln_pool = sem("ln_pe"), sem("ln_dve"), sem("ln_act"), sem("ln_pool")

        class Norm:
            n = 0

        def norm_block(add_half, normed):
            base = Norm.n
            Norm.n += BATCHES
            with nc.Block() as block:
                @block.vector
                def _(dve):
                    for b in range(BATCHES):
                        k = 5 * (base + b)
                        if add_half:
                            dve.scalar_tensor_tensor(resid[:, b, :], xs[:, b, :], 0.5, resid[:, b, :],
                                                     ALU.mult, ALU.add).then_inc(ln_dve, 1)
                        else:
                            dve.engine_nop().then_inc(ln_dve, 1)
                        if not normed:
                            for _i in range(4):
                                dve.engine_nop().then_inc(ln_dve, 1)
                            continue
                        dve.wait_ge(ln_pe, 3 * (base + b) + 1)
                        dve.wait_ge(ln_dve, k + 1)
                        dve.tensor_tensor(xc[:, :], resid[:, b, :], proj[0][:, :], ALU.subtract).then_inc(ln_dve, 1)
                        dve.wait_ge(ln_pe, 3 * (base + b) + 2)
                        dve.tensor_scalar(veps[:, :], proj[1][:, 0:TILES], LN_EPS, None, ALU.add).then_inc(ln_dve, 1)
                        dve.wait_ge(ln_pool, base + b + 1)
                        dve.tensor_tensor(diag[:, :, :], ident[:, :].unsqueeze(1).broadcast_to([P, TILES, P]),
                                          rstd[:, :].unsqueeze(2).broadcast_to([P, TILES, P]),
                                          ALU.mult).then_inc(ln_dve, 1)
                        dve.wait_ge(ln_pe, 3 * (base + b) + 3)
                        dve.tensor_tensor(xs[:, b, :], xc[:, :], proj[0][:, :], ALU.mult).then_inc(ln_dve, 1)
                        dve.wait_ge(ln_dve, k + 5)
                if not normed:
                    return

                @block.scalar
                def _(act):
                    for b in range(BATCHES):
                        act.wait_ge(ln_dve, 5 * (base + b) + 2)
                        act.activation(sqd[:, :], xc[:, :], ACT.Square).then_inc(ln_act, 1)

                @block.gpsimd
                def _(pool):
                    for b in range(BATCHES):
                        pool.wait_ge(ln_dve, 5 * (base + b) + 3)
                        pool.tensor_tensor(rstd[:, :], veps[:, :], half_neg[:, 0:TILES], ALU.pow).then_inc(ln_pool, 1)

                @block.tensor
                def _(pe):
                    for b in range(BATCHES):
                        k = 5 * (base + b)
                        pe.wait_ge(ln_dve, k + 1)
                        pe.matmul(proj[0][:, :], mean_w[:, :], resid[:, b, :], start=True, stop=True).then_inc(ln_pe, 1)
                        pe.wait_ge(ln_act, base + b + 1)
                        for i in range(TILES):
                            last = pe.matmul(proj[1][:, i:i + 1], sqd[:, i * P:(i + 1) * P], mean_w[:, 0:1],
                                             start=True, stop=True)
                        last.then_inc(ln_pe, 1)
                        pe.wait_ge(ln_dve, k + 4)
                        pe.matmul(proj[0][:, :], ones_w[:, :], diag[:, :, :].rearrange("p t c -> p (t c)"),
                                  start=True, stop=True).then_inc(ln_pe, 1)

        def stack(half):
            L0 = half * DEPTH

            def dma_block(sp):
                with sp.Fori(0, DEPTH) as l:
                    L = l + L0
                    sp.wait_ge(dve_wlo, layer_done(L - 1, 5, 6))
                    sp.dma_start(w_stage[:, :], Wqkv[bass.ds(l, 1), :, :].rearrange("a p n -> p (a n)")).then_inc(w_loaded, 16)
                    sp.wait_ge(dve_tab, layer_done(L - 1, TILES - 1, TILES))
                    for i, src in enumerate((q_scale, k_scale)):
                        row = src[bass.ds(l, 1), :]
                        hd = DH // 2
                        sp.dma_start(qks[:, 2 * i, :], row.broadcast_to([P, DH])).then_inc(t_loaded, 16)
                        sp.dma_start(qks[:, 2 * i + 1, 0:hd], row[:, hd:DH].broadcast_to([P, hd])).then_inc(t_loaded, 16)
                        sp.dma_start(qks[:, 2 * i + 1, hd:DH], row[:, 0:hd].broadcast_to([P, hd])).then_inc(t_loaded, 16)
                    sp.wait_ge(dve_x2, batch_done(BATCHES * L - 1))
                    sp.dma_start(wo_sb[:, :, :], Wo[bass.ds(l, 1), :, :].rearrange("a (c p) n -> p (a c) n", p=P)).then_inc(f_loaded, 16)
                    sp.dma_start(w1_sb[:, :], W1[bass.ds(l, 1), :, :].rearrange("a p n -> p (a n)")).then_inc(f_loaded, 16)
                    for f, (o, n) in enumerate(FCH):
                        sp.dma_start(w2_sb[0:n, f, :], W2[bass.ds(l, 1), o:o + n, :].rearrange("a p n -> p (a n)")).then_inc(f_loaded, 16)
                        for k in range(2):
                            sp.dma_start(b1_sb[0:n, k, f:f + 1],
                                         b1[bass.ds(l, 1), k * HID + o:k * HID + o + n].rearrange("a p -> p a")).then_inc(f_loaded, 16)
                    for i, src in enumerate((ln_g, ln_b, b2)):
                        sp.dma_start(vec[:, i:i + 1], src[bass.ds(l, 1), :].rearrange("a p -> p a")).then_inc(f_loaded, 16)

            F_DMAS = 2 + 3 * len(FCH) + 3
            T_DMAS = 6

            def pe_program(pe):
                passed[pe] = passed_pe

                def tr_fill(n):
                    pe.wait_ge(act_tr, n + (TR_LEAD - 1))

                def tqk(T, p, n):
                    for c in range(4):
                        tr_fill(n + c)
                        pe.wait_ge(dve_qkn, tile_done(T, c, 4))
                        for i in range(4):
                            last = pe.transpose(tr[c % 2][:, i * P:(i + 1) * P], qkn[:, p, c, i * P:(i + 1) * P], ident[:, :])
                        last.then_inc(pe_tqk, 1)

                def three_pass(dst, cols, wcols):
                    pe.matmul(dst, in_hi[:, cols], wcols(w_hi), start=True, stop=False)
                    pe.matmul(dst, in_hi[:, cols], wcols(w_lo), start=False, stop=False)
                    return pe.matmul(dst, in_lo[:, cols], wcols(w_hi), start=False, stop=True)

                def a_qk(T, s, c, free):
                    for sm, v in free:
                        pe.wait_ge(sm, v)
                    cols = slice(WIN + s * P, WIN + (s + 1) * P)
                    three_pass(proj[c % 2][:, :], cols, lambda w: w[:, c * CH:(c + 1) * CH]).then_inc(pe_qk, 1)

                def values(T, s, free0, free1):
                    for j in range(WPT):
                        if j == 0:
                            for sm, v in free0:
                                pe.wait_ge(sm, v)
                        elif j == 1:
                            for sm, v in free1:
                                pe.wait_ge(sm, v)
                        else:
                            pe.wait_ge(act_v, tile_done(T, j - 2, 4))
                        cols = slice(WIN * (WPT * s + j), WIN * (WPT * s + j) + KEYS)
                        for par in range(2):
                            last = three_pass(proj[j % 2][par * KEYS:(par + 1) * KEYS, :], cols,
                                              lambda w: w[:, 2 * INNER:].rearrange("p (n a d) -> p n a d", a=2, d=DH)[:, :, par, :])
                        last.then_inc(pe_v, 1)

                def scores(T, s, n):
                    p = s % 2
                    pe.wait_ge(dve_sub, tile_done(T - 1, 1, 2))
                    pe.wait_ge(act_tr, n + TR_LEAD)
                    pe.wait_ge(pool_carry, tile_done(T))
                    for par in range(2):
                        pe.matmul(sc[par][:, :], identb[:, :],
                                  maskb[:, 1 if s == 0 else 0, :].unsqueeze(1).broadcast_to([P, HPC, KEYS]),
                                  start=True, stop=False, skip_group_check=True)
                    for pair in range(PAIRS):
                        for par in range(2):
                            r = slice(par * DH, (par + 1) * DH)
                            for w in range(WPT):
                                last = pe.matmul(sc[par][w * WIN:(w + 1) * WIN, pair * KEYS:(pair + 1) * KEYS],
                                                 qT[r, p, pair, w * WIN:(w + 1) * WIN],
                                                 kT[r, p, pair, w * WIN:w * WIN + KEYS],
                                                 start=False, stop=True, skip_group_check=True)
                    last.then_inc(pe_s, 1)

                def tprob(T, p, n):
                    pe.wait_ge(act_exp, tile_done(T))
                    for g in range(2):
                        tr_fill(n + g)
                        for i in range(4):
                            last = pe.transpose(tr[g][:, i * P:(i + 1) * P],
                                                prob[:, p, 4 * g + i, :, :].rearrange("q a k -> q (a k)"), ident[:, :])
                        last.then_inc(pe_tp, 1)

                def outputs(T, p, par, n):
                    pe.wait_ge(dve_on, tile_done(T - 1, par, 2))
                    pe.wait_ge(act_tr, n + TR_LEAD)
                    wait_apart(pe, act_v, tile_done(T, WPT - 1, 4))
                    r = slice(par * KEYS, (par + 1) * KEYS)
                    for pair in range(PAIRS):
                        for w in range(WPT):
                            last = pe.matmul(ov[par][w * WIN:(w + 1) * WIN, pair * DH:(pair + 1) * DH],
                                             pT[r, pair, w * WIN:(w + 1) * WIN], vw[r, p, w, pair * DH:(pair + 1) * DH],
                                             start=True, stop=True, skip_group_check=True)
                    last.then_inc(pe_pv, 1)

                def tout(T, n):
                    pe.wait_ge(dve_on, tile_done(T, 1, 2))
                    for g in range(2):
                        tr_fill(n + g)
                        for i in range(4):
                            last = pe.transpose(tr[g][:, i * P:(i + 1) * P],
                                                on[:, 4 * g + i, :, :].rearrange("q a d -> q (a d)"), ident[:, :])
                        last.then_inc(pe_to, 1)

                def f_wo(B, free, n):
                    pe.wait_ge(f_loaded, 16 * F_DMAS * (B_layer(B) + 1))
                    for sm, v in free:
                        pe.wait_ge(sm, v)
                    pe.wait_ge(act_tr, n)
                    for c in range(PAIRS):
                        last = pe.matmul(proj[0][:, :], wo_sb[:, c, :], oT[:, c, :], start=c == 0, stop=c == PAIRS - 1)
                    last.then_inc(pe_wo, 1)

                def f_mean(B, free):
                    for sm, v in free:
                        pe.wait_ge(sm, v)
                    pe.wait_ge(act_fin, batch_done(B, 1, 2))
                    pe.matmul(proj[0][:, :], mean_w[:, :], f_in[:, :], start=True, stop=True).then_inc(pe_mean, 1)

                def f_var(B, free):
                    for sm, v in free:
                        pe.wait_ge(sm, v)
                    pe.wait_ge(act_sqd, batch_done(B))
                    for i in range(TILES):
                        last = pe.matmul(proj[1][:, i:i + 1], sqd[:, i * P:(i + 1) * P], mean_w[:, 0:1], start=True, stop=True)
                    last.then_inc(pe_var, 1)

                def f_rep(B, free):
                    for sm, v in free:
                        pe.wait_ge(sm, v)
                    pe.wait_ge(dve_diag, batch_done(B))
                    pe.matmul(proj[0][:, :], ones_w[:, :], diag[:, :, :].rearrange("p t c -> p (t c)"),
                              start=True, stop=True).then_inc(pe_rep, 1)

                def f_hid(B, free):
                    for sm, v in free:
                        pe.wait_ge(sm, v)
                    pe.wait_ge(act_xg, batch_done(B))
                    for f, (o, n) in enumerate(FCH):
                        if f:
                            pe.wait_ge(act_gelu, batch_done(B, f - 1, 3))
                        pe.matmul(proj[0][0:n, :], w1_sb[:, HID + o:HID + o + n], xg[:, :], start=True, stop=True).then_inc(pe_gate, 1)
                        if f:
                            pe.wait_ge(dve_hid, batch_done(B, f - 1, 3))
                        pe.matmul(proj[1][0:n, :], w1_sb[:, o:o + n], xg[:, :], start=True, stop=True).then_inc(pe_up, 1)

                def f_w2(B, free):
                    for sm, v in free:
                        pe.wait_ge(sm, v)
                    pe.wait_ge(dve_hid, batch_done(B, 2, 3))
                    for f, (o, n) in enumerate(FCH):
                        last = pe.matmul(proj[1][:, :], w2_sb[0:n, f, :], hid[0:n, f, :], start=f == 0, stop=f == 2)
                    last.then_inc(pe_w2, 1)

                B_layer = lambda B: B[1]

                def step(L, B, T, s, n, has_a, has1, has2, ff):
                    p1 = (s - 1) % 2
                    if has1:
                        tqk(T - 1, p1, n)
                        n = n + 4
                    scored = n
                    late = []
                    if ff and s == 2:
                        late = [(dve_x1, batch_done(B[0]))]
                    if ff and s == 3:
                        late = [(dve_xn, batch_done(B[0]))]
                    if has_a:
                        if s == 0:
                            pe.wait_ge(dve_in, batch_done(T_batch(T, s), 1, 2))
                            pe.wait_ge(dve_wlo, layer_done(L, 5, 6))
                        a_qk(T, s, 0, [(act_v, tile_done(T - 1, 2, 4))] + late)
                        a_qk(T, s, 1, [(act_v, tile_done(T - 1, 3, 4))] + after_w2)
                    if has1:
                        scores(T - 1, (s - 1) % 4, scored)
                    late = [[], []]
                    if ff and s == 2:
                        f_mean_(B, [(dve_rot, tile_done(T, 0, 4))])
                        late[0] = [(dve_xc, batch_done(B[0]))]
                    if ff and s == 3:
                        f_hid_(B, [(dve_rot, tile_done(T, 1, 4))])
                        late = [[(act_gelu, batch_done(B[0], 2, 3))], [(dve_hid, batch_done(B[0], 2, 3))]]
                    if has_a:
                        a_qk(T, s, 2, [(dve_rot, tile_done(T, 0, 4))] + late[0])
                    if has2:
                        outputs(T - 2, s % 2, 0, n - 4 if has1 else n)
                    if has_a:
                        a_qk(T, s, 3, [(dve_rot, tile_done(T, 1, 4))] + late[1])
                    if has2:
                        outputs(T - 2, s % 2, 1, n - 4 if has1 else n)
                    late = []
                    if ff and s == 2:
                        f_var_(B, [(dve_rot, tile_done(T, 3, 4))])
                        late = [(dve_veps, batch_done(B[0]))]
                    if ff and s == 3:
                        f_w2_(B, [(dve_rot, tile_done(T, 3, 4))])
                        late = [(dve_x2, batch_done(B[0]))]
                    if has_a:
                        values(T, s, [(dve_rot, tile_done(T, 2, 4))], [(dve_rot, tile_done(T, 3, 4))] + late)
                    if has2:
                        tout(T - 2, n)
                        n = n + 2
                    if has1:
                        tprob(T - 1, p1, n)
                        n = n + 2
                    if ff and s == 1:
                        f_wo_(B, [(act_v, tile_done(T, 2, 4))], n - 2 + TR_LEAD)
                    if ff and s == 2:
                        f_rep_(B, [(act_v, tile_done(T, 2, 4))])
                    return n

                after_w2 = []
                T_batch = lambda T, s: T_of[0]
                T_of = [None]

                def f_wo_(B, free, n):
                    f_wo(B, free, n)

                def run(name, B, free, *a):
                    for sm, v in free:
                        pe.wait_ge(sm, v)

                def f_mean_(B, free):
                    f_mean(B[0], free)

                def f_var_(B, free):
                    f_var(B[0], free)

                def f_rep_(B, free):
                    f_rep(B[0], free)

                def f_hid_(B, free):
                    f_hid(B[0], free)

                def f_w2_(B, free):
                    f_w2(B[0], free)

                def f_wo(B, free, n):
                    b, L = B
                    pe.wait_ge(f_loaded, (L + 1) * (16 * F_DMAS))
                    for sm, v in free:
                        pe.wait_ge(sm, v)
                    pe.wait_ge(act_tr, n)
                    for c in range(PAIRS):
                        last = pe.matmul(proj[0][:, :], wo_sb[:, c, :], oT[:, c, :], start=c == 0, stop=c == PAIRS - 1)
                    last.then_inc(pe_wo, 1)

                with pe.Fori(0, DEPTH) as l:
                    L = l + L0
                    T0 = L * LAYER_TILES
                    n0 = L * (8 * LAYER_TILES)
                    n = n0
                    T_of[0] = L * BATCHES
                    for s in range(4):
                        n = step(L, None, T0 + s, s, n, True, s >= 1, s >= 2, False)
                    with pe.Fori(1, BATCHES) as b:
                        Bb = L * BATCHES + b
                        T_of[0] = Bb
                        Tb = Bb * TILES
                        n = n0 + b * 32 - 10
                        for s in range(4):
                            n = step(L, (Bb - 1, L), Tb + s, s, n, True, True, True, True)
                    n = n0 + (32 * BATCHES - 10)
                    Te = T0 + LAYER_TILES
                    B = (L * BATCHES + (BATCHES - 1), L)
                    n = step(L, B, Te, 4, n, False, True, True, False)
                    n = step(L, B, Te + 1, 5, n, False, False, True, False)
                    f_wo(B, [(act_v, tile_done(Te - 1, 2, 4))], n + TR_LEAD)
                    f_mean(B[0], [(dve_x1, batch_done(B[0]))])
                    f_var(B[0], [(act_v, tile_done(Te - 1, 3, 4))])
                    f_rep(B[0], [(dve_xc, batch_done(B[0]))])
                    f_hid(B[0], [(dve_xn, batch_done(B[0])), (dve_veps, batch_done(B[0]))])
                    f_w2(B[0], [(dve_hid, batch_done(B[0], 2, 3))])

            def act_program(act):
                def squares(T, c):
                    act.wait_ge(pe_qk, tile_done(T, c, 4))
                    act.wait_ge(dve_n2, tile_done(T, c - 2, 4))
                    act.activation(sq[:, c % 2, :], proj[c % 2][:, :], ACT.Square).then_inc(act_sq, 1)

                def store_qk(T, s):
                    p = s % 2
                    act.wait_ge(pe_s, tile_done(T - 2))
                    for c in range(4):
                        act.wait_ge(pe_tqk, tile_done(T, c, 4))
                        src = tr[c % 2][:, :].rearrange("p (n t) -> p n t", n=4)
                        g = 4 * (c % 2)
                        if c == 2:
                            act.wait_ge(pool_carry, tile_done(T - 1))
                        dst = qT[:, p, g:g + 4, :] if c < 2 else kT[:, p, g:g + 4, WIN:WIN + P]
                        act.activation(dst, src, ACT.Copy).then_inc(act_tr, 1)

                def exps(T, p):
                    act.wait_ge(dve_sub, tile_done(T, 1, 2))
                    v = prob[:, p, :, :, :].rearrange("q n a k -> q (n a k)")
                    act.activation(v, v, ACT.Exp).then_inc(act_exp, 1)

                def store_v(T, p):
                    act.wait_ge(pe_pv, tile_done(T - 2, 1, 2))
                    for j in range(WPT):
                        act.wait_ge(pe_v, tile_done(T, j, 4))
                        act.activation(vw[:, p, j, :], proj[j % 2][:, :], ACT.Copy, scale=1.0 / W_SCALE).then_inc(act_v, 1)

                def store_out(T, B, s):
                    act.wait_ge(pe_wo, batch_done(B - 1))
                    for g in range(2):
                        act.wait_ge(pe_to, tile_done(T, g, 2))
                        act.activation(oT[:, 4 * g:4 * g + 4, s * P:(s + 1) * P],
                                       tr[g][:, :].rearrange("p (n t) -> p n t", n=4), ACT.Copy).then_inc(act_tr, 1)

                def store_prob(T):
                    act.wait_ge(pe_pv, tile_done(T - 1, 1, 2))
                    for g in range(2):
                        act.wait_ge(pe_tp, tile_done(T, g, 2))
                        act.activation(pT[:, 4 * g:4 * g + 4, :],
                                       tr[g][:, :].rearrange("p (n t) -> p n t", n=4), ACT.Copy).then_inc(act_tr, 1)

                def f_input(B, xb):
                    act.wait_ge(dve_x1, batch_done(B))
                    act.wait_ge(dve_xc, batch_done(B - 1))
                    h = DIM // 2
                    act.activation(f_in[0:h, :], xs[0:h, xb, :], ACT.Copy).then_inc(act_fin, 1)
                    act.activation(f_in[h:DIM, 1:SEQ], xs[h:DIM, xb, 0:SEQ - 1], ACT.Copy).then_inc(act_fin, 1)

                def f_square(B):
                    act.wait_ge(dve_xc, batch_done(B))
                    act.wait_ge(pe_var, batch_done(B - 1))
                    act.activation(sqd[:, :], xc[:, :], ACT.Square).then_inc(act_sqd, 1)

                def f_affine(B):
                    act.wait_ge(dve_xn, batch_done(B))
                    act.wait_ge(pe_up, batch_done(B - 1, 2, 3))
                    act.activation(xg[:, :], xn[:, :], ACT.Identity, bias=vec[:, 1:2], scale=vec[:, 0:1]).then_inc(act_xg, 1)

                def f_gelu(B):
                    for f, (o, n) in enumerate(FCH):
                        act.wait_ge(pe_gate, batch_done(B, f, 3))
                        act.wait_ge(dve_hid, batch_done(B, f - 2, 3))
                        act.activation(gel[0:n, f % 2, :], proj[0][0:n, :], ACT.Gelu, bias=b1_sb[0:n, 1, f:f + 1]).then_inc(act_gelu, 1)

                def split_in(B, xb):
                    act.wait_ge(dve_x2, batch_done(B - BATCHES))
                    act.wait_ge(pe_v, tile_done(B * TILES - 1, 3, 4))
                    h = DIM // 2
                    act.activation(in_hi[0:h, WIN:], xs[0:h, xb, :], ACT.Copy).then_inc(act_in, 1)
                    act.activation(in_hi[h:DIM, WIN + 1:], xs[h:DIM, xb, 0:SEQ - 1], ACT.Copy).then_inc(act_in, 1)

                def step(T, s, has_a, has1, has2, ff, B, xb, Bo=None):
                    if has1:
                        store_qk(T - 1, (s - 1) % 4)
                    if ff and s == 3:
                        f_affine(B)
                    if has_a:
                        squares(T, 0)
                        squares(T, 1)
                    if ff and s == 3:
                        f_gelu(B)
                    if has_a:
                        squares(T, 2)
                    if has1:
                        exps(T - 1, (s - 1) % 2)
                    if ff and s == 2:
                        f_square(B)
                    if has_a:
                        squares(T, 3)
                        store_v(T, s % 2)
                    if has2:
                        store_out(T - 2, Bo, (s - 2) % 4)
                    if has1:
                        store_prob(T - 1)
                    if ff and s == 1:
                        f_input(B, xb)

                with act.Fori(0, DEPTH) as l:
                    L = l + L0
                    act.wait_ge(w_loaded, (L + 2) * 16)
                    act.wait_ge(pe_v, tile_done(L * LAYER_TILES - 1, 3, 4))
                    for c in range(6):
                        act.activation(w_hi[:, c * CH:(c + 1) * CH], w_stage[:, c * CH:(c + 1) * CH], ACT.Copy,
                                       scale=W_SCALE).then_inc(act_whi, 1)
                    T0 = L * LAYER_TILES
                    B0 = L * BATCHES
                    split_in(B0, 0)
                    for s in range(4):
                        step(T0 + s, s, True, s >= 1, s >= 2, False, None, 0, B0)
                    with act.Fori(1, BATCHES) as b:
                        B = B0 + b
                        split_in(B, bass.ds(b, 1))
                        for s in range(4):
                            step(B * TILES + s, s, True, True, True, True, B - 1, bass.ds(b - 1, 1), B - 1 if s < 2 else B)
                    B = B0 + (BATCHES - 1)
                    Te = T0 + LAYER_TILES
                    step(Te, 4, False, True, True, False, B, BATCHES - 1, B)
                    step(Te + 1, 5, False, False, True, False, B, BATCHES - 1, B)
                    f_input(B, BATCHES - 1)
                    f_square(B)
                    f_affine(B)
                    f_gelu(B)

            def dve_program(dve):
                def bc(ap, n):
                    return ap.unsqueeze(2).broadcast_to([P, HPC, n])

                def rotary(T, s, c):
                    k = 0 if c < 2 else 2
                    hd = DH // 2
                    b = c % 2
                    dve.wait_ge(act_sq, tile_done(T, c, 4))
                    dve.wait_ge(pool_r, tile_done(T, 2 * (c - 2), 8))
                    dve.tensor_reduce(n2[:, b, :], sq[:, b, :].rearrange("p (h d) -> p h d", d=DH),
                                      axis=AX.X, op=ALU.add).then_inc(dve_n2, 1)
                    dve.wait_ge(pool_add, tile_done(T, c - 2, 4))
                    src = proj[b][:, :].rearrange("p (h d) -> p h d", d=DH)
                    a1 = t1[:, b, :].rearrange("p (h d) -> p h d", d=DH)
                    a2 = t2[:, b, :].rearrange("p (h d) -> p h d", d=DH)
                    cos = table[:, s, k, :].unsqueeze(1).broadcast_to([P, HPC, DH])
                    sin = table[:, s, k + 1, :].unsqueeze(1).broadcast_to([P, HPC, DH])
                    dve.tensor_tensor(a1, src, cos, ALU.mult)
                    dve.tensor_tensor(a2[:, :, 0:hd], src[:, :, hd:DH], sin[:, :, 0:hd], ALU.mult)
                    dve.tensor_tensor(a2[:, :, hd:DH], src[:, :, 0:hd], sin[:, :, hd:DH], ALU.mult).then_inc(dve_rot, 1)

                def normalise(T, s, c):
                    b = c % 2
                    dve.wait_ge(pool_add, tile_done(T, c, 4))
                    dve.wait_ge(pool_r, tile_done(T, 2 * c + 1, 8))
                    if c == 0:
                        dve.wait_ge(pe_tqk, tile_done(T - 2, 3, 4))
                    dve.tensor_tensor(qkn[:, s % 2, c, :].rearrange("p (h d) -> p h d", d=DH),
                                      rot[:, b, :].rearrange("p (h d) -> p h d", d=DH), bc(rn[:, b, :], DH),
                                      ALU.mult).then_inc(dve_qkn, 1)

                def shift_max(T, p):
                    dve.wait_ge(pe_s, tile_done(T))
                    dve.wait_ge(pe_tp, tile_done(T - 2, 1, 2))
                    dve.wait_ge(dve_sum, tile_done(T - 2))
                    for par in range(2):
                        src = sc[par][:, :].rearrange("q (n k) -> q n k", k=KEYS)
                        dve.wait_ge(dve_sub, tile_done(T - 1, par, 2))
                        dve.tensor_reduce(smax[:, par, :], src, axis=AX.X, op=ALU.max).then_inc(dve_max, 1)
                        dve.wait_ge(dve_max, tile_done(T, par, 2))
                        dve.tensor_tensor(prob[:, p, :, par, :], src, bc(smax[:, par, :], KEYS), ALU.subtract).then_inc(dve_sub, 1)

                def sums(T, p):
                    dve.wait_ge(act_exp, tile_done(T))
                    dve.wait_ge(dve_rs, tile_done(T - 2))
                    dve.tensor_reduce(psumr[:, p, :], prob[:, p, :, :, :].rearrange("q n a k -> q (n a) k"),
                                      axis=AX.X, op=ALU.add).then_inc(dve_sum, 1)
                    dve.wait_ge(dve_sum, tile_done(T))
                    dve.wait_ge(dve_on, tile_done(T - 2, 1, 2))
                    dve.reciprocal(rsum[:, p, :], psumr[:, p, :]).then_inc(dve_rs, 1)

                def out_norm(T, p):
                    dve.wait_ge(dve_rs, tile_done(T))
                    dve.wait_ge(pe_to, tile_done(T - 1, 1, 2))
                    for par in range(2):
                        dve.wait_ge(pe_pv, tile_done(T, par, 2))
                        dve.tensor_tensor(on[:, :, par, :], ov[par][:, :].rearrange("q (n d) -> q n d", d=DH),
                                          bc(rsum[:, p, :].rearrange("q (n a) -> q n a", a=2)[:, :, par], DH),
                                          ALU.mult).then_inc(dve_on, 1)

                def f_resid1(B, xb):
                    dve.wait_ge(pe_wo, batch_done(B))
                    dve.tensor_tensor(xs[:, xb, :], xs[:, xb, :], proj[0][:, :], ALU.add).then_inc(dve_x1, 1)

                def f_centre(B):
                    dve.wait_ge(pe_mean, batch_done(B))
                    dve.wait_ge(dve_xn, batch_done(B - 1))
                    dve.tensor_tensor(xc[:, :], f_in[:, :], proj[0][:, :], ALU.subtract).then_inc(dve_xc, 1)

                def f_veps(B):
                    dve.wait_ge(pe_var, batch_done(B))
                    dve.wait_ge(pool_rstd, batch_done(B - 1))
                    dve.tensor_scalar(veps[:, :], proj[1][:, 0:TILES], LN_EPS, None, ALU.add).then_inc(dve_veps, 1)

                def f_diag(B):
                    dve.wait_ge(pool_rstd, batch_done(B))
                    dve.wait_ge(pe_rep, batch_done(B - 1))
                    dve.tensor_tensor(diag[:, :, :], ident[:, :].unsqueeze(1).broadcast_to([P, TILES, P]),
                                      rstd[:, :].unsqueeze(2).broadcast_to([P, TILES, P]), ALU.mult).then_inc(dve_diag, 1)

                def f_scale(B):
                    dve.wait_ge(pe_rep, batch_done(B))
                    dve.wait_ge(act_xg, batch_done(B - 1))
                    dve.tensor_tensor(xn[:, :], xc[:, :], proj[0][:, :], ALU.mult).then_inc(dve_xn, 1)

                def f_gated(B):
                    dve.wait_ge(pe_w2, batch_done(B - 1))
                    for f, (o, n) in enumerate(FCH):
                        dve.wait_ge(pe_up, batch_done(B, f, 3))
                        dve.wait_ge(act_gelu, batch_done(B, f, 3))
                        dve.scalar_tensor_tensor(hid[0:n, f, :], proj[1][0:n, :], b1_sb[0:n, 0, f:f + 1], gel[0:n, f % 2, :],
                                                 ALU.add, ALU.mult).then_inc(dve_hid, 1)

                def f_resid2(B, xb):
                    dve.wait_ge(pe_w2, batch_done(B))
                    dve.wait_ge(act_fin, batch_done(B, 1, 2))
                    dve.scalar_tensor_tensor(xs[:, xb, :], proj[1][:, :], vec[:, 2:3], xs[:, xb, :], ALU.add, ALU.add).then_inc(dve_x2, 1)

                def split_in(B, xb):
                    h = DIM // 2
                    dve.wait_ge(act_in, batch_done(B, 1, 2))
                    dve.tensor_tensor(in_lo[0:h, WIN:], xs[0:h, xb, :], in_hi[0:h, WIN:], ALU.subtract).then_inc(dve_in, 1)
                    dve.tensor_tensor(in_lo[h:DIM, WIN + 1:], xs[h:DIM, xb, 0:SEQ - 1], in_hi[h:DIM, WIN + 1:], ALU.subtract).then_inc(dve_in, 1)

                def step(T, s, has_a, has1, has2, ff, B, xb):
                    if ff and s == 3:
                        f_scale(B)
                    if has_a:
                        rotary(T, s, 0)
                        rotary(T, s, 1)
                        normalise(T, s, 0)
                    if has1:
                        shift_max(T - 1, (s - 1) % 2)
                    if ff and s == 2:
                        f_centre(B)
                    if ff and s == 3:
                        f_gated(B)
                    if has_a:
                        normalise(T, s, 1)
                        rotary(T, s, 2)
                        rotary(T, s, 3)
                        normalise(T, s, 2)
                    if has2:
                        out_norm(T - 2, s % 2)
                    if ff and s == 2:
                        f_veps(B)
                    if has1:
                        sums(T - 1, (s - 1) % 2)
                    if has_a:
                        normalise(T, s, 3)
                    if ff and s == 1:
                        f_resid1(B, xb)
                    if ff and s == 2:
                        f_diag(B)
                    if ff and s == 3:
                        f_resid2(B, xb)

                with dve.Fori(0, DEPTH) as l:
                    L = l + L0
                    for c in range(6):
                        dve.wait_ge(act_whi, layer_done(L, c, 6))
                        dve.scalar_tensor_tensor(w_lo[:, c * CH:(c + 1) * CH], w_stage[:, c * CH:(c + 1) * CH], W_SCALE,
                                                 w_hi[:, c * CH:(c + 1) * CH], ALU.mult, ALU.subtract).then_inc(dve_wlo, 1)
                    dve.wait_ge(t_loaded, (L + 1) * (16 * T_DMAS))
                    dve.wait_ge(dve_rot, tile_done(L * LAYER_TILES - 1, 3, 4))
                    for s in range(TILES):
                        dve.tensor_tensor(table[:, s, :, :], rope[:, s, :, :], qks[:, :, :], ALU.mult).then_inc(dve_tab, 1)
                    dve.wait_ge(dve_tab, layer_done(L, TILES - 1, TILES))
                    T0 = L * LAYER_TILES
                    B0 = L * BATCHES
                    split_in(B0, 0)
                    for s in range(4):
                        step(T0 + s, s, True, s >= 1, s >= 2, False, None, 0)
                    with dve.Fori(1, BATCHES) as b:
                        B = B0 + b
                        split_in(B, bass.ds(b, 1))
                        for s in range(4):
                            step(B * TILES + s, s, True, True, True, True, B - 1, bass.ds(b - 1, 1))
                    B = B0 + (BATCHES - 1)
                    Te = T0 + LAYER_TILES
                    step(Te, 4, False, True, True, False, B, BATCHES - 1)
                    step(Te + 1, 5, False, False, True, False, B, BATCHES - 1)
                    f_resid1(B, BATCHES - 1)
                    f_centre(B)
                    f_veps(B)
                    f_diag(B)
                    f_scale(B)
                    f_gated(B)
                    f_resid2(B, BATCHES - 1)

            def pool_program(pool):
                passed[pool] = passed_pool

                def chunk(T, c):
                    b = c % 2
                    pool.wait_ge(dve_n2, tile_done(T, c, 4))
                    wait_apart(pool, pool_r, tile_done(T, 2 * (c - 2) + 1, 8))
                    pool.tensor_scalar(n2f[:, b, :], n2[:, b, :], NORM_FLOOR, None, ALU.max).then_inc(pool_r, 1)
                    pool.wait_ge(pool_r, tile_done(T, 2 * c, 8))
                    pool.wait_ge(dve_qkn, tile_done(T, c - 2, 4))
                    pool.tensor_tensor(rn[:, b, :], n2f[:, b, :], half_neg[:, :], ALU.pow).then_inc(pool_r, 1)
                    pool.wait_ge(dve_rot, tile_done(T, c, 4))
                    pool.tensor_tensor(rot[:, b, :], t1[:, b, :], t2[:, b, :], ALU.add).then_inc(pool_add, 1)

                def carry(T, s):
                    p = s % 2
                    wait_apart(pool, pe_s, tile_done(T - 2))
                    if s == 0:
                        pool.memset(kT[:, p, :, 0:WIN], 0.0).then_inc(pool_carry, 1)
                    else:
                        pool.tensor_copy(kT[:, p, :, 0:WIN], kT[:, 1 - p, :, P:P + WIN]).then_inc(pool_carry, 1)

                def f_rstd(B):
                    pool.wait_ge(dve_veps, batch_done(B))
                    pool.wait_ge(dve_diag, batch_done(B - 1))
                    pool.tensor_tensor(rstd[:, :], veps[:, :], half_neg[:, 0:TILES], ALU.pow).then_inc(pool_rstd, 1)

                with pool.Fori(0, DEPTH) as l:
                    L = l + L0
                    T0 = L * LAYER_TILES
                    n0 = L * (8 * LAYER_TILES)
                    for s in range(4):
                        T = T0 + s
                        chunk(T, 0)
                        chunk(T, 1)
                        if s:
                            fills = 4 if s == 1 else 8 * s - 10 + 4
                            pool.wait_ge(act_tr, n0 + (fills + TR_LEAD))
                        carry(T, s)
                        chunk(T, 2)
                        chunk(T, 3)
                    with pool.Fori(1, BATCHES) as b:
                        B = L * BATCHES + b
                        for s in range(4):
                            T = B * TILES + s
                            chunk(T, 0)
                            chunk(T, 1)
                            if s:
                                pool.wait_ge(act_tr, n0 + b * 32 + (8 * s - 10 + 4 + TR_LEAD))
                            carry(T, s)
                            chunk(T, 2)
                            chunk(T, 3)
                            if s == 2:
                                f_rstd(B - 1)
                    f_rstd(L * BATCHES + (BATCHES - 1))

            with nc.Block() as block:
                block.sync(dma_block)
                block.tensor(pe_program)
                block.scalar(act_program)
                block.vector(dve_program)
                block.gpsimd(pool_program)

        g_pe_q, g_act_hi, g_dve_st = sem("g_pe_q"), sem("g_act_hi"), sem("g_dve_st")
        g_pe_v, g_act_v, g_pe_s, g_act_sig = sem("g_pe_v"), sem("g_act_v"), sem("g_pe_s"), sem("g_act_sig")
        g_pe_o, g_act_o, g_pe_nd, g_dve_r, g_pe_wo, g_dve_x = (sem(n) for n in ("g_pe_o", "g_act_o", "g_pe_nd", "g_dve_r", "g_pe_wo", "g_dve_x"))
        g_zero = sem("g_zero")

        def global_attention():
            qk_hi = qkn[:, 0, :, :]
            st = vw[:, :, :, :].bitcast(F16)
            q_st = st[:, 0, :, 0:SEQ]
            k_st = st[:, 1, :, 0:SEQ]
            hi16 = qk_hi.bitcast(F16)
            vaug = w_stage[:, 0:TILES * GH * 32].rearrange("p (t h c) -> p t h c", t=TILES, h=GH)
            sig = oT[:, 0:8, :].rearrange("p (a b) t -> p a b t", a=4)
            og = hid_og[:, :, :]
            num = t1[:, 0, :]
            rden = t1[:, 1, :]
            den = t2[:, 0, :]
            att = t2[:, 1, :]
            with nc.Block() as block:
                @block.gpsimd
                def _(pool):
                    pool.memset(vaug, 0.0).then_inc(g_zero, 1)
                    pool.wait_ge(g_zero, 1)
                    pool.memset(vaug[:, :, :, GD:GD + 1], 1.0).then_inc(g_zero, 1)

                @block.tensor
                def _(pe):
                    pe.wait_ge(g_zero, 2)
                    for b in range(BATCHES):
                        for g in range(GROUPS):
                            for k in range(2):
                                i = 8 * b + 2 * g + k
                                if i >= 2:
                                    pe.wait_ge(g_dve_st, i - 1)
                                elif b:
                                    pe.wait_ge(g_dve_x, b)
                                if b and g == 0:
                                    pe.wait_ge(g_dve_x, b)
                                pe.matmul(ps[6 + k][:, :], gw_qk[:, k, g, :, :, :].rearrange("p i r d -> p (i r d)"),
                                          xs[:, b, :], start=True, stop=True).then_inc(g_pe_q, 1)
                        pe.wait_ge(g_dve_st, 8 * (b + 1) - 1)
                        for t in range(TILES):
                            last = pe.matmul(ps[6][:, t * P:(t + 1) * P], xs[:, b, t * P:(t + 1) * P], gwT[:, 2, :],
                                             start=True, stop=True)
                        last.then_inc(g_pe_v, 1)
                        pe.wait_ge(g_act_v, b + 1)
                        pe.wait_ge(g_dve_st, 8 * (b + 1))
                        units = [(g, t, h) for g in range(GROUPS) for t in range(TILES) for h in range(2)]

                        def score(u):
                            g, t, h = units[u]
                            n = len(units) * b + u
                            if n >= 2:
                                pe.wait_ge(g_act_sig, n - 1)
                            for j in range(2):
                                i = 2 * h + j
                                r = slice(32 * i, 32 * i + 32)
                                last = pe.matmul(ps[i][:, :], k_st[r, g, t * P:(t + 1) * P], q_st[r, g, :], start=True, stop=True)
                            last.then_inc(g_pe_s, 1)

                        def apply(u):
                            g, t, h = units[u]
                            n = len(units) * b + u
                            pe.wait_ge(g_act_sig, n + 1)
                            if t == 0 and h == 0 and GROUPS * b + g >= 2:
                                pe.wait_ge(g_act_o, GROUPS * b + g - 1)
                            for j in range(2):
                                i = 2 * h + j
                                last = pe.matmul(ps[4 + g % 2][32 * i:32 * i + 32, :], vaug[:, t, HPG * g + i, :],
                                                 sig[:, n % 4, j, :], start=t == 0, stop=t == TILES - 1,
                                                 skip_group_check=True)
                            last.then_inc(g_pe_o, 1)

                        for u in range(len(units) + 2):
                            if u < len(units):
                                score(u)
                            if u >= 2:
                                apply(u - 2)
                        pe.wait_ge(g_act_o, GROUPS * (b + 1))
                        for k in range(2):
                            for g in range(GROUPS):
                                last = pe.matmul(ps[6 + k][:, :], sel[:, k, g, :], og[:, g, :], start=g == 0, stop=g == GROUPS - 1)
                            last.then_inc(g_pe_nd, 1)
                        pe.wait_ge(g_dve_r, 3 * (b + 1))
                        pe.matmul(ps[6][:, :], gwT[:, 3, :], att, start=True, stop=True).then_inc(g_pe_wo, 1)

                @block.scalar
                def _(act):
                    for b in range(BATCHES):
                        for i in range(8 * b, 8 * b + 8):
                            act.wait_ge(g_pe_q, i + 1)
                            if i >= 2:
                                act.wait_ge(g_dve_st, i - 1)
                            act.activation(hi16[:, i % 2, 0:SEQ], ps[6 + i % 2][:, :], ACT.Copy).then_inc(g_act_hi, 1)
                        act.wait_ge(g_pe_v, b + 1)
                        act.activation(vaug[:, :, :, 0:GD], ps[6][:, :].rearrange("p (t h d) -> p t h d", t=TILES, h=GH),
                                       ACT.Copy).then_inc(g_act_v, 1)
                        for u in range(32):
                            n = 32 * b + u
                            act.wait_ge(g_pe_s, n + 1)
                            if n >= 4:
                                act.wait_ge(g_pe_o, n - 3)
                            h = u % 2
                            for j in range(2):
                                last = act.activation(sig[:, n % 4, j, :], ps[2 * h + j][:, :], ACT.Sigmoid, scale=GD ** -0.5)
                            last.then_inc(g_act_sig, 1)
                            if u % 8 == 7:
                                g = u // 8
                                act.wait_ge(g_pe_o, n + 1)
                                if g == 0 and b:
                                    act.wait_ge(g_pe_nd, 2 * b)
                                act.activation(og[:, g, :], ps[4 + g % 2][:, :], ACT.Copy).then_inc(g_act_o, 1)

                @block.vector
                def _(dve):
                    for b in range(BATCHES):
                        for i in range(8 * b, 8 * b + 8):
                            k = i % 2
                            g = (i // 2) % GROUPS
                            dve.wait_ge(g_act_hi, i + 1)
                            dve.scalar_tensor_tensor((q_st if k == 0 else k_st)[:, g, :], hi16[:, k, 0:SEQ], slot[:, k:k + 1],
                                                     ps[6 + k][:, :], ALU.mult, ALU.add).then_inc(g_dve_st, 1)
                        dve.wait_ge(g_pe_nd, 2 * b + 2)
                        dve.tensor_scalar(den, ps[7][:, :], SIG_EPS, None, ALU.add).then_inc(g_dve_r, 1)
                        dve.wait_ge(g_dve_r, 3 * b + 1)
                        dve.reciprocal(rden, den).then_inc(g_dve_r, 1)
                        dve.wait_ge(g_dve_r, 3 * b + 2)
                        dve.tensor_tensor(att, rden, ps[6][:, :], ALU.mult).then_inc(g_dve_r, 1)
                        dve.wait_ge(g_pe_wo, b + 1)
                        dve.tensor_tensor(resid[:, b, :], resid[:, b, :], ps[6][:, :], ALU.add).then_inc(g_dve_x, 1)
                    dve.wait_ge(g_dve_x, BATCHES)

        hid_og = sb("hid_og", [P, GROUPS, SEQ])

        norm_block(False, True)
        norm_block_done = None
        stack(0)
        norm_block(True, True)
        global_attention()
        norm_block(False, True)
        stack(1)
        norm_block(True, False)

        fin_pe, fin_act, stored = sem("fin_pe"), sem("fin_act"), sem("stored")
        with nc.Block() as block:
            @block.tensor
            def _(pe):
                for g in range(4):
                    if g >= 2:
                        pe.wait_ge(fin_act, g - 1)
                    for i in range(4):
                        last = pe.transpose(tr[g % 2][:, i * P:(i + 1) * P], resid[:, g, i * P:(i + 1) * P], ident[:, :])
                    last.then_inc(fin_pe, 1)

            @block.scalar
            def _(act):
                for g in range(4):
                    act.wait_ge(fin_pe, g + 1)
                    act.activation(xtok[:, 4 * g:4 * g + 4, :], tr[g % 2][:, :].rearrange("p (t d) -> p t d", d=DIM),
                                   ACT.Copy).then_inc(fin_act, 1)

            @block.sync
            def _(sp):
                for g in range(4):
                    sp.wait_ge(fin_act, g + 1)
                    sp.dma_start(out[g, :, :].rearrange("(t p) d -> p t d", p=P), xtok[:, 4 * g:4 * g + 4, :]).then_inc(stored, 16)
                sp.wait_ge(stored, 64)


def rope_tables():
    f = np.float32
    half = np.arange(0, DH, 2, dtype=f)
    inv_freq = (f(1.0) / np.power(f(10000.0), half / f(DH))).astype(f)
    t = np.arange(SEQ, dtype=f)
    ang = (t[:, None] * inv_freq[None, :]).astype(f)
    base = ((half + f(0.4 * DH)) / f(1.4 * DH)).astype(f)
    power = ((t - SEQ // 2) / f(WIN // 2)).astype(f)
    scale = np.power(base[None, :].astype(np.float64), power[:, None])
    cos, sin = np.cos(ang.astype(np.float64)), np.sin(ang.astype(np.float64))
    rows = []
    for sc, mul in ((scale, 8.0), (1.0 / scale, 1.0)):
        c, s = cos * sc * mul, sin * sc * mul
        rows += [np.concatenate([c, c], -1), np.concatenate([-s, s], -1)]
    return np.stack(rows, 1).astype(f)


def window_masks():
    i = np.arange(WIN)[:, None] + WIN
    j = np.arange(KEYS)[None, :]
    m = np.where((i < j) | (i > j + WIN), MASKED, 0.0)
    inner = np.tile(m, (WPT, 1))
    first = inner.copy()
    first[:WIN, :WIN] = MASKED
    return np.ascontiguousarray(np.stack([inner, first], 1).astype(np.float32))


def slot_signs():
    r = (np.arange(P) // GD) % 4
    return np.ascontiguousarray(np.stack([-(r % 2 == 1), -(r >= 2)], 1).astype(np.float32) if False else
                                np.stack([np.where(r % 2 == 1, -1.0, 0.0), np.where(r >= 2, -1.0, 0.0)], 1).astype(np.float32))


def selectors():
    s = np.zeros((P, 2, GROUPS, P), np.float32)
    for g in range(GROUPS):
        for i in range(HPG):
            for d in range(GD):
                m = (HPG * g + i) * GD + d
                s[32 * i + d, 0, g, m] = 1.0
                s[32 * i + GD, 1, g, m] = 1.0
    return s


_INS = ['L0_attn_x', 'L0_attn_Wq', 'L0_attn_Wk', 'L0_attn_Wv', 'L0_attn_Wo', 'L0_ffn_Wqkv', 'L0_ffn_q_scale',
        'L0_ffn_k_scale', 'L0_ffn_Wo', 'L0_ffn_ln_g', 'L0_ffn_ln_b', 'L0_ffn_W1', 'L0_ffn_b1', 'L0_ffn_W2', 'L0_ffn_b2']


def kernel(**inputs):
    import concourse.bacc as bacc
    from concourse.bass_utils import run_bass_kernel_spmd

    nc = bacc.Bacc("TRN2", target_bir_lowering=False, num_devices=1)
    arrays, args = {}, []
    for name in _INS:
        arrays[f"in_{name}"] = np.ascontiguousarray(inputs[name])
    for name, a in (("rope", rope_tables()), ("ident", np.eye(P, dtype=np.float32)), ("mask", window_masks()),
                    ("slot", slot_signs()), ("sel", selectors())):
        arrays[f"const_{name}"] = a
    for name, a in arrays.items():
        args.append(nc.dram_tensor(name, a.shape, mybir.dt.from_np(a.dtype), kind="ExternalInput").ap())
    args.append(nc.dram_tensor("out", (BATCHES, SEQ, DIM), F32, kind="ExternalOutput").ap())
    build(nc, *args)
    r = run_bass_kernel_spmd(nc, [arrays], core_ids=[0])
    return r.results[0]["out"]
```

```python
import numpy as np
import concourse.bass as bass
from concourse import mybir
from contextlib import ExitStack

F32 = mybir.dt.float32
F16 = mybir.dt.float16
BF16 = mybir.dt.bfloat16
ALU = mybir.AluOpType
ACT = mybir.ActivationFunctionType
AX = mybir.AxisListType

P = 128
DIM = 128
BATCHES, SEQ = 4, 512
TOKENS = BATCHES * SEQ
DEPTH = 6
HEADS, DH, WIN = 16, 64, 32
INNER = HEADS * DH
PAIRS = HEADS // 2
TILES = SEQ // P
WPT = P // WIN
KEYS = 2 * WIN
CH = 512
HPC = CH // DH
W_SCALE = 64.0
NORM_FLOOR = (1e-12 * W_SCALE) ** 2
MASKED = -1e30
HID = int(DIM * 4 * 2 / 3)
FCH = [(0, 128), (128, 128), (256, HID - 256)]
LN_EPS = 1e-5
GH, GD = 16, 8
HPG = 4
GROUPS = GH // HPG
SIG_EPS = 1e-6

LAYER_TILES = BATCHES * TILES
TILE_LEAD, BATCH_LEAD, LAYER_LEAD = 4, 4, 1
TR_LEAD = 2


def tile_done(T, j=0, per=1):
    return (T + TILE_LEAD) * per + (j + 1)


def batch_done(B, j=0, per=1):
    return (B + BATCH_LEAD) * per + (j + 1)


def layer_done(L, j=0, per=1):
    return (L + LAYER_LEAD) * per + (j + 1)


def build(nc, x_in, gWq, gWk, gWv, gWo, Wqkv, q_scale, k_scale, Wo, ln_g, ln_b, W1, b1, W2, b2,
          rope_in, ident_in, mask_in, slot_in, sel_in, out):
    ctx = ExitStack()
    with ctx:
        def sb(name, shape, dt=F32):
            return ctx.enter_context(nc.sbuf_tensor(name, shape, dt))

        ident = sb("ident", [P, P])
        identb = sb("identb", [P, P], BF16)
        maskf = sb("maskf", [P, 2, KEYS])
        maskb = sb("maskb", [P, 2, KEYS], BF16)
        mean_w = sb("mean_w", [P, P])
        ones_w = sb("ones_w", [P, P])
        half_neg = sb("half_neg", [P, HPC])
        rope = sb("rope", [P, TILES, 4, DH])
        slot = sb("slot", [P, 2])
        sel = sb("sel", [P, 2, GROUPS, P])
        resid = sb("resid", [P, BATCHES, SEQ])
        xs = sb("xs", [P, BATCHES, SEQ])
        w_stage = sb("w_stage", [P, 3 * INNER])
        w_hi = sb("w_hi", [P, 3 * INNER], F16)
        w_lo = sb("w_lo", [P, 3 * INNER], F16)
        wo_sb = sb("wo_sb", [P, PAIRS, DIM])
        w1_sb = sb("w1_sb", [P, 2 * HID])
        w2_sb = sb("w2_sb", [P, 3, DIM])
        b1_sb = sb("b1_sb", [P, 2, 3])
        vec = sb("vec", [P, 3])
        qks = sb("qks", [P, 4, DH])
        table = sb("table", [P, TILES, 4, DH])
        in_hi = sb("in_hi", [P, WIN + SEQ], F16)
        in_lo = sb("in_lo", [P, WIN + SEQ], F16)
        raw = sb("raw", [P, 4, CH])
        sq = sb("sq", [P, 4, CH])
        n2 = sb("n2", [P, 4, HPC])
        n2f = sb("n2f", [P, 4, HPC])
        rn = sb("rn", [P, 4, HPC])
        t1 = sb("t1", [P, 2, CH])
        t2 = sb("t2", [P, 2, CH])
        rot = sb("rot", [P, 2, CH])
        qkn = sb("qkn", [P, 1, 4, CH])
        qT = sb("qT", [P, 2, PAIRS, P])
        kT = sb("kT", [P, 2, PAIRS, WIN + P])
        vw = sb("vw", [P, TILES, WPT, CH])
        smax = sb("smax", [P, 2, HPC])
        prob = sb("prob", [P, 2, PAIRS, 2, KEYS])
        psumr = sb("psumr", [P, 2, HEADS])
        rsum = sb("rsum", [P, 2, HEADS])
        pT = sb("pT", [P, PAIRS, P])
        on = sb("on", [P, PAIRS, 2, DH])
        oT = sb("oT", [P, PAIRS, SEQ])
        f_in = sb("f_in", [P, SEQ])
        xc = sb("xc", [P, SEQ])
        sqd = sb("sqd", [P, SEQ])
        veps = sb("veps", [P, TILES])
        rstd = sb("rstd", [P, TILES])
        diag = sb("diag", [P, TILES, P])
        xn = xc
        xg = sqd
        gel = sb("gel", [P, 2, SEQ])
        hid = sb("hid", [P, 3, SEQ])

        ps = [ctx.enter_context(nc.psum_tensor(f"ps{i}", [P, 512], F32)) for i in range(8)]
        proj, tr, sc, ov = ps[0:2], ps[2:4], ps[4:6], ps[6:8]

        def sem(name):
            return ctx.enter_context(nc.semaphore(name))

        loaded = sem("loaded")
        const_ready = sem("const_ready")
        tile_sems = {}

        def tsem(name, per):
            s = sem(name)
            tile_sems[name] = (s, per * TILE_LEAD)
            return s

        def bsem(name, per=1):
            s = sem(name)
            tile_sems[name] = (s, per * BATCH_LEAD)
            return s

        def lsem(name, credit):
            s = sem(name)
            tile_sems[name] = (s, credit)
            return s

        pe_qk = tsem("pe_qk", 4)
        pe_v = tsem("pe_v", 4)
        pe_tqk = tsem("pe_tqk", 4)
        pe_s = tsem("pe_s", 2)
        pe_tp = tsem("pe_tp", 2)
        pe_pv = tsem("pe_pv", 2)
        pe_to = tsem("pe_to", 2)
        act_sq = tsem("act_sq", 4)
        act_v = tsem("act_v", 4)
        act_tr = lsem("act_tr", TR_LEAD)
        act_exp = tsem("act_exp", 1)
        dve_n2 = tsem("dve_n2", 4)
        dve_rot = tsem("dve_rot", 4)
        dve_qkn = tsem("dve_qkn", 4)
        dve_max = tsem("dve_max", 2)
        dve_sub = tsem("dve_sub", 2)
        dve_sum = tsem("dve_sum", 1)
        dve_rs = tsem("dve_rs", 1)
        dve_on = tsem("dve_on", 2)
        pool_r = tsem("pool_r", 8)
        pool_add = tsem("pool_add", 4)
        pool_carry = tsem("pool_carry", 1)
        act_in = bsem("act_in", 2)
        dve_in = bsem("dve_in", 2)
        pe_wo = bsem("pe_wo")
        dve_x1 = bsem("dve_x1")
        act_fin = bsem("act_fin", 2)
        pe_mean = bsem("pe_mean")
        dve_xc = bsem("dve_xc")
        act_sqd = bsem("act_sqd")
        pe_var = bsem("pe_var")
        dve_veps = bsem("dve_veps")
        pool_rstd = bsem("pool_rstd")
        dve_diag = bsem("dve_diag")
        pe_rep = bsem("pe_rep")
        dve_xn = bsem("dve_xn")
        act_xg = bsem("act_xg")
        pe_gate = bsem("pe_gate", 3)
        pe_up = bsem("pe_up", 3)
        act_gelu = bsem("act_gelu", 3)
        dve_hid = bsem("dve_hid", 3)
        pe_w2 = bsem("pe_w2")
        dve_x2 = bsem("dve_x2")
        w_loaded = lsem("w_loaded", 16)
        f_loaded = lsem("f_loaded", 0)
        wo_loaded = lsem("wo_loaded", 0)
        t_loaded = lsem("t_loaded", 0)
        act_whi = lsem("act_whi", 6)
        dve_wlo = lsem("dve_wlo", 6)
        dve_tab = lsem("dve_tab", TILES)

        passed = {}

        def wait_apart(eng, semaphore, value):
            eng.wait_ge(semaphore, value)
            eng.sem_inc(passed[eng], 1)

        x_flat = x_in.rearrange("b (t p) d -> p (b t) d", p=P)
        n_x = BATCHES * TILES
        xtok = vw[:, :, :, :].rearrange("p a w c -> p (a w c)")[:, 0:n_x * DIM].rearrange("p (t d) -> p t d", d=DIM)
        gw_in = rope_tmp = w_stage[:, 0:4 * P].rearrange("p (k c) -> p k c", k=4)
        gwT = sb("gwT", [P, 4, P])
        passed_pe, passed_pool = sem("passed_pe"), sem("passed_pool")
        init_pe, init_act = sem("init_pe"), sem("init_act")

        with nc.Block() as block:
            @block.sync
            def _(sp):
                for s, credit in tile_sems.values():
                    if credit:
                        sp.sem_inc(s, credit)
                sp.dma_start(ident[:, :], ident_in).then_inc(loaded, 16)
                sp.dma_start(xtok, x_flat).then_inc(loaded, 16)
                for i, w in enumerate((gWq, gWk, gWv, gWo)):
                    sp.dma_start(gw_in[:, i, :], w).then_inc(loaded, 16)
                sp.dma_start(maskf[:, :, :], mask_in).then_inc(loaded, 16)
                sp.dma_start(rope[:, :, :, :], rope_in.rearrange("(t p) k d -> p t k d", p=P)).then_inc(loaded, 16)
                sp.dma_start(slot[:, :], slot_in).then_inc(loaded, 16)
                sp.dma_start(sel[:, :, :, :], sel_in).then_inc(loaded, 16)

            @block.gpsimd
            def _(pool):
                pool.memset(mean_w[:, :], 1.0 / DIM)
                pool.memset(ones_w[:, :], 1.0)
                pool.memset(half_neg[:, :], -0.5)
                pool.memset(in_hi[:, 0:WIN + 1], 0.0)
                pool.memset(in_lo[:, 0:WIN + 1], 0.0)
                pool.memset(f_in[:, 0:1], 0.0).then_inc(const_ready, 1)

            @block.vector
            def _(dve):
                dve.wait_ge(loaded, 160)
                dve.tensor_copy(identb[:, :], ident[:, :])
                dve.tensor_copy(maskb[:, :, :], maskf[:, :, :]).then_inc(const_ready, 1)

            @block.tensor
            def _(pe):
                pe.wait_ge(loaded, 160)
                for g in range(4):
                    if g >= 2:
                        pe.wait_ge(init_act, g - 1)
                    for i in range(4):
                        last = pe.transpose(tr[g % 2][:, i * P:(i + 1) * P], xtok[:, 4 * g + i, :], ident[:, :])
                    last.then_inc(init_pe, 1)
                pe.wait_ge(init_act, 3)
                for i in range(4):
                    last = pe.transpose(tr[0][:, i * P:(i + 1) * P], gw_in[:, i, :], ident[:, :])
                last.then_inc(init_pe, 1)

            @block.scalar
            def _(act):
                for g in range(4):
                    act.wait_ge(init_pe, g + 1)
                    act.activation(resid[:, g, :], tr[g % 2][:, :], ACT.Copy).then_inc(init_act, 1)
                act.wait_ge(init_pe, 5)
                act.activation(gwT[:, :, :], tr[0][:, :].rearrange("p (k c) -> p k c", k=4), ACT.Copy)
                act.activation(veps[:, 0:1], ident[:, 0:1], ACT.Copy).then_inc(init_act, 1)

        ln_pe, ln_dve, ln_act, ln_pool = sem("ln_pe"), sem("ln_dve"), sem("ln_act"), sem("ln_pool")

        class Norm:
            n = 0

        def norm_block(add_half, normed):
            base = Norm.n
            Norm.n += BATCHES
            with nc.Block() as block:
                @block.vector
                def _(dve):
                    for b in range(BATCHES):
                        k = 5 * (base + b)
                        if add_half:
                            dve.scalar_tensor_tensor(resid[:, b, :], xs[:, b, :], 0.5, resid[:, b, :],
                                                     ALU.mult, ALU.add).then_inc(ln_dve, 1)
                        else:
                            dve.engine_nop().then_inc(ln_dve, 1)
                        if not normed:
                            for _i in range(4):
                                dve.engine_nop().then_inc(ln_dve, 1)
                            continue
                        dve.wait_ge(ln_pe, 3 * (base + b) + 1)
                        dve.wait_ge(ln_dve, k + 1)
                        dve.tensor_tensor(xc[:, :], resid[:, b, :], proj[0][:, :], ALU.subtract).then_inc(ln_dve, 1)
                        dve.wait_ge(ln_pe, 3 * (base + b) + 2)
                        dve.tensor_scalar(veps[:, :], proj[1][:, 0:TILES], LN_EPS, None, ALU.add).then_inc(ln_dve, 1)
                        dve.wait_ge(ln_pool, base + b + 1)
                        dve.tensor_tensor(diag[:, :, :], ident[:, :].unsqueeze(1).broadcast_to([P, TILES, P]),
                                          rstd[:, :].unsqueeze(2).broadcast_to([P, TILES, P]),
                                          ALU.mult).then_inc(ln_dve, 1)
                        dve.wait_ge(ln_pe, 3 * (base + b) + 3)
                        dve.tensor_tensor(xs[:, b, :], xc[:, :], proj[0][:, :], ALU.mult).then_inc(ln_dve, 1)
                        dve.wait_ge(ln_dve, k + 5)
                if not normed:
                    return

                @block.scalar
                def _(act):
                    for b in range(BATCHES):
                        act.wait_ge(ln_dve, 5 * (base + b) + 2)
                        act.activation(sqd[:, :], xc[:, :], ACT.Square).then_inc(ln_act, 1)

                @block.gpsimd
                def _(pool):
                    for b in range(BATCHES):
                        pool.wait_ge(ln_dve, 5 * (base + b) + 3)
                        pool.tensor_tensor(rstd[:, :], veps[:, :], half_neg[:, 0:TILES], ALU.pow).then_inc(ln_pool, 1)

                @block.tensor
                def _(pe):
                    for b in range(BATCHES):
                        k = 5 * (base + b)
                        pe.wait_ge(ln_dve, k + 1)
                        pe.matmul(proj[0][:, :], mean_w[:, :], resid[:, b, :], start=True, stop=True).then_inc(ln_pe, 1)
                        pe.wait_ge(ln_act, base + b + 1)
                        for i in range(TILES):
                            last = pe.matmul(proj[1][:, i:i + 1], sqd[:, i * P:(i + 1) * P], mean_w[:, 0:1],
                                             start=True, stop=True)
                        last.then_inc(ln_pe, 1)
                        pe.wait_ge(ln_dve, k + 4)
                        pe.matmul(proj[0][:, :], ones_w[:, :], diag[:, :, :].rearrange("p t c -> p (t c)"),
                                  start=True, stop=True).then_inc(ln_pe, 1)

        def stack(half):
            L0 = half * DEPTH

            def dma_block(sp):
                with sp.Fori(0, DEPTH) as l:
                    L = l + L0
                    sp.wait_ge(dve_wlo, layer_done(L - 1, 5, 6))
                    sp.dma_start(w_stage[:, :], Wqkv[bass.ds(l, 1), :, :].rearrange("a p n -> p (a n)")).then_inc(w_loaded, 16)
                    sp.wait_ge(dve_tab, layer_done(L - 1, TILES - 1, TILES))
                    for i, src in enumerate((q_scale, k_scale)):
                        row = src[bass.ds(l, 1), :]
                        hd = DH // 2
                        sp.dma_start(qks[:, 2 * i, :], row.broadcast_to([P, DH])).then_inc(t_loaded, 16)
                        sp.dma_start(qks[:, 2 * i + 1, 0:hd], row[:, hd:DH].broadcast_to([P, hd])).then_inc(t_loaded, 16)
                        sp.dma_start(qks[:, 2 * i + 1, hd:DH], row[:, 0:hd].broadcast_to([P, hd])).then_inc(t_loaded, 16)
                    sp.wait_ge(pe_wo, batch_done(BATCHES * L - 1))
                    sp.dma_start(wo_sb[:, :, :], Wo[bass.ds(l, 1), :, :].rearrange("a (c p) n -> p (a c) n", p=P)).then_inc(wo_loaded, 16)
                    sp.wait_ge(dve_x2, batch_done(BATCHES * L - 1))
                    sp.dma_start(w1_sb[:, :], W1[bass.ds(l, 1), :, :].rearrange("a p n -> p (a n)")).then_inc(f_loaded, 16)
                    for f, (o, n) in enumerate(FCH):
                        sp.dma_start(w2_sb[0:n, f, :], W2[bass.ds(l, 1), o:o + n, :].rearrange("a p n -> p (a n)")).then_inc(f_loaded, 16)
                        for k in range(2):
                            sp.dma_start(b1_sb[0:n, k, f:f + 1],
                                         b1[bass.ds(l, 1), k * HID + o:k * HID + o + n].rearrange("a p -> p a")).then_inc(f_loaded, 16)
                    for i, src in enumerate((ln_g, ln_b, b2)):
                        sp.dma_start(vec[:, i:i + 1], src[bass.ds(l, 1), :].rearrange("a p -> p a")).then_inc(f_loaded, 16)

            F_DMAS = 1 + 3 * len(FCH) + 3
            T_DMAS = 6

            def pe_program(pe):
                passed[pe] = passed_pe

                def tr_fill(n):
                    pe.wait_ge(act_tr, n + (TR_LEAD - 1))

                def tqk(T, p, cs, n):
                    for c in cs:
                        tr_fill(n + c)
                        pe.wait_ge(dve_qkn, tile_done(T, c, 4))
                        for i in range(4):
                            last = pe.transpose(tr[c % 2][:, i * P:(i + 1) * P], qkn[:, 0, c, i * P:(i + 1) * P], ident[:, :])
                        last.then_inc(pe_tqk, 1)

                def three_pass(dst, cols, wcols):
                    pe.matmul(dst, in_hi[:, cols], wcols(w_hi), start=True, stop=False)
                    pe.matmul(dst, in_hi[:, cols], wcols(w_lo), start=False, stop=False)
                    return pe.matmul(dst, in_lo[:, cols], wcols(w_hi), start=False, stop=True)

                def a_qk(T, s, c, free):
                    for sm, v in free:
                        pe.wait_ge(sm, v)
                    cols = slice(WIN + s * P, WIN + (s + 1) * P)
                    three_pass(proj[c % 2][:, :], cols, lambda w: w[:, c * CH:(c + 1) * CH]).then_inc(pe_qk, 1)

                def values(T, s, windows, free=()):
                    for sm, v in free:
                        pe.wait_ge(sm, v)
                    for j in windows:
                        if j < 2:
                            pe.wait_ge(act_sq, tile_done(T, j + 2, 4))
                        else:
                            pe.wait_ge(act_v, tile_done(T, j - 2, 4))
                        cols = slice(WIN * (WPT * s + j), WIN * (WPT * s + j) + KEYS)
                        for par in range(2):
                            last = three_pass(proj[j % 2][par * KEYS:(par + 1) * KEYS, :], cols,
                                              lambda w: w[:, 2 * INNER:].rearrange("p (n a d) -> p n a d", a=2, d=DH)[:, :, par, :])
                        last.then_inc(pe_v, 1)

                def scores(T, s, par, n, free):
                    p = s % 2
                    for sm, v in free:
                        pe.wait_ge(sm, v)
                    pe.wait_ge(dve_sub, tile_done(T - 1, par, 2))
                    if par == 0:
                        pe.wait_ge(act_tr, n + TR_LEAD)
                        pe.wait_ge(pool_carry, tile_done(T))
                    pe.matmul(sc[par][:, :], identb[:, :],
                              maskb[:, 1 if s == 0 else 0, :].unsqueeze(1).broadcast_to([P, HPC, KEYS]),
                              start=True, stop=False, skip_group_check=True)
                    r = slice(par * DH, (par + 1) * DH)
                    for pair in range(PAIRS):
                        for w in range(WPT):
                            last = pe.matmul(sc[par][w * WIN:(w + 1) * WIN, pair * KEYS:(pair + 1) * KEYS],
                                             qT[r, p, pair, w * WIN:(w + 1) * WIN],
                                             kT[r, p, pair, w * WIN:w * WIN + KEYS],
                                             start=False, stop=True, skip_group_check=True)
                    last.then_inc(pe_s, 1)

                def tprob(T, p, n):
                    pe.wait_ge(act_exp, tile_done(T))
                    for g in range(2):
                        tr_fill(n + g)
                        for i in range(4):
                            last = pe.transpose(tr[g][:, i * P:(i + 1) * P],
                                                prob[:, p, 4 * g + i, :, :].rearrange("q a k -> q (a k)"), ident[:, :])
                        last.then_inc(pe_tp, 1)

                def outputs(T, v, par, n):
                    pe.wait_ge(dve_on, tile_done(T - 1, par, 2))
                    pe.wait_ge(act_tr, n + TR_LEAD)
                    wait_apart(pe, act_v, tile_done(T, WPT - 1, 4))
                    r = slice(par * KEYS, (par + 1) * KEYS)
                    for pair in range(PAIRS):
                        for w in range(WPT):
                            last = pe.matmul(ov[par][w * WIN:(w + 1) * WIN, pair * DH:(pair + 1) * DH],
                                             pT[r, pair, w * WIN:(w + 1) * WIN], vw[r, v, w, pair * DH:(pair + 1) * DH],
                                             start=True, stop=True, skip_group_check=True)
                    last.then_inc(pe_pv, 1)

                def tout(T, n):
                    pe.wait_ge(dve_on, tile_done(T, 1, 2))
                    for g in range(2):
                        tr_fill(n + g)
                        for i in range(4):
                            last = pe.transpose(tr[g][:, i * P:(i + 1) * P],
                                                on[:, 4 * g + i, :, :].rearrange("q a d -> q (a d)"), ident[:, :])
                        last.then_inc(pe_to, 1)

                def f_wo(B, free, n):
                    b, L = B
                    pe.wait_ge(wo_loaded, (L + 1) * 16)
                    for sm, v in free:
                        pe.wait_ge(sm, v)
                    pe.wait_ge(act_tr, n)
                    for c in range(PAIRS):
                        last = pe.matmul(proj[1][:, :], wo_sb[:, c, :], oT[:, c, :], start=c == 0, stop=c == PAIRS - 1)
                    last.then_inc(pe_wo, 1)

                def f_mean(B, T):
                    pe.wait_ge(dve_sub, tile_done(T, 0, 2))
                    pe.wait_ge(act_fin, batch_done(B, 1, 2))
                    pe.matmul(sc[0][:, :], mean_w[:, :], f_in[:, :], start=True, stop=True).then_inc(pe_mean, 1)

                def f_var(B, T):
                    pe.wait_ge(dve_sub, tile_done(T, 1, 2))
                    pe.wait_ge(act_sqd, batch_done(B))
                    for i in range(TILES):
                        last = pe.matmul(sc[1][:, i:i + 1], sqd[:, i * P:(i + 1) * P], mean_w[:, 0:1], start=True, stop=True)
                    last.then_inc(pe_var, 1)

                def f_rep(B, T):
                    pe.wait_ge(dve_sub, tile_done(T, 0, 2))
                    pe.wait_ge(dve_diag, batch_done(B))
                    pe.matmul(sc[0][:, :], ones_w[:, :], diag[:, :, :].rearrange("p t c -> p (t c)"),
                              start=True, stop=True).then_inc(pe_rep, 1)

                def f_hid(B, f, free=()):
                    o, n = FCH[f]
                    pe.wait_ge(act_xg, batch_done(B))
                    for k, (bank, done) in enumerate(((HID, pe_gate), (0, pe_up))):
                        if f:
                            pe.wait_ge(*((act_gelu, batch_done(B, f - 1, 3)), (dve_hid, batch_done(B, f - 1, 3)))[k])
                        elif free:
                            pe.wait_ge(*free[k])
                        pe.matmul(proj[k][0:n, :], w1_sb[:, bank + o:bank + o + n], xg[:, :], start=True, stop=True).then_inc(done, 1)

                def f_w2(B, T):
                    pe.wait_ge(dve_sub, tile_done(T, 0, 2))
                    pe.wait_ge(dve_hid, batch_done(B, 2, 3))
                    for f, (o, n) in enumerate(FCH):
                        last = pe.matmul(sc[0][:, :], w2_sb[0:n, f, :], hid[0:n, f, :], start=f == 0, stop=f == 2)
                    last.then_inc(pe_w2, 1)

                def step(L, new_layer, B, T, s, n, has_a, has1, has2, has3, ff, tail):
                    B, Lf = B
                    free_s0 = free_s1 = free_v0 = free_v1 = ()
                    if tail and s in (0, 4):
                        free_s0 = [(dve_xn, batch_done(B - 2))]
                        free_s1 = [(dve_veps, batch_done(B - 2))]
                    if tail and s == 1:
                        free_v0 = [(act_gelu, batch_done(B - 2, 2, 3))]
                        free_v1 = [(dve_hid, batch_done(B - 2, 2, 3))]
                    if tail and s == 2:
                        free_s0 = [(dve_x2, batch_done(B - 2))]
                    if ff and s == 2:
                        free_v1 = [(dve_x1, batch_done(B - 1))]
                    if ff and s == 3:
                        free_s0 = [(dve_xc, batch_done(B - 1))]
                    n_out = n + (2 if has3 else 0)
                    n_qk = n_out + (4 if has1 else 0)
                    n_prob = n_qk + (2 if has2 else 0)

                    def a(*cs):
                        for c in cs:
                            if has_a:
                                if s == 0 and c == 0:
                                    pe.wait_ge(dve_in, batch_done(B, 1, 2))
                                if new_layer:
                                    pe.wait_ge(dve_wlo, layer_done(L, c, 6))
                                a_qk(T, s, c, [(act_v, tile_done(T - 1, 2 + c, 4))] if c < 2 else [(act_sq, tile_done(T, c - 2, 4))])

                    def tq(*cs):
                        if has1:
                            tqk(T - 1, (s - 1) % 2, cs, n_out)

                    def pv(par):
                        if has2:
                            outputs(T - 2, (s - 2) % TILES, par, n_prob)

                    def sco0():
                        if has1:
                            scores(T - 1, (s - 1) % 4, 0, n_qk, free_s0)

                    def sco1():
                        if has2:
                            scores(T - 2, (s - 2) % 4, 1, None, free_s1)

                    def val(*js):
                        for j in js:
                            if has_a:
                                if new_layer:
                                    pe.wait_ge(dve_wlo, layer_done(L, 5, 6))
                                values(T, s, (j,), (free_v0, free_v1, (), ())[j])

                    if s:
                        a(0, 1)
                    sco1()
                    if has3:
                        tout(T - 3, n)
                    if s == 0:
                        a(0, 1)
                    a(2)
                    tq(0, 1)
                    if ff and s == 3:
                        f_mean(B - 1, T - 2)
                    if tail and s in (0, 4):
                        f_rep(B - 2, T - 2)
                    a(3)
                    tq(2, 3)

                    def tp():
                        if has2:
                            tprob(T - 2, s % 2, n_qk)

                    if tail and s in (1, 5):
                        f_hid(B - 2, 0, [(act_sq, tile_done(T, 2, 4)), (act_sq, tile_done(T, 3, 4))] if has_a else ())
                        sco0()
                        tp()
                        f_hid(B - 2, 1)
                        pv(0)
                        f_hid(B - 2, 2)
                        pv(1)
                        val(0, 1)
                        f_w2(B - 2, T - 1 if has1 else T - 2)
                        val(2, 3)
                    elif ff and s == 2:
                        val(0)
                        sco0()
                        tp()
                        f_wo((B - 1, Lf), [(act_sq, tile_done(T, 3, 4))], n_out + TR_LEAD)
                        pv(0)
                        pv(1)
                        val(1, 2, 3)
                    else:
                        val(0, 1)
                        sco0()
                        tp()
                        val(2, 3)
                        if ff and s == 3:
                            f_var(B - 1, T - 2)
                        pv(0)
                        pv(1)
                    return n_prob

                n_half = half * (8 * DEPTH * LAYER_TILES)

                def body(L, B, new_layer, started, Lf=None):
                    n = n_half if not started else n_half + (B - L0 * BATCHES) * 32 - 14
                    for s in range(4):
                        n = step(L, new_layer and s == 0, (B, Lf), B * TILES + s, s, n, True,
                                 started or s >= 1, started or s >= 2, started or s >= 3, started >= 1, started >= 2)

                body(L0, L0 * BATCHES, True, 0)
                body(L0, L0 * BATCHES + 1, False, 1, L0)
                with pe.Fori(2, BATCHES) as b:
                    body(L0, b + L0 * BATCHES, False, 2, L0)
                with pe.Fori(1, DEPTH) as l:
                    L = l + L0
                    body(L, L * BATCHES, True, 2, L - 1)
                    with pe.Fori(1, BATCHES) as b:
                        body(L, L * BATCHES + b, False, 2, L)
                n = n_half + 8 * DEPTH * LAYER_TILES - 14
                L = L0 + DEPTH - 1
                B = (L + 1) * BATCHES
                Te = B * TILES
                n = step(L, False, (B, L), Te, 4, n, False, True, True, True, False, True)
                n = step(L, False, (B, L), Te + 1, 5, n, False, False, True, True, False, True)
                n = step(L, False, (B, L), Te + 2, 6, n, False, False, False, True, False, False)
                f_wo((B - 1, L), [(dve_hid, batch_done(B - 2, 2, 3))], n + TR_LEAD)
                pe.wait_ge(dve_x2, batch_done(B - 2))
                f_mean(B - 1, Te - 1)
                f_var(B - 1, Te - 1)
                f_rep(B - 1, Te - 1)
                pe.wait_ge(dve_x1, batch_done(B - 1))
                for f in range(3):
                    f_hid(B - 1, f)
                f_w2(B - 1, Te - 1)

            def act_program(act):
                def squares(T, c):
                    act.wait_ge(pe_qk, tile_done(T, c, 4))
                    act.wait_ge(dve_rot, tile_done(T - 1, c, 4))
                    act.activation(raw[:, c, :], proj[c % 2][:, :], ACT.Copy)
                    act.activation(sq[:, c, :], proj[c % 2][:, :], ACT.Square).then_inc(act_sq, 1)

                def store_qk(T, s, cs):
                    p = s % 2
                    act.wait_ge(pe_s, tile_done(T - 2, 1, 2))
                    for c in cs:
                        act.wait_ge(pe_tqk, tile_done(T, c, 4))
                        src = tr[c % 2][:, :].rearrange("p (n t) -> p n t", n=4)
                        g = 4 * (c % 2)
                        if c == 2:
                            act.wait_ge(pool_carry, tile_done(T - 1))
                        dst = qT[:, p, g:g + 4, :] if c < 2 else kT[:, p, g:g + 4, WIN:WIN + P]
                        act.activation(dst, src, ACT.Copy).then_inc(act_tr, 1)

                def exps(T, p):
                    act.wait_ge(dve_sub, tile_done(T, 1, 2))
                    v = prob[:, p, :, :, :].rearrange("q n a k -> q (n a k)")
                    act.activation(v, v, ACT.Exp).then_inc(act_exp, 1)

                def store_v(T, p, windows):
                    act.wait_ge(pe_pv, tile_done(T - TILES, 1, 2))
                    for j in windows:
                        act.wait_ge(pe_v, tile_done(T, j, 4))
                        act.activation(vw[:, p, j, :], proj[j % 2][:, :], ACT.Copy, scale=1.0 / W_SCALE).then_inc(act_v, 1)

                def store_out(T, B, s):
                    act.wait_ge(pe_wo, batch_done(B - 1))
                    for g in range(2):
                        act.wait_ge(pe_to, tile_done(T, g, 2))
                        act.activation(oT[:, 4 * g:4 * g + 4, s * P:(s + 1) * P],
                                       tr[g][:, :].rearrange("p (n t) -> p n t", n=4), ACT.Copy).then_inc(act_tr, 1)

                def store_prob(T):
                    act.wait_ge(pe_pv, tile_done(T - 1, 1, 2))
                    for g in range(2):
                        act.wait_ge(pe_tp, tile_done(T, g, 2))
                        act.activation(pT[:, 4 * g:4 * g + 4, :],
                                       tr[g][:, :].rearrange("p (n t) -> p n t", n=4), ACT.Copy).then_inc(act_tr, 1)

                def f_input(B, xb):
                    act.wait_ge(dve_x1, batch_done(B))
                    act.wait_ge(dve_xc, batch_done(B - 1))
                    h = DIM // 2
                    act.activation(f_in[0:h, :], xs[0:h, xb, :], ACT.Copy).then_inc(act_fin, 1)
                    act.activation(f_in[h:DIM, 1:SEQ], xs[h:DIM, xb, 0:SEQ - 1], ACT.Copy).then_inc(act_fin, 1)

                def f_square(B, L):
                    act.wait_ge(f_loaded, (L + 1) * (16 * F_DMAS))
                    act.wait_ge(dve_xc, batch_done(B))
                    act.wait_ge(pe_up, batch_done(B - 1, 2, 3))
                    act.activation(sqd[:, :], xc[:, :], ACT.Square).then_inc(act_sqd, 1)

                def f_affine(B):
                    act.wait_ge(dve_xn, batch_done(B))
                    act.wait_ge(pe_var, batch_done(B))
                    act.activation(xg[:, :], xn[:, :], ACT.Identity, bias=vec[:, 1:2], scale=vec[:, 0:1]).then_inc(act_xg, 1)

                def f_gelu(B, *fs):
                    for f in fs:
                        o, n = FCH[f]
                        act.wait_ge(pe_gate, batch_done(B, f, 3))
                        act.wait_ge(dve_hid, batch_done(B, f - 2, 3))
                        act.activation(gel[0:n, f % 2, :], proj[0][0:n, :], ACT.Gelu, bias=b1_sb[0:n, 1, f:f + 1]).then_inc(act_gelu, 1)

                def split_in(B, xb):
                    act.wait_ge(dve_x2, batch_done(B - BATCHES))
                    act.wait_ge(pe_v, tile_done(B * TILES - 1, 3, 4))
                    h = DIM // 2
                    act.activation(in_hi[0:h, WIN:], xs[0:h, xb, :], ACT.Copy).then_inc(act_in, 1)
                    act.activation(in_hi[h:DIM, WIN + 1:], xs[h:DIM, xb, 0:SEQ - 1], ACT.Copy).then_inc(act_in, 1)

                def step(T, s, has_a, has1, has2, has3, ff, tail, B, xb, Lf):
                    def sq(c):
                        if has_a:
                            squares(T, c)

                    if s:
                        sq(0)
                        sq(1)
                    if has3:
                        store_out(T - 3, B if s == 3 else B - 1, (s - 3) % 4)
                    if s == 0:
                        sq(0)
                        sq(1)
                    sq(2)
                    if has1:
                        store_qk(T - 1, (s - 1) % 4, (0, 1))
                    sq(3)
                    if has1:
                        store_qk(T - 1, (s - 1) % 4, (2, 3))
                    if tail and s in (1, 5):
                        f_gelu(B - 2, 0)
                    if has2:
                        exps(T - 2, s % 2)
                    if ff and s == 3:
                        f_square(B - 1, Lf)
                    if tail and s in (0, 4):
                        f_affine(B - 2)
                    if tail and s in (1, 5):
                        if has2:
                            store_prob(T - 2)
                        f_gelu(B - 2, 1)
                        f_gelu(B - 2, 2)
                        if has_a:
                            store_v(T, s % 4, (0, 1, 2, 3))
                    elif ff and s == 2:
                        store_v(T, s % 4, (0,))
                        store_prob(T - 2)
                        store_v(T, s % 4, (1, 2, 3))
                        f_input(B - 1, xb)
                    else:
                        if has_a:
                            store_v(T, s % 4, (0, 1))
                        if has2:
                            store_prob(T - 2)
                        if has_a:
                            store_v(T, s % 4, (2, 3))

                def body(L, B, xb, new_layer, started, prev_xb=None, Lf=None):
                    if new_layer:
                        act.wait_ge(w_loaded, (L + 2) * 16)
                        act.wait_ge(pe_v, tile_done(B * TILES - 1, 3, 4))
                        for c in range(6):
                            act.activation(w_hi[:, c * CH:(c + 1) * CH], w_stage[:, c * CH:(c + 1) * CH], ACT.Copy,
                                           scale=W_SCALE).then_inc(act_whi, 1)
                    split_in(B, xb)
                    for s in range(4):
                        step(B * TILES + s, s, True, started or s >= 1, started or s >= 2, started or s >= 3, started >= 1,
                             started >= 2, B, prev_xb, Lf)

                body(L0, L0 * BATCHES, 0, True, 0)
                body(L0, L0 * BATCHES + 1, 1, False, 1, 0, L0)
                with act.Fori(2, BATCHES) as b:
                    body(L0, b + L0 * BATCHES, bass.ds(b, 1), False, 2, bass.ds(b - 1, 1), L0)
                with act.Fori(1, DEPTH) as l:
                    L = l + L0
                    body(L, L * BATCHES, 0, True, 2, BATCHES - 1, L - 1)
                    with act.Fori(1, BATCHES) as b:
                        body(L, L * BATCHES + b, bass.ds(b, 1), False, 2, bass.ds(b - 1, 1), L)
                B = (L0 + DEPTH) * BATCHES
                Te = B * TILES
                step(Te, 4, False, True, True, True, False, True, B, None, None)
                step(Te + 1, 5, False, False, True, True, False, True, B, None, None)
                store_out(Te - 1, B - 1, TILES - 1)
                f_input(B - 1, BATCHES - 1)
                f_square(B - 1, L0 + DEPTH - 1)
                f_affine(B - 1)
                f_gelu(B - 1, 0, 1, 2)

            def dve_program(dve):
                def bc(ap, n):
                    return ap.unsqueeze(2).broadcast_to([P, HPC, n])

                def rotary(T, s, c):
                    k = 0 if c < 2 else 2
                    hd = DH // 2
                    b = c % 2
                    dve.wait_ge(act_sq, tile_done(T, c, 4))
                    dve.wait_ge(pool_r, tile_done(T - 1, 2 * c, 8))
                    dve.tensor_reduce(n2[:, c, :], sq[:, c, :].rearrange("p (h d) -> p h d", d=DH),
                                      axis=AX.X, op=ALU.add).then_inc(dve_n2, 1)
                    dve.wait_ge(pool_add, tile_done(T, c - 2, 4))
                    src = raw[:, c, :].rearrange("p (h d) -> p h d", d=DH)
                    a1 = t1[:, b, :].rearrange("p (h d) -> p h d", d=DH)
                    a2 = t2[:, b, :].rearrange("p (h d) -> p h d", d=DH)
                    cos = table[:, s, k, :].unsqueeze(1).broadcast_to([P, HPC, DH])
                    sin = table[:, s, k + 1, :].unsqueeze(1).broadcast_to([P, HPC, DH])
                    dve.tensor_tensor(a1, src, cos, ALU.mult)
                    dve.tensor_tensor(a2[:, :, 0:hd], src[:, :, hd:DH], sin[:, :, 0:hd], ALU.mult)
                    dve.tensor_tensor(a2[:, :, hd:DH], src[:, :, 0:hd], sin[:, :, hd:DH], ALU.mult).then_inc(dve_rot, 1)

                def normalise(T, s, c):
                    dve.wait_ge(pool_add, tile_done(T, c, 4))
                    dve.wait_ge(pool_r, tile_done(T, 2 * c + 1, 8))
                    dve.wait_ge(pe_tqk, tile_done(T - 1, c, 4))
                    dve.tensor_tensor(qkn[:, 0, c, :].rearrange("p (h d) -> p h d", d=DH),
                                      rot[:, c % 2, :].rearrange("p (h d) -> p h d", d=DH), bc(rn[:, c, :], DH),
                                      ALU.mult).then_inc(dve_qkn, 1)

                def shift_max(T, p, par):
                    dve.wait_ge(pe_s, tile_done(T, par, 2))
                    dve.wait_ge(pe_tp, tile_done(T - 2, 1, 2))
                    dve.wait_ge(dve_sum, tile_done(T - 2))
                    if True:
                        src = sc[par][:, :].rearrange("q (n k) -> q n k", k=KEYS)
                        dve.wait_ge(dve_sub, tile_done(T - 1, par, 2))
                        dve.tensor_reduce(smax[:, par, :], src, axis=AX.X, op=ALU.max).then_inc(dve_max, 1)
                        dve.wait_ge(dve_max, tile_done(T, par, 2))
                        dve.tensor_tensor(prob[:, p, :, par, :], src, bc(smax[:, par, :], KEYS), ALU.subtract).then_inc(dve_sub, 1)

                def sums(T, p):
                    dve.wait_ge(act_exp, tile_done(T))
                    dve.wait_ge(dve_rs, tile_done(T - 2))
                    dve.tensor_reduce(psumr[:, p, :], prob[:, p, :, :, :].rearrange("q n a k -> q (n a) k"),
                                      axis=AX.X, op=ALU.add).then_inc(dve_sum, 1)
                    dve.wait_ge(dve_sum, tile_done(T))
                    dve.wait_ge(dve_on, tile_done(T - 2, 1, 2))
                    dve.reciprocal(rsum[:, p, :], psumr[:, p, :]).then_inc(dve_rs, 1)

                def out_norm(T, p):
                    dve.wait_ge(dve_rs, tile_done(T))
                    dve.wait_ge(pe_to, tile_done(T - 1, 1, 2))
                    for par in range(2):
                        dve.wait_ge(pe_pv, tile_done(T, par, 2))
                        dve.tensor_tensor(on[:, :, par, :], ov[par][:, :].rearrange("q (n d) -> q n d", d=DH),
                                          bc(rsum[:, p, :].rearrange("q (n a) -> q n a", a=2)[:, :, par], DH),
                                          ALU.mult).then_inc(dve_on, 1)

                def f_resid1(B, xb):
                    dve.wait_ge(pe_wo, batch_done(B))
                    dve.tensor_tensor(xs[:, xb, :], xs[:, xb, :], proj[1][:, :], ALU.add).then_inc(dve_x1, 1)

                def f_centre(B):
                    dve.wait_ge(pe_mean, batch_done(B))
                    dve.wait_ge(act_xg, batch_done(B - 1))
                    dve.tensor_tensor(xc[:, :], f_in[:, :], sc[0][:, :], ALU.subtract).then_inc(dve_xc, 1)

                def f_veps(B):
                    dve.wait_ge(pe_var, batch_done(B))
                    dve.wait_ge(pool_rstd, batch_done(B - 1))
                    dve.tensor_scalar(veps[:, :], sc[1][:, 0:TILES], LN_EPS, None, ALU.add).then_inc(dve_veps, 1)

                def f_diag(B):
                    dve.wait_ge(pool_rstd, batch_done(B))
                    dve.wait_ge(pe_rep, batch_done(B - 1))
                    dve.tensor_tensor(diag[:, :, :], ident[:, :].unsqueeze(1).broadcast_to([P, TILES, P]),
                                      rstd[:, :].unsqueeze(2).broadcast_to([P, TILES, P]), ALU.mult).then_inc(dve_diag, 1)

                def f_scale(B):
                    dve.wait_ge(pe_rep, batch_done(B))
                    dve.wait_ge(act_sqd, batch_done(B))
                    dve.tensor_tensor(xn[:, :], xc[:, :], sc[0][:, :], ALU.mult).then_inc(dve_xn, 1)

                def f_gated(B, fs):
                    dve.wait_ge(pe_w2, batch_done(B - 1))
                    for f in fs:
                        o, n = FCH[f]
                        dve.wait_ge(pe_up, batch_done(B, f, 3))
                        dve.wait_ge(act_gelu, batch_done(B, f, 3))
                        dve.scalar_tensor_tensor(hid[0:n, f, :], proj[1][0:n, :], b1_sb[0:n, 0, f:f + 1], gel[0:n, f % 2, :],
                                                 ALU.add, ALU.mult).then_inc(dve_hid, 1)

                def f_resid2(B, xb):
                    dve.wait_ge(pe_w2, batch_done(B))
                    dve.wait_ge(act_fin, batch_done(B, 1, 2))
                    dve.scalar_tensor_tensor(xs[:, xb, :], sc[0][:, :], vec[:, 2:3], xs[:, xb, :], ALU.add, ALU.add).then_inc(dve_x2, 1)

                def split_in(B, xb):
                    h = DIM // 2
                    dve.wait_ge(act_in, batch_done(B, 1, 2))
                    dve.tensor_tensor(in_lo[0:h, WIN:], xs[0:h, xb, :], in_hi[0:h, WIN:], ALU.subtract).then_inc(dve_in, 1)
                    dve.tensor_tensor(in_lo[h:DIM, WIN + 1:], xs[h:DIM, xb, 0:SEQ - 1], in_hi[h:DIM, WIN + 1:], ALU.subtract).then_inc(dve_in, 1)

                def step(T, s, has_a, has1, has2, ff, tail, B, xb, tail_xb):
                    def rot(c):
                        if has_a:
                            rotary(T, s, c)

                    def norm(*cs):
                        for c in cs:
                            if has_a:
                                normalise(T, s, c)

                    if s == 0 and has2:
                        shift_max(T - 2, 0, 1)
                    rot(0)
                    if s and has2:
                        shift_max(T - 2, s % 2, 1)
                    if tail and s in (0, 4):
                        f_diag(B - 2)
                    rot(1)
                    if tail and s in (2, 6):
                        f_resid2(B - 2, tail_xb)
                    if ff and s == 3:
                        f_centre(B - 1)
                    if tail and s in (0, 4):
                        f_scale(B - 2)
                    rot(2)
                    norm(0)
                    if tail and s in (1, 5):
                        f_gated(B - 2, (0,))
                    if has1:
                        shift_max(T - 1, (s - 1) % 2, 0)
                    rot(3)
                    norm(1)
                    if tail and s in (1, 5):
                        f_gated(B - 2, (1,))
                    if has2:
                        sums(T - 2, s % 2)
                    norm(2)
                    if tail and s in (1, 5):
                        f_gated(B - 2, (2,))
                    if ff and s == 3:
                        f_veps(B - 1)
                    if ff and s == 2:
                        norm(3)
                        f_resid1(B - 1, xb)
                    if has2:
                        out_norm(T - 2, s % 2)
                    if not (ff and s == 2):
                        norm(3)

                def body(L, B, xb, new_layer, started, prev_xb=None, tail_xb=None):
                    if new_layer:
                        for c in range(6):
                            dve.wait_ge(act_whi, layer_done(L, c, 6))
                            dve.scalar_tensor_tensor(w_lo[:, c * CH:(c + 1) * CH], w_stage[:, c * CH:(c + 1) * CH], W_SCALE,
                                                     w_hi[:, c * CH:(c + 1) * CH], ALU.mult, ALU.subtract).then_inc(dve_wlo, 1)
                    split_in(B, xb)
                    if new_layer:
                        dve.wait_ge(t_loaded, (L + 1) * (16 * T_DMAS))
                        dve.wait_ge(dve_rot, tile_done(B * TILES - 1, 3, 4))
                        for s in range(TILES):
                            dve.tensor_tensor(table[:, s, :, :], rope[:, s, :, :], qks[:, :, :], ALU.mult).then_inc(dve_tab, 1)
                        dve.wait_ge(dve_tab, layer_done(L, TILES - 1, TILES))
                    for s in range(4):
                        step(B * TILES + s, s, True, started or s >= 1, started or s >= 2, started >= 1, started >= 2,
                             B, prev_xb, tail_xb)

                body(L0, L0 * BATCHES, 0, True, 0)
                body(L0, L0 * BATCHES + 1, 1, False, 1, 0)
                with dve.Fori(2, BATCHES) as b:
                    body(L0, b + L0 * BATCHES, bass.ds(b, 1), False, 2, bass.ds(b - 1, 1), bass.ds(b - 2, 1))
                with dve.Fori(1, DEPTH) as l:
                    L = l + L0
                    body(L, L * BATCHES, 0, True, 2, BATCHES - 1, BATCHES - 2)
                    with dve.Fori(1, BATCHES) as b:
                        body(L, L * BATCHES + b, bass.ds(b, 1), False, 2, bass.ds(b - 1, 1), bass.ds((b + BATCHES - 2) & (BATCHES - 1), 1))
                B = (L0 + DEPTH) * BATCHES
                Te = B * TILES
                step(Te, 4, False, True, True, False, True, B, None, BATCHES - 2)
                step(Te + 1, 5, False, False, True, False, True, B, None, None)
                f_resid2(B - 2, BATCHES - 2)
                f_resid1(B - 1, BATCHES - 1)
                f_centre(B - 1)
                f_veps(B - 1)
                f_diag(B - 1)
                f_scale(B - 1)
                f_gated(B - 1, (0, 1, 2))
                f_resid2(B - 1, BATCHES - 1)

            def pool_program(pool):
                passed[pool] = passed_pool

                def chunk(T, c):
                    b = c % 2
                    pool.wait_ge(dve_n2, tile_done(T, c, 4))
                    wait_apart(pool, pool_r, tile_done(T - 1, 2 * c + 1, 8))
                    pool.tensor_scalar(n2f[:, c, :], n2[:, c, :], NORM_FLOOR, None, ALU.max).then_inc(pool_r, 1)
                    pool.wait_ge(pool_r, tile_done(T, 2 * c, 8))
                    pool.wait_ge(dve_qkn, tile_done(T - 1, c, 4))
                    pool.tensor_tensor(rn[:, c, :], n2f[:, c, :], half_neg[:, :], ALU.pow).then_inc(pool_r, 1)
                    pool.wait_ge(dve_rot, tile_done(T, c, 4))
                    pool.wait_ge(dve_qkn, tile_done(T, c - 2, 4))
                    pool.tensor_tensor(rot[:, c % 2, :], t1[:, b, :], t2[:, b, :], ALU.add).then_inc(pool_add, 1)

                def carry(T, s):
                    p = s % 2
                    wait_apart(pool, pe_s, tile_done(T - 2, 1, 2))
                    if s == 0:
                        pool.memset(kT[:, p, :, 0:WIN], 0.0).then_inc(pool_carry, 1)
                    else:
                        pool.tensor_copy(kT[:, p, :, 0:WIN], kT[:, 1 - p, :, P:P + WIN]).then_inc(pool_carry, 1)

                def f_rstd(B):
                    pool.wait_ge(dve_veps, batch_done(B))
                    pool.wait_ge(dve_diag, batch_done(B - 1))
                    pool.tensor_tensor(rstd[:, :], veps[:, :], half_neg[:, 0:TILES], ALU.pow).then_inc(pool_rstd, 1)

                def body(B, first):
                    T0 = B * TILES
                    for s in range(4):
                        T = T0 + s
                        chunk(T, 0)
                        chunk(T, 1)
                        if s:
                            fills = n_half + 4 if first and s == 1 else n_half + (B - L0 * BATCHES) * 32 + (8 * s - 8)
                            pool.wait_ge(act_tr, fills + TR_LEAD)
                        carry(T, s)
                        chunk(T, 2)
                        chunk(T, 3)
                        if s == 3 and not first:
                            f_rstd(B - 1)

                n_half = half * (8 * DEPTH * LAYER_TILES)
                body(L0 * BATCHES, True)
                with pool.Fori(1, DEPTH * BATCHES) as i:
                    body(i + L0 * BATCHES, False)
                f_rstd((L0 + DEPTH) * BATCHES - 1)

            with nc.Block() as block:
                block.sync(dma_block)
                block.tensor(pe_program)
                block.scalar(act_program)
                block.vector(dve_program)
                block.gpsimd(pool_program)

        g_pe_q, g_act_hi, g_dve_st = sem("g_pe_q"), sem("g_act_hi"), sem("g_dve_st")
        g_pe_v, g_act_v, g_pe_s, g_act_sig = sem("g_pe_v"), sem("g_act_v"), sem("g_pe_s"), sem("g_act_sig")
        g_pe_o, g_act_o, g_pe_nd, g_dve_r, g_pe_wo, g_dve_x = (sem(n) for n in ("g_pe_o", "g_act_o", "g_pe_nd", "g_dve_r", "g_pe_wo", "g_dve_x"))
        g_zero, g_act_w = sem("g_zero"), sem("g_act_w")

        def global_attention():
            qk_hi = qkn[:, 0, :, :]
            st = vw[:, :, :, :].bitcast(F16)
            q_st = st[:, 0, :, 0:SEQ]
            k_st = st[:, 1, :, 0:SEQ]
            hi16 = qk_hi.bitcast(F16)
            vaug = w_stage[:, 0:TILES * GH * 32].rearrange("p (t h c) -> p t h c", t=TILES, h=GH)
            sig = oT[:, 0:8, :].rearrange("p (a b) t -> p a b t", a=4)
            og = qT[:, :, :, :].rearrange("p a n t -> p (a n t)").rearrange("p (g t) -> p g t", g=GROUPS)
            gw_qk = rot[:, 0:2, :].rearrange("p k (g i r d) -> p k g i r d", g=GROUPS, i=HPG, r=4)
            num = t1[:, 0, :]
            rden = t1[:, 1, :]
            den = t2[:, 0, :]
            att = t2[:, 1, :]
            with nc.Block() as block:
                @block.gpsimd
                def _(pool):
                    pool.memset(vaug, 0.0).then_inc(g_zero, 1)
                    pool.wait_ge(g_zero, 1)
                    pool.memset(vaug[:, :, :, GD:GD + 1], 1.0).then_inc(g_zero, 1)

                @block.tensor
                def _(pe):
                    pe.wait_ge(g_zero, 2)
                    pe.wait_ge(g_act_w, 1)
                    for b in range(BATCHES):
                        for g in range(GROUPS):
                            for k in range(2):
                                i = 8 * b + 2 * g + k
                                if i >= 2:
                                    pe.wait_ge(g_dve_st, i - 1)
                                elif b:
                                    pe.wait_ge(g_dve_x, b)
                                if b and g == 0:
                                    pe.wait_ge(g_dve_x, b)
                                pe.matmul(ps[6 + k][:, :], gw_qk[:, k, g, :, :, :].rearrange("p i r d -> p (i r d)"),
                                          xs[:, b, :], start=True, stop=True).then_inc(g_pe_q, 1)
                        pe.wait_ge(g_dve_st, 8 * (b + 1) - 1)
                        for t in range(TILES):
                            last = pe.matmul(ps[6][:, t * P:(t + 1) * P], xs[:, b, t * P:(t + 1) * P], gwT[:, 2, :],
                                             start=True, stop=True)
                        last.then_inc(g_pe_v, 1)
                        pe.wait_ge(g_act_v, b + 1)
                        pe.wait_ge(g_dve_st, 8 * (b + 1))
                        units = [(g, t, h) for g in range(GROUPS) for t in range(TILES) for h in range(2)]

                        def score(u):
                            g, t, h = units[u]
                            n = len(units) * b + u
                            if n >= 2:
                                pe.wait_ge(g_act_sig, n - 1)
                            for j in range(2):
                                i = 2 * h + j
                                r = slice(32 * i, 32 * i + 32)
                                last = pe.matmul(ps[i][:, :], k_st[r, g, t * P:(t + 1) * P], q_st[r, g, :], start=True, stop=True)
                            last.then_inc(g_pe_s, 1)

                        def apply(u):
                            g, t, h = units[u]
                            n = len(units) * b + u
                            pe.wait_ge(g_act_sig, n + 1)
                            if t == 0 and h == 0 and GROUPS * b + g >= 2:
                                pe.wait_ge(g_act_o, GROUPS * b + g - 1)
                            for j in range(2):
                                i = 2 * h + j
                                last = pe.matmul(ps[4 + g % 2][32 * i:32 * i + 32, :], vaug[:, t, HPG * g + i, :],
                                                 sig[:, n % 4, j, :], start=t == 0, stop=t == TILES - 1,
                                                 skip_group_check=True)
                            last.then_inc(g_pe_o, 1)

                        for u in range(len(units) + 2):
                            if u < len(units):
                                score(u)
                            if u >= 2:
                                apply(u - 2)
                        pe.wait_ge(g_act_o, GROUPS * (b + 1))
                        for k in range(2):
                            for g in range(GROUPS):
                                last = pe.matmul(ps[6 + k][:, :], sel[:, k, g, :], og[:, g, :], start=g == 0, stop=g == GROUPS - 1)
                            last.then_inc(g_pe_nd, 1)
                        pe.wait_ge(g_dve_r, 3 * (b + 1))
                        pe.matmul(ps[6][:, :], gwT[:, 3, :], att, start=True, stop=True).then_inc(g_pe_wo, 1)

                @block.scalar
                def _(act):
                    for k in range(2):
                        for r in range(4):
                            last = act.activation(gw_qk[:, k, :, :, r, :],
                                                  gwT[:, k, :].rearrange("p (g i d) -> p g i d", g=GROUPS, i=HPG), ACT.Copy)
                    last.then_inc(g_act_w, 1)
                    for b in range(BATCHES):
                        for i in range(8 * b, 8 * b + 8):
                            act.wait_ge(g_pe_q, i + 1)
                            if i >= 2:
                                act.wait_ge(g_dve_st, i - 1)
                            act.activation(hi16[:, i % 2, 0:SEQ], ps[6 + i % 2][:, :], ACT.Copy).then_inc(g_act_hi, 1)
                        act.wait_ge(g_pe_v, b + 1)
                        act.activation(vaug[:, :, :, 0:GD], ps[6][:, :].rearrange("p (t h d) -> p t h d", t=TILES, h=GH),
                                       ACT.Copy).then_inc(g_act_v, 1)
                        for u in range(32):
                            n = 32 * b + u
                            act.wait_ge(g_pe_s, n + 1)
                            if n >= 4:
                                act.wait_ge(g_pe_o, n - 3)
                            h = u % 2
                            for j in range(2):
                                last = act.activation(sig[:, n % 4, j, :], ps[2 * h + j][:, :], ACT.Sigmoid, scale=GD ** -0.5)
                            last.then_inc(g_act_sig, 1)
                            if u % 8 == 7:
                                g = u // 8
                                act.wait_ge(g_pe_o, n + 1)
                                if g == 0 and b:
                                    act.wait_ge(g_pe_nd, 2 * b)
                                act.activation(og[:, g, :], ps[4 + g % 2][:, :], ACT.Copy).then_inc(g_act_o, 1)

                @block.vector
                def _(dve):
                    for b in range(BATCHES):
                        for i in range(8 * b, 8 * b + 8):
                            k = i % 2
                            g = (i // 2) % GROUPS
                            dve.wait_ge(g_act_hi, i + 1)
                            dve.scalar_tensor_tensor((q_st if k == 0 else k_st)[:, g, :], hi16[:, k, 0:SEQ], slot[:, k:k + 1],
                                                     ps[6 + k][:, :], ALU.mult, ALU.add).then_inc(g_dve_st, 1)
                        dve.wait_ge(g_pe_nd, 2 * b + 2)
                        dve.tensor_scalar(den, ps[7][:, :], SIG_EPS, None, ALU.add).then_inc(g_dve_r, 1)
                        dve.wait_ge(g_dve_r, 3 * b + 1)
                        dve.reciprocal(rden, den).then_inc(g_dve_r, 1)
                        dve.wait_ge(g_dve_r, 3 * b + 2)
                        dve.tensor_tensor(att, rden, ps[6][:, :], ALU.mult).then_inc(g_dve_r, 1)
                        dve.wait_ge(g_pe_wo, b + 1)
                        dve.tensor_tensor(resid[:, b, :], resid[:, b, :], ps[6][:, :], ALU.add).then_inc(g_dve_x, 1)
                    dve.wait_ge(g_dve_x, BATCHES)


        norm_block(False, True)
        norm_block_done = None
        stack(0)
        norm_block(True, True)
        global_attention()
        norm_block(False, True)
        stack(1)
        norm_block(True, False)

        fin_pe, fin_act, stored = sem("fin_pe"), sem("fin_act"), sem("stored")
        with nc.Block() as block:
            @block.tensor
            def _(pe):
                for g in range(4):
                    if g >= 2:
                        pe.wait_ge(fin_act, g - 1)
                    for i in range(4):
                        last = pe.transpose(tr[g % 2][:, i * P:(i + 1) * P], resid[:, g, i * P:(i + 1) * P], ident[:, :])
                    last.then_inc(fin_pe, 1)

            @block.scalar
            def _(act):
                for g in range(4):
                    act.wait_ge(fin_pe, g + 1)
                    act.activation(xtok[:, 4 * g:4 * g + 4, :], tr[g % 2][:, :].rearrange("p (t d) -> p t d", d=DIM),
                                   ACT.Copy).then_inc(fin_act, 1)

            @block.sync
            def _(sp):
                for g in range(4):
                    sp.wait_ge(fin_act, g + 1)
                    sp.dma_start(out[g, :, :].rearrange("(t p) d -> p t d", p=P), xtok[:, 4 * g:4 * g + 4, :]).then_inc(stored, 16)
                sp.wait_ge(stored, 64)


def rope_tables():
    f = np.float32
    half = np.arange(0, DH, 2, dtype=f)
    inv_freq = (f(1.0) / np.power(f(10000.0), half / f(DH))).astype(f)
    t = np.arange(SEQ, dtype=f)
    ang = (t[:, None] * inv_freq[None, :]).astype(f)
    base = ((half + f(0.4 * DH)) / f(1.4 * DH)).astype(f)
    power = ((t - SEQ // 2) / f(WIN // 2)).astype(f)
    scale = np.power(base[None, :].astype(np.float64), power[:, None])
    cos, sin = np.cos(ang.astype(np.float64)), np.sin(ang.astype(np.float64))
    rows = []
    for sc, mul in ((scale, 8.0), (1.0 / scale, 1.0)):
        c, s = cos * sc * mul, sin * sc * mul
        rows += [np.concatenate([c, c], -1), np.concatenate([-s, s], -1)]
    return np.stack(rows, 1).astype(f)


def window_masks():
    i = np.arange(WIN)[:, None] + WIN
    j = np.arange(KEYS)[None, :]
    m = np.where((i < j) | (i > j + WIN), MASKED, 0.0)
    inner = np.tile(m, (WPT, 1))
    first = inner.copy()
    first[:WIN, :WIN] = MASKED
    return np.ascontiguousarray(np.stack([inner, first], 1).astype(np.float32))


def slot_signs():
    r = (np.arange(P) // GD) % 4
    return np.ascontiguousarray(np.stack([-(r % 2 == 1), -(r >= 2)], 1).astype(np.float32) if False else
                                np.stack([np.where(r % 2 == 1, -1.0, 0.0), np.where(r >= 2, -1.0, 0.0)], 1).astype(np.float32))


def selectors():
    s = np.zeros((P, 2, GROUPS, P), np.float32)
    for g in range(GROUPS):
        for i in range(HPG):
            for d in range(GD):
                m = (HPG * g + i) * GD + d
                s[32 * i + d, 0, g, m] = 1.0
                s[32 * i + GD, 1, g, m] = 1.0
    return s


_INS = ['L0_attn_x', 'L0_attn_Wq', 'L0_attn_Wk', 'L0_attn_Wv', 'L0_attn_Wo', 'L0_ffn_Wqkv', 'L0_ffn_q_scale',
        'L0_ffn_k_scale', 'L0_ffn_Wo', 'L0_ffn_ln_g', 'L0_ffn_ln_b', 'L0_ffn_W1', 'L0_ffn_b1', 'L0_ffn_W2', 'L0_ffn_b2']


def kernel(**inputs):
    import concourse.bacc as bacc
    from concourse.bass_utils import run_bass_kernel_spmd

    nc = bacc.Bacc("TRN2", target_bir_lowering=False, num_devices=1)
    arrays, args = {}, []
    for name in _INS:
        arrays[f"in_{name}"] = np.ascontiguousarray(inputs[name])
    for name, a in (("rope", rope_tables()), ("ident", np.eye(P, dtype=np.float32)), ("mask", window_masks()),
                    ("slot", slot_signs()), ("sel", selectors())):
        arrays[f"const_{name}"] = a
    for name, a in arrays.items():
        args.append(nc.dram_tensor(name, a.shape, mybir.dt.from_np(a.dtype), kind="ExternalInput").ap())
    args.append(nc.dram_tensor("out", (BATCHES, SEQ, DIM), F32, kind="ExternalOutput").ap())
    build(nc, *args)
    r = run_bass_kernel_spmd(nc, [arrays], core_ids=[0])
    return r.results[0]["out"]
```

```python
import numpy as np
import concourse.bass as bass
from concourse import mybir
from contextlib import ExitStack

F32 = mybir.dt.float32
F16 = mybir.dt.float16
BF16 = mybir.dt.bfloat16
ALU = mybir.AluOpType
ACT = mybir.ActivationFunctionType
AX = mybir.AxisListType

P = 128
DIM = 128
BATCHES, SEQ = 4, 512
TOKENS = BATCHES * SEQ
DEPTH = 6
HEADS, DH, WIN = 16, 64, 32
INNER = HEADS * DH
PAIRS = HEADS // 2
TILES = SEQ // P
WPT = P // WIN
KEYS = 2 * WIN
CH = 512
HPC = CH // DH
W_SCALE = 64.0
NORM_FLOOR = (1e-12 * W_SCALE) ** 2
MASKED = -1e30
HID = int(DIM * 4 * 2 / 3)
FCH = [(0, 128), (128, 128), (256, HID - 256)]
LN_EPS = 1e-5
GH, GD = 16, 8
HPG = 4
GROUPS = GH // HPG
SIG_EPS = 1e-6

LAYER_TILES = BATCHES * TILES
TILE_LEAD, BATCH_LEAD, LAYER_LEAD = 4, 4, 1
TR_LEAD = 2


def tile_done(T, j=0, per=1):
    return (T + TILE_LEAD) * per + (j + 1)


def batch_done(B, j=0, per=1):
    return (B + BATCH_LEAD) * per + (j + 1)


def layer_done(L, j=0, per=1):
    return (L + LAYER_LEAD) * per + (j + 1)


def build(nc, x_in, gWq, gWk, gWv, gWo, Wqkv, q_scale, k_scale, Wo, ln_g, ln_b, W1, b1, W2, b2,
          rope_in, ident_in, mask_in, slot_in, sel_in, out):
    ctx = ExitStack()
    with ctx:
        def sb(name, shape, dt=F32):
            return ctx.enter_context(nc.sbuf_tensor(name, shape, dt))

        ident = sb("ident", [P, P])
        identb = sb("identb", [P, P], BF16)
        maskf = sb("maskf", [P, 2, KEYS])
        maskb = sb("maskb", [P, 2, KEYS], BF16)
        mean_w = sb("mean_w", [P, P])
        ones_w = sb("ones_w", [P, P])
        half_neg = sb("half_neg", [P, BATCHES * TILES])
        rope = sb("rope", [P, TILES, 4, DH])
        slot = sb("slot", [P, 2])
        sel = sb("sel", [P, 2, GROUPS, P])
        resid = sb("resid", [P, BATCHES, SEQ])
        xs = sb("xs", [P, BATCHES, SEQ])
        w_stage = sb("w_stage", [P, 3 * INNER])
        w_hi = sb("w_hi", [P, 3 * INNER], F16)
        w_lo = sb("w_lo", [P, 3 * INNER], F16)
        wo_sb = sb("wo_sb", [P, PAIRS, DIM])
        w1_sb = sb("w1_sb", [P, 2 * HID])
        w2_sb = sb("w2_sb", [P, 3, DIM])
        b1_sb = sb("b1_sb", [P, 2, 3])
        vec = sb("vec", [P, 3])
        qks = sb("qks", [P, 4, DH])
        table = sb("table", [P, TILES, 4, DH])
        in_hi = sb("in_hi", [P, WIN + SEQ], F16)
        in_lo = sb("in_lo", [P, WIN + SEQ], F16)
        raw = sb("raw", [P, 4, CH])
        sq = sb("sq", [P, 4, CH])
        n2 = sb("n2", [P, 4, HPC])
        n2f = sb("n2f", [P, 4, HPC])
        rn = sb("rn", [P, 4, HPC])
        t1 = sb("t1", [P, 2, CH])
        t2 = sb("t2", [P, 2, CH])
        rot = sb("rot", [P, 2, CH])
        qkn = sb("qkn", [P, 1, 4, CH])
        qT = sb("qT", [P, 2, PAIRS, P])
        kT = sb("kT", [P, 2, PAIRS, WIN + P])
        vw = sb("vw", [P, TILES, WPT, CH])
        smax = sb("smax", [P, 2, HPC])
        prob = sb("prob", [P, 2, PAIRS, 2, KEYS])
        psumr = sb("psumr", [P, 2, HEADS])
        rsum = sb("rsum", [P, 2, HEADS])
        pT = sb("pT", [P, PAIRS, P])
        on = sb("on", [P, PAIRS, 2, DH])
        oT = sb("oT", [P, PAIRS, SEQ])
        f_in = sb("f_in", [P, SEQ])
        xc = sb("xc", [P, SEQ])
        sqd = sb("sqd", [P, SEQ])
        veps = sb("veps", [P, TILES])
        rstd = sb("rstd", [P, TILES])
        diag = sb("diag", [P, TILES, P])
        xn = xc
        xg = sqd
        gel = sb("gel", [P, 2, SEQ])
        hid = sb("hid", [P, 3, SEQ])

        ps = [ctx.enter_context(nc.psum_tensor(f"ps{i}", [P, 512], F32)) for i in range(8)]
        proj, tr, sc, ov = ps[0:2], ps[2:4], ps[4:6], ps[6:8]

        def sem(name):
            return ctx.enter_context(nc.semaphore(name))

        loaded = sem("loaded")
        const_ready = sem("const_ready")
        credits = {}

        def credited(name, credit):
            s = sem(name)
            credits[name] = (s, credit)
            return s

        def tsem(name, per):
            return credited(name, per * TILE_LEAD)

        def bsem(name, per=1):
            return credited(name, per * BATCH_LEAD)

        def lsem(name, credit):
            return credited(name, credit)

        pe_qk = tsem("pe_qk", 4)
        pe_v = tsem("pe_v", 4)
        pe_tqk = tsem("pe_tqk", 4)
        pe_s = tsem("pe_s", 2)
        pe_tp = tsem("pe_tp", 2)
        pe_pv = tsem("pe_pv", 2)
        pe_to = tsem("pe_to", 2)
        act_sq = tsem("act_sq", 4)
        act_v = tsem("act_v", 4)
        act_tr = lsem("act_tr", TR_LEAD)
        act_exp = tsem("act_exp", 1)
        dve_n2 = tsem("dve_n2", 4)
        dve_rot = tsem("dve_rot", 4)
        dve_qkn = tsem("dve_qkn", 4)
        dve_max = tsem("dve_max", 2)
        dve_sub = tsem("dve_sub", 2)
        dve_sum = tsem("dve_sum", 1)
        dve_rs = tsem("dve_rs", 1)
        dve_on = tsem("dve_on", 2)
        pool_r = tsem("pool_r", 8)
        pool_add = tsem("pool_add", 4)
        pool_carry = tsem("pool_carry", 1)
        act_in = bsem("act_in", 2)
        dve_in = bsem("dve_in", 2)
        pe_wo = bsem("pe_wo")
        dve_x1 = bsem("dve_x1")
        act_fin = bsem("act_fin", 2)
        pe_mean = bsem("pe_mean")
        dve_xc = bsem("dve_xc")
        act_sqd = bsem("act_sqd")
        pe_var = bsem("pe_var")
        dve_veps = bsem("dve_veps")
        pool_rstd = bsem("pool_rstd")
        dve_diag = bsem("dve_diag")
        pe_rep = bsem("pe_rep")
        dve_xn = bsem("dve_xn")
        act_xg = bsem("act_xg")
        pe_gate = bsem("pe_gate", 3)
        pe_up = bsem("pe_up", 3)
        act_gelu = bsem("act_gelu", 3)
        dve_hid = bsem("dve_hid", 3)
        pe_w2 = bsem("pe_w2")
        dve_x2 = bsem("dve_x2")
        w_loaded = lsem("w_loaded", 16)
        f_loaded = lsem("f_loaded", 0)
        wo_loaded = lsem("wo_loaded", 0)
        t_loaded = lsem("t_loaded", 0)
        act_whi = lsem("act_whi", 6)
        dve_wlo = lsem("dve_wlo", 6)
        dve_tab = lsem("dve_tab", TILES)

        passed = {}

        def wait_apart(eng, semaphore, value):
            eng.wait_ge(semaphore, value)
            eng.sem_inc(passed[eng], 1)

        x_flat = x_in.rearrange("b (t p) d -> p (b t) d", p=P)
        n_x = BATCHES * TILES
        xtok = vw[:, :, :, :].rearrange("p a w c -> p (a w c)")[:, 0:n_x * DIM].rearrange("p (t d) -> p t d", d=DIM)
        gw_in = w_stage[:, 0:4 * P].rearrange("p (k c) -> p k c", k=4)
        gwT = sb("gwT", [P, 4, P])
        passed_pe, passed_pool = sem("passed_pe"), sem("passed_pool")
        init_pe, init_act = sem("init_pe"), sem("init_act")

        with nc.Block() as block:
            @block.sync
            def _(sp):
                for s, credit in credits.values():
                    if credit:
                        sp.sem_inc(s, credit)
                sp.dma_start(ident[:, :], ident_in).then_inc(loaded, 16)
                sp.dma_start(xtok, x_flat).then_inc(loaded, 16)
                for i, w in enumerate((gWq, gWk, gWv, gWo)):
                    sp.dma_start(gw_in[:, i, :], w).then_inc(loaded, 16)
                sp.dma_start(maskf[:, :, :], mask_in).then_inc(loaded, 16)
                sp.dma_start(rope[:, :, :, :], rope_in.rearrange("(t p) k d -> p t k d", p=P)).then_inc(loaded, 16)
                sp.dma_start(slot[:, :], slot_in).then_inc(loaded, 16)
                sp.dma_start(sel[:, :, :, :], sel_in).then_inc(loaded, 16)

            @block.gpsimd
            def _(pool):
                pool.memset(mean_w[:, :], 1.0 / DIM)
                pool.memset(ones_w[:, :], 1.0)
                pool.memset(half_neg[:, :], -0.5)
                pool.memset(in_hi[:, 0:WIN + 1], 0.0)
                pool.memset(in_lo[:, 0:WIN + 1], 0.0)
                pool.memset(f_in[:, 0:1], 0.0).then_inc(const_ready, 1)

            @block.vector
            def _(dve):
                dve.wait_ge(loaded, 160)
                dve.tensor_copy(identb[:, :], ident[:, :])
                dve.tensor_copy(maskb[:, :, :], maskf[:, :, :]).then_inc(const_ready, 1)

            @block.tensor
            def _(pe):
                pe.wait_ge(loaded, 160)
                for g in range(4):
                    if g >= 2:
                        pe.wait_ge(init_act, g - 1)
                    for i in range(4):
                        last = pe.transpose(tr[g % 2][:, i * P:(i + 1) * P], xtok[:, 4 * g + i, :], ident[:, :])
                    last.then_inc(init_pe, 1)
                pe.wait_ge(init_act, 3)
                for i in range(4):
                    last = pe.transpose(tr[0][:, i * P:(i + 1) * P], gw_in[:, i, :], ident[:, :])
                last.then_inc(init_pe, 1)

            @block.scalar
            def _(act):
                for g in range(4):
                    act.wait_ge(init_pe, g + 1)
                    act.activation(resid[:, g, :], tr[g % 2][:, :], ACT.Copy).then_inc(init_act, 1)
                act.wait_ge(init_pe, 5)
                act.activation(gwT[:, :, :], tr[0][:, :].rearrange("p (k c) -> p k c", k=4), ACT.Copy)
                act.activation(veps[:, 0:1], ident[:, 0:1], ACT.Copy).then_inc(init_act, 1)

        ln_pe, ln_dve, ln_act, ln_pool, ln_add = (sem(n) for n in ("ln_pe", "ln_dve", "ln_act", "ln_pool", "ln_add"))

        ln_done = [0, 0]
        vall = sb("vall", [P, BATCHES, TILES])
        rall = sb("rall", [P, BATCHES, TILES])

        def norm_block(add_half, normed):
            k_norm, k_add = ln_done
            ln_done[0] += normed
            ln_done[1] += add_half
            squares = [t1[:, 0, :], t1[:, 1, :], t2[:, 0, :], t2[:, 1, :]]
            dve_n, pe_n = 3 * BATCHES + 1, 2 * BATCHES + 1
            with nc.Block() as block:
                @block.vector
                def _(dve):
                    if add_half:
                        for b in range(BATCHES):
                            dve.scalar_tensor_tensor(resid[:, b, :], xs[:, b, :], 0.5, resid[:, b, :],
                                                     ALU.mult, ALU.add).then_inc(ln_add, 1)
                        if not normed:
                            dve.wait_ge(ln_add, BATCHES * (k_add + 1))
                            return
                    for b in range(BATCHES):
                        dve.wait_ge(ln_pe, pe_n * k_norm + b + 1)
                        if add_half:
                            dve.wait_ge(ln_add, BATCHES * k_add + b + 1)
                        dve.tensor_tensor(xs[:, b, :], resid[:, b, :], ps[b][:, :], ALU.subtract).then_inc(ln_dve, 1)
                    dve.wait_ge(ln_pe, pe_n * k_norm + BATCHES + 1)
                    dve.tensor_scalar(vall[:, :, :], ps[4][:, 0:BATCHES * TILES].rearrange("p (b t) -> p b t", b=BATCHES),
                                      LN_EPS, None, ALU.add).then_inc(ln_dve, 1)
                    dve.wait_ge(ln_pool, k_norm + 1)
                    for b in range(BATCHES):
                        dve.tensor_tensor(sq[:, b, :].rearrange("p (t c) -> p t c", t=TILES),
                                          ident[:, :].unsqueeze(1).broadcast_to([P, TILES, P]),
                                          rall[:, b, :].unsqueeze(2).broadcast_to([P, TILES, P]),
                                          ALU.mult).then_inc(ln_dve, 1)
                    for b in range(BATCHES):
                        dve.wait_ge(ln_pe, pe_n * k_norm + BATCHES + 2 + b)
                        dve.wait_ge(ln_dve, dve_n * k_norm + b + 1)
                        dve.tensor_tensor(xs[:, b, :], xs[:, b, :], ps[b][:, :], ALU.mult).then_inc(ln_dve, 1)
                    dve.wait_ge(ln_dve, dve_n * (k_norm + 1))
                if not normed:
                    return

                @block.scalar
                def _(act):
                    for b in range(BATCHES):
                        act.wait_ge(ln_dve, dve_n * k_norm + b + 1)
                        act.activation(squares[b], xs[:, b, :], ACT.Square).then_inc(ln_act, 1)

                @block.gpsimd
                def _(pool):
                    pool.wait_ge(ln_dve, dve_n * k_norm + BATCHES + 1)
                    pool.tensor_tensor(rall[:, :, :].rearrange("p b t -> p (b t)"), vall[:, :, :].rearrange("p b t -> p (b t)"),
                                       half_neg[:, :], ALU.pow).then_inc(ln_pool, 1)

                @block.tensor
                def _(pe):
                    for b in range(BATCHES):
                        if add_half:
                            pe.wait_ge(ln_add, BATCHES * k_add + b + 1)
                        pe.matmul(ps[b][:, :], mean_w[:, :], resid[:, b, :], start=True, stop=True).then_inc(ln_pe, 1)
                    for b in range(BATCHES):
                        pe.wait_ge(ln_act, BATCHES * k_norm + b + 1)
                        for i in range(TILES):
                            c = TILES * b + i
                            last = pe.matmul(ps[4][:, c:c + 1], squares[b][:, i * P:(i + 1) * P], mean_w[:, 0:1],
                                             start=True, stop=True)
                    last.then_inc(ln_pe, 1)
                    for b in range(BATCHES):
                        pe.wait_ge(ln_dve, dve_n * k_norm + BATCHES + 2 + b)
                        pe.matmul(ps[b][:, :], ones_w[:, :], sq[:, b, :], start=True, stop=True).then_inc(ln_pe, 1)

        def stack(half):
            L0 = half * DEPTH

            def dma_block(sp):
                with sp.Fori(0, DEPTH) as l:
                    L = l + L0
                    sp.wait_ge(dve_wlo, layer_done(L - 1, 5, 6))
                    sp.dma_start(w_stage[:, :], Wqkv[bass.ds(l, 1), :, :].rearrange("a p n -> p (a n)")).then_inc(w_loaded, 16)
                    sp.wait_ge(dve_tab, layer_done(L - 1, TILES - 1, TILES))
                    for i, src in enumerate((q_scale, k_scale)):
                        row = src[bass.ds(l, 1), :]
                        hd = DH // 2
                        sp.dma_start(qks[:, 2 * i, :], row.broadcast_to([P, DH])).then_inc(t_loaded, 16)
                        sp.dma_start(qks[:, 2 * i + 1, 0:hd], row[:, hd:DH].broadcast_to([P, hd])).then_inc(t_loaded, 16)
                        sp.dma_start(qks[:, 2 * i + 1, hd:DH], row[:, 0:hd].broadcast_to([P, hd])).then_inc(t_loaded, 16)
                    sp.wait_ge(pe_wo, batch_done(BATCHES * L - 1))
                    sp.dma_start(wo_sb[:, :, :], Wo[bass.ds(l, 1), :, :].rearrange("a (c p) n -> p (a c) n", p=P)).then_inc(wo_loaded, 16)
                    sp.wait_ge(dve_x2, batch_done(BATCHES * L - 1))
                    sp.dma_start(w1_sb[:, :], W1[bass.ds(l, 1), :, :].rearrange("a p n -> p (a n)")).then_inc(f_loaded, 16)
                    for f, (o, n) in enumerate(FCH):
                        sp.dma_start(w2_sb[0:n, f, :], W2[bass.ds(l, 1), o:o + n, :].rearrange("a p n -> p (a n)")).then_inc(f_loaded, 16)
                        for k in range(2):
                            sp.dma_start(b1_sb[0:n, k, f:f + 1],
                                         b1[bass.ds(l, 1), k * HID + o:k * HID + o + n].rearrange("a p -> p a")).then_inc(f_loaded, 16)
                    for i, src in enumerate((ln_g, ln_b, b2)):
                        sp.dma_start(vec[:, i:i + 1], src[bass.ds(l, 1), :].rearrange("a p -> p a")).then_inc(f_loaded, 16)

            F_DMAS = 1 + 3 * len(FCH) + 3
            T_DMAS = 6

            def pe_program(pe):
                passed[pe] = passed_pe

                def tr_fill(n):
                    pe.wait_ge(act_tr, n + (TR_LEAD - 1))

                def tqk(T, p, cs, n):
                    for c in cs:
                        tr_fill(n + c)
                        pe.wait_ge(dve_qkn, tile_done(T, c, 4))
                        for i in range(4):
                            last = pe.transpose(tr[c % 2][:, i * P:(i + 1) * P], qkn[:, 0, c, i * P:(i + 1) * P], ident[:, :])
                        last.then_inc(pe_tqk, 1)

                def three_pass(dst, cols, wcols):
                    pe.matmul(dst, in_hi[:, cols], wcols(w_hi), start=True, stop=False)
                    pe.matmul(dst, in_hi[:, cols], wcols(w_lo), start=False, stop=False)
                    return pe.matmul(dst, in_lo[:, cols], wcols(w_hi), start=False, stop=True)

                def a_qk(T, s, c, free):
                    for sm, v in free:
                        pe.wait_ge(sm, v)
                    cols = slice(WIN + s * P, WIN + (s + 1) * P)
                    three_pass(proj[c % 2][:, :], cols, lambda w: w[:, c * CH:(c + 1) * CH]).then_inc(pe_qk, 1)

                def values(T, s, windows, free=()):
                    for sm, v in free:
                        pe.wait_ge(sm, v)
                    for j in windows:
                        if j < 2:
                            pe.wait_ge(act_sq, tile_done(T, j + 2, 4))
                        else:
                            pe.wait_ge(act_v, tile_done(T, j - 2, 4))
                        cols = slice(WIN * (WPT * s + j), WIN * (WPT * s + j) + KEYS)
                        for par in range(2):
                            last = three_pass(proj[j % 2][par * KEYS:(par + 1) * KEYS, :], cols,
                                              lambda w: w[:, 2 * INNER:].rearrange("p (n a d) -> p n a d", a=2, d=DH)[:, :, par, :])
                        last.then_inc(pe_v, 1)

                def scores(T, s, par, n, free):
                    p = s % 2
                    for sm, v in free:
                        pe.wait_ge(sm, v)
                    pe.wait_ge(dve_sub, tile_done(T - 1, par, 2))
                    if par == 0:
                        pe.wait_ge(act_tr, n + TR_LEAD)
                        pe.wait_ge(pool_carry, tile_done(T))
                    pe.matmul(sc[par][:, :], identb[:, :],
                              maskb[:, 1 if s == 0 else 0, :].unsqueeze(1).broadcast_to([P, HPC, KEYS]),
                              start=True, stop=False, skip_group_check=True)
                    r = slice(par * DH, (par + 1) * DH)
                    for pair in range(PAIRS):
                        for w in range(WPT):
                            last = pe.matmul(sc[par][w * WIN:(w + 1) * WIN, pair * KEYS:(pair + 1) * KEYS],
                                             qT[r, p, pair, w * WIN:(w + 1) * WIN],
                                             kT[r, p, pair, w * WIN:w * WIN + KEYS],
                                             start=False, stop=True, skip_group_check=True)
                    last.then_inc(pe_s, 1)

                def tprob(T, p, n):
                    pe.wait_ge(act_exp, tile_done(T))
                    for g in range(2):
                        tr_fill(n + g)
                        for i in range(4):
                            last = pe.transpose(tr[g][:, i * P:(i + 1) * P],
                                                prob[:, p, 4 * g + i, :, :].rearrange("q a k -> q (a k)"), ident[:, :])
                        last.then_inc(pe_tp, 1)

                def outputs(T, v, par, n):
                    pe.wait_ge(dve_on, tile_done(T - 1, par, 2))
                    pe.wait_ge(act_tr, n + TR_LEAD)
                    wait_apart(pe, act_v, tile_done(T, WPT - 1, 4))
                    r = slice(par * KEYS, (par + 1) * KEYS)
                    for pair in range(PAIRS):
                        for w in range(WPT):
                            last = pe.matmul(ov[par][w * WIN:(w + 1) * WIN, pair * DH:(pair + 1) * DH],
                                             pT[r, pair, w * WIN:(w + 1) * WIN], vw[r, v, w, pair * DH:(pair + 1) * DH],
                                             start=True, stop=True, skip_group_check=True)
                    last.then_inc(pe_pv, 1)

                def tout(T, n):
                    pe.wait_ge(dve_on, tile_done(T, 1, 2))
                    for g in range(2):
                        tr_fill(n + g)
                        for i in range(4):
                            last = pe.transpose(tr[g][:, i * P:(i + 1) * P],
                                                on[:, 4 * g + i, :, :].rearrange("q a d -> q (a d)"), ident[:, :])
                        last.then_inc(pe_to, 1)

                def f_wo(B, free, n):
                    b, L = B
                    pe.wait_ge(wo_loaded, (L + 1) * 16)
                    for sm, v in free:
                        pe.wait_ge(sm, v)
                    pe.wait_ge(act_tr, n)
                    for c in range(PAIRS):
                        last = pe.matmul(proj[1][:, :], wo_sb[:, c, :], oT[:, c, :], start=c == 0, stop=c == PAIRS - 1)
                    last.then_inc(pe_wo, 1)

                def f_mean(B, T):
                    pe.wait_ge(dve_sub, tile_done(T, 0, 2))
                    pe.wait_ge(act_fin, batch_done(B, 1, 2))
                    pe.matmul(sc[0][:, :], mean_w[:, :], f_in[:, :], start=True, stop=True).then_inc(pe_mean, 1)

                def f_var(B, T):
                    pe.wait_ge(dve_sub, tile_done(T, 1, 2))
                    pe.wait_ge(act_sqd, batch_done(B))
                    for i in range(TILES):
                        last = pe.matmul(sc[1][:, i:i + 1], sqd[:, i * P:(i + 1) * P], mean_w[:, 0:1], start=True, stop=True)
                    last.then_inc(pe_var, 1)

                def f_rep(B, T):
                    pe.wait_ge(dve_sub, tile_done(T, 0, 2))
                    pe.wait_ge(dve_diag, batch_done(B))
                    pe.matmul(sc[0][:, :], ones_w[:, :], diag[:, :, :].rearrange("p t c -> p (t c)"),
                              start=True, stop=True).then_inc(pe_rep, 1)

                def f_hid(B, f, free=(), parts=(0, 1)):
                    o, n = FCH[f]
                    pe.wait_ge(act_xg, batch_done(B))
                    for k in parts:
                        bank, done = ((HID, pe_gate), (0, pe_up))[k]
                        if f:
                            pe.wait_ge(*((act_gelu, batch_done(B, f - 1, 3)), (dve_hid, batch_done(B, f - 1, 3)))[k])
                        elif free:
                            pe.wait_ge(*free[k])
                        pe.matmul(proj[k][0:n, :], w1_sb[:, bank + o:bank + o + n], xg[:, :], start=True, stop=True).then_inc(done, 1)

                def f_w2(B, T):
                    pe.wait_ge(dve_sub, tile_done(T, 0, 2))
                    pe.wait_ge(dve_hid, batch_done(B, 2, 3))
                    for f, (o, n) in enumerate(FCH):
                        last = pe.matmul(sc[0][:, :], w2_sb[0:n, f, :], hid[0:n, f, :], start=f == 0, stop=f == 2)
                    last.then_inc(pe_w2, 1)

                def step(L, new_layer, B, T, s, n, has_a, has1, has2, has3, ff, tail):
                    B, Lf = B
                    free_s0 = free_s1 = free_v0 = free_v1 = ()
                    if tail and s in (0, 4):
                        free_s0 = [(dve_xn, batch_done(B - 2))]
                        free_s1 = [(dve_veps, batch_done(B - 2))]
                    if tail and s == 1:
                        free_v0 = [(act_gelu, batch_done(B - 2, 2, 3))]
                        free_v1 = [(dve_hid, batch_done(B - 2, 2, 3))]
                    if tail and s == 2:
                        free_s0 = [(dve_x2, batch_done(B - 2))]
                    if ff and s == 2:
                        free_v1 = [(dve_x1, batch_done(B - 1))]
                    if ff and s == 3:
                        free_s0 = [(dve_xc, batch_done(B - 1))]
                    n_out = n + (2 if has3 else 0)
                    n_qk = n_out + (4 if has1 else 0)
                    n_prob = n_qk + (2 if has2 else 0)

                    def a(*cs):
                        for c in cs:
                            if has_a:
                                if s == 0 and c == 0:
                                    pe.wait_ge(dve_in, batch_done(B, 1, 2))
                                if new_layer:
                                    pe.wait_ge(dve_wlo, layer_done(L, c, 6))
                                a_qk(T, s, c, [(act_v, tile_done(T - 1, 2 + c, 4))] if c < 2 else [(act_sq, tile_done(T, c - 2, 4))])

                    def tq(*cs):
                        if has1:
                            tqk(T - 1, (s - 1) % 2, cs, n_out)

                    def pv(par):
                        if has2:
                            outputs(T - 2, (s - 2) % TILES, par, n_prob)

                    def sco0():
                        if has1:
                            scores(T - 1, (s - 1) % 4, 0, n_qk, free_s0)

                    def sco1():
                        if has2:
                            scores(T - 2, (s - 2) % 4, 1, None, free_s1)

                    def val(*js):
                        for j in js:
                            if has_a:
                                if new_layer:
                                    pe.wait_ge(dve_wlo, layer_done(L, 5, 6))
                                values(T, s, (j,), (free_v0, free_v1, (), ())[j])

                    a(0, 1)
                    sco1()
                    if has3:
                        tout(T - 3, n)
                    a(2)
                    tq(0, 1)
                    if ff and s == 3:
                        f_mean(B - 1, T - 2)
                    if tail and s in (0, 4):
                        f_rep(B - 2, T - 2)
                    a(3)
                    tq(2, 3)

                    def tp():
                        if has2:
                            tprob(T - 2, s % 2, n_qk)

                    if tail and s in (1, 5):
                        f_hid(B - 2, 0, [(act_sq, tile_done(T, 2, 4)), (act_sq, tile_done(T, 3, 4))] if has_a else ())
                        sco0()
                        tp()
                        f_hid(B - 2, 1)
                        pv(0)
                        f_hid(B - 2, 2, parts=(0,))
                        pv(1)
                        f_hid(B - 2, 2, parts=(1,))
                        val(0, 1)
                        f_w2(B - 2, T - 1 if has1 else T - 2)
                        val(2, 3)
                    elif ff and s == 2:
                        val(0)
                        sco0()
                        f_wo((B - 1, Lf), [(act_sq, tile_done(T, 3, 4))], n_out + TR_LEAD)
                        tp()
                        val(1)
                        pv(0)
                        val(2)
                        pv(1)
                        val(3)
                    else:
                        val(0, 1)
                        sco0()
                        if s == 3:
                            tp()
                            val(2, 3)
                            if ff:
                                f_var(B - 1, T - 2)
                            pv(0)
                            pv(1)
                        else:
                            tp()
                            val(2)
                            pv(0)
                            val(3)
                            pv(1)
                    return n_prob

                n_half = half * (8 * DEPTH * LAYER_TILES)

                def body(L, B, new_layer, started, Lf=None):
                    n = n_half if not started else n_half + (B - L0 * BATCHES) * 32 - 14
                    for s in range(4):
                        n = step(L, new_layer and s == 0, (B, Lf), B * TILES + s, s, n, True,
                                 started or s >= 1, started or s >= 2, started or s >= 3, started >= 1, started >= 2)

                body(L0, L0 * BATCHES, True, 0)
                body(L0, L0 * BATCHES + 1, False, 1, L0)
                with pe.Fori(2, BATCHES) as b:
                    body(L0, b + L0 * BATCHES, False, 2, L0)
                with pe.Fori(1, DEPTH) as l:
                    L = l + L0
                    body(L, L * BATCHES, True, 2, L - 1)
                    with pe.Fori(1, BATCHES) as b:
                        body(L, L * BATCHES + b, False, 2, L)
                n = n_half + 8 * DEPTH * LAYER_TILES - 14
                L = L0 + DEPTH - 1
                B = (L + 1) * BATCHES
                Te = B * TILES
                n = step(L, False, (B, L), Te, 4, n, False, True, True, True, False, True)
                n = step(L, False, (B, L), Te + 1, 5, n, False, False, True, True, False, True)
                n = step(L, False, (B, L), Te + 2, 6, n, False, False, False, True, False, False)
                f_wo((B - 1, L), [(dve_hid, batch_done(B - 2, 2, 3))], n + TR_LEAD)
                pe.wait_ge(dve_x2, batch_done(B - 2))
                f_mean(B - 1, Te - 1)
                f_var(B - 1, Te - 1)
                f_rep(B - 1, Te - 1)
                pe.wait_ge(dve_x1, batch_done(B - 1))
                for f in range(3):
                    f_hid(B - 1, f)
                f_w2(B - 1, Te - 1)

            def act_program(act):
                def squares(T, c):
                    act.wait_ge(pe_qk, tile_done(T, c, 4))
                    act.wait_ge(dve_rot, tile_done(T - 1, c, 4))
                    act.activation(raw[:, c, :], proj[c % 2][:, :], ACT.Copy)
                    act.activation(sq[:, c, :], proj[c % 2][:, :], ACT.Square).then_inc(act_sq, 1)

                def store_qk(T, s, cs):
                    p = s % 2
                    act.wait_ge(pe_s, tile_done(T - 2, 1, 2))
                    for c in cs:
                        act.wait_ge(pe_tqk, tile_done(T, c, 4))
                        src = tr[c % 2][:, :].rearrange("p (n t) -> p n t", n=4)
                        g = 4 * (c % 2)
                        if c == 2:
                            act.wait_ge(pool_carry, tile_done(T - 1))
                        dst = qT[:, p, g:g + 4, :] if c < 2 else kT[:, p, g:g + 4, WIN:WIN + P]
                        act.activation(dst, src, ACT.Copy).then_inc(act_tr, 1)

                def exps(T, p):
                    act.wait_ge(dve_sub, tile_done(T, 1, 2))
                    v = prob[:, p, :, :, :].rearrange("q n a k -> q (n a k)")
                    act.activation(v, v, ACT.Exp).then_inc(act_exp, 1)

                def store_v(T, p, windows):
                    act.wait_ge(pe_pv, tile_done(T - TILES, 1, 2))
                    for j in windows:
                        act.wait_ge(pe_v, tile_done(T, j, 4))
                        act.activation(vw[:, p, j, :], proj[j % 2][:, :], ACT.Copy, scale=1.0 / W_SCALE).then_inc(act_v, 1)

                def store_out(T, B, s):
                    act.wait_ge(pe_wo, batch_done(B - 1))
                    for g in range(2):
                        act.wait_ge(pe_to, tile_done(T, g, 2))
                        act.activation(oT[:, 4 * g:4 * g + 4, s * P:(s + 1) * P],
                                       tr[g][:, :].rearrange("p (n t) -> p n t", n=4), ACT.Copy).then_inc(act_tr, 1)

                def store_prob(T):
                    act.wait_ge(pe_pv, tile_done(T - 1, 1, 2))
                    for g in range(2):
                        act.wait_ge(pe_tp, tile_done(T, g, 2))
                        act.activation(pT[:, 4 * g:4 * g + 4, :],
                                       tr[g][:, :].rearrange("p (n t) -> p n t", n=4), ACT.Copy).then_inc(act_tr, 1)

                def f_input(B, xb):
                    act.wait_ge(dve_x1, batch_done(B))
                    act.wait_ge(dve_xc, batch_done(B - 1))
                    h = DIM // 2
                    act.activation(f_in[0:h, :], xs[0:h, xb, :], ACT.Copy).then_inc(act_fin, 1)
                    act.activation(f_in[h:DIM, 1:SEQ], xs[h:DIM, xb, 0:SEQ - 1], ACT.Copy).then_inc(act_fin, 1)

                def f_square(B, L):
                    act.wait_ge(f_loaded, (L + 1) * (16 * F_DMAS))
                    act.wait_ge(dve_xc, batch_done(B))
                    act.wait_ge(pe_up, batch_done(B - 1, 2, 3))
                    act.activation(sqd[:, :], xc[:, :], ACT.Square).then_inc(act_sqd, 1)

                def f_affine(B):
                    act.wait_ge(dve_xn, batch_done(B))
                    act.wait_ge(pe_var, batch_done(B))
                    act.activation(xg[:, :], xn[:, :], ACT.Identity, bias=vec[:, 1:2], scale=vec[:, 0:1]).then_inc(act_xg, 1)

                def f_gelu(B, *fs):
                    for f in fs:
                        o, n = FCH[f]
                        act.wait_ge(pe_gate, batch_done(B, f, 3))
                        act.wait_ge(dve_hid, batch_done(B, f - 2, 3))
                        act.activation(gel[0:n, f % 2, :], proj[0][0:n, :], ACT.Gelu, bias=b1_sb[0:n, 1, f:f + 1]).then_inc(act_gelu, 1)

                def split_in(B, xb):
                    act.wait_ge(dve_x2, batch_done(B - BATCHES))
                    act.wait_ge(pe_v, tile_done(B * TILES - 1, 3, 4))
                    h = DIM // 2
                    act.activation(in_hi[0:h, WIN:], xs[0:h, xb, :], ACT.Copy).then_inc(act_in, 1)
                    act.activation(in_hi[h:DIM, WIN + 1:], xs[h:DIM, xb, 0:SEQ - 1], ACT.Copy).then_inc(act_in, 1)

                def step(T, s, has_a, has1, has2, has3, ff, tail, B, xb, Lf):
                    def sq(c):
                        if has_a:
                            squares(T, c)

                    sq(0)
                    sq(1)
                    if has3:
                        store_out(T - 3, B if s == 3 else B - 1, (s - 3) % 4)
                    sq(2)
                    if has1:
                        store_qk(T - 1, (s - 1) % 4, (0, 1))
                    sq(3)
                    if has1:
                        store_qk(T - 1, (s - 1) % 4, (2, 3))
                    if has2:
                        exps(T - 2, s % 2)
                    if tail and s in (1, 5):
                        f_gelu(B - 2, 0)
                    if ff and s == 3:
                        f_square(B - 1, Lf)
                    if tail and s in (0, 4):
                        f_affine(B - 2)
                    if tail and s in (1, 5):
                        if has2:
                            store_prob(T - 2)
                        f_gelu(B - 2, 1)
                        f_gelu(B - 2, 2)
                        if has_a:
                            store_v(T, s % 4, (0, 1, 2, 3))
                    elif ff and s == 2:
                        store_v(T, s % 4, (0,))
                        store_prob(T - 2)
                        store_v(T, s % 4, (1, 2, 3))
                        f_input(B - 1, xb)
                    else:
                        if has_a:
                            store_v(T, s % 4, (0, 1))
                        if has2:
                            store_prob(T - 2)
                        if has_a:
                            store_v(T, s % 4, (2, 3))

                def body(L, B, xb, new_layer, started, prev_xb=None, Lf=None):
                    split_in(B, xb)
                    if new_layer:
                        act.wait_ge(w_loaded, (L + 2) * 16)
                        act.wait_ge(pe_v, tile_done(B * TILES - 1, 3, 4))
                        for c in range(6):
                            act.activation(w_hi[:, c * CH:(c + 1) * CH], w_stage[:, c * CH:(c + 1) * CH], ACT.Copy,
                                           scale=W_SCALE).then_inc(act_whi, 1)
                    for s in range(4):
                        step(B * TILES + s, s, True, started or s >= 1, started or s >= 2, started or s >= 3, started >= 1,
                             started >= 2, B, prev_xb, Lf)

                body(L0, L0 * BATCHES, 0, True, 0)
                body(L0, L0 * BATCHES + 1, 1, False, 1, 0, L0)
                with act.Fori(2, BATCHES) as b:
                    body(L0, b + L0 * BATCHES, bass.ds(b, 1), False, 2, bass.ds(b - 1, 1), L0)
                with act.Fori(1, DEPTH) as l:
                    L = l + L0
                    body(L, L * BATCHES, 0, True, 2, BATCHES - 1, L - 1)
                    with act.Fori(1, BATCHES) as b:
                        body(L, L * BATCHES + b, bass.ds(b, 1), False, 2, bass.ds(b - 1, 1), L)
                B = (L0 + DEPTH) * BATCHES
                Te = B * TILES
                step(Te, 4, False, True, True, True, False, True, B, None, None)
                step(Te + 1, 5, False, False, True, True, False, True, B, None, None)
                store_out(Te - 1, B - 1, TILES - 1)
                f_input(B - 1, BATCHES - 1)
                f_square(B - 1, L0 + DEPTH - 1)
                f_affine(B - 1)
                f_gelu(B - 1, 0, 1, 2)

            def dve_program(dve):
                def bc(ap, n):
                    return ap.unsqueeze(2).broadcast_to([P, HPC, n])

                def rotary(T, s, c):
                    k = 0 if c < 2 else 2
                    hd = DH // 2
                    b = c % 2
                    dve.wait_ge(act_sq, tile_done(T, c, 4))
                    dve.wait_ge(pool_r, tile_done(T - 1, 2 * c, 8))
                    dve.tensor_reduce(n2[:, c, :], sq[:, c, :].rearrange("p (h d) -> p h d", d=DH),
                                      axis=AX.X, op=ALU.add).then_inc(dve_n2, 1)
                    dve.wait_ge(pool_add, tile_done(T, c - 2, 4))
                    src = raw[:, c, :].rearrange("p (h d) -> p h d", d=DH)
                    a1 = t1[:, b, :].rearrange("p (h d) -> p h d", d=DH)
                    a2 = t2[:, b, :].rearrange("p (h d) -> p h d", d=DH)
                    cos = table[:, s, k, :].unsqueeze(1).broadcast_to([P, HPC, DH])
                    sin = table[:, s, k + 1, :].unsqueeze(1).broadcast_to([P, HPC, DH])
                    dve.tensor_tensor(a1, src, cos, ALU.mult)
                    dve.tensor_tensor(a2[:, :, 0:hd], src[:, :, hd:DH], sin[:, :, 0:hd], ALU.mult)
                    dve.tensor_tensor(a2[:, :, hd:DH], src[:, :, 0:hd], sin[:, :, hd:DH], ALU.mult).then_inc(dve_rot, 1)

                def normalise(T, s, c):
                    dve.wait_ge(pool_add, tile_done(T, c, 4))
                    dve.wait_ge(pool_r, tile_done(T, 2 * c + 1, 8))
                    dve.wait_ge(pe_tqk, tile_done(T - 1, c, 4))
                    dve.tensor_tensor(qkn[:, 0, c, :].rearrange("p (h d) -> p h d", d=DH),
                                      rot[:, c % 2, :].rearrange("p (h d) -> p h d", d=DH), bc(rn[:, c, :], DH),
                                      ALU.mult).then_inc(dve_qkn, 1)

                def shift_max(T, p, par):
                    dve.wait_ge(pe_s, tile_done(T, par, 2))
                    dve.wait_ge(pe_tp, tile_done(T - 2, 1, 2))
                    dve.wait_ge(dve_sum, tile_done(T - 2))
                    src = sc[par][:, :].rearrange("q (n k) -> q n k", k=KEYS)
                    dve.wait_ge(dve_sub, tile_done(T - 1, par, 2))
                    dve.tensor_reduce(smax[:, par, :], src, axis=AX.X, op=ALU.max).then_inc(dve_max, 1)
                    dve.wait_ge(dve_max, tile_done(T, par, 2))
                    dve.tensor_tensor(prob[:, p, :, par, :], src, bc(smax[:, par, :], KEYS), ALU.subtract).then_inc(dve_sub, 1)

                def sums(T, p):
                    dve.wait_ge(act_exp, tile_done(T))
                    dve.wait_ge(dve_rs, tile_done(T - 2))
                    dve.tensor_reduce(psumr[:, p, :], prob[:, p, :, :, :].rearrange("q n a k -> q (n a) k"),
                                      axis=AX.X, op=ALU.add).then_inc(dve_sum, 1)
                    dve.wait_ge(dve_sum, tile_done(T))
                    dve.wait_ge(dve_on, tile_done(T - 2, 1, 2))
                    dve.reciprocal(rsum[:, p, :], psumr[:, p, :]).then_inc(dve_rs, 1)

                def out_norm(T, p):
                    dve.wait_ge(dve_rs, tile_done(T))
                    dve.wait_ge(pe_to, tile_done(T - 1, 1, 2))
                    for par in range(2):
                        dve.wait_ge(pe_pv, tile_done(T, par, 2))
                        dve.tensor_tensor(on[:, :, par, :], ov[par][:, :].rearrange("q (n d) -> q n d", d=DH),
                                          bc(rsum[:, p, :].rearrange("q (n a) -> q n a", a=2)[:, :, par], DH),
                                          ALU.mult).then_inc(dve_on, 1)

                def f_resid1(B, xb):
                    dve.wait_ge(pe_wo, batch_done(B))
                    dve.tensor_tensor(xs[:, xb, :], xs[:, xb, :], proj[1][:, :], ALU.add).then_inc(dve_x1, 1)

                def f_centre(B):
                    dve.wait_ge(pe_mean, batch_done(B))
                    dve.wait_ge(act_xg, batch_done(B - 1))
                    dve.tensor_tensor(xc[:, :], f_in[:, :], sc[0][:, :], ALU.subtract).then_inc(dve_xc, 1)

                def f_veps(B):
                    dve.wait_ge(pe_var, batch_done(B))
                    dve.wait_ge(pool_rstd, batch_done(B - 1))
                    dve.tensor_scalar(veps[:, :], sc[1][:, 0:TILES], LN_EPS, None, ALU.add).then_inc(dve_veps, 1)

                def f_diag(B):
                    dve.wait_ge(pool_rstd, batch_done(B))
                    dve.wait_ge(pe_rep, batch_done(B - 1))
                    dve.tensor_tensor(diag[:, :, :], ident[:, :].unsqueeze(1).broadcast_to([P, TILES, P]),
                                      rstd[:, :].unsqueeze(2).broadcast_to([P, TILES, P]), ALU.mult).then_inc(dve_diag, 1)

                def f_scale(B):
                    dve.wait_ge(pe_rep, batch_done(B))
                    dve.wait_ge(act_sqd, batch_done(B))
                    dve.tensor_tensor(xn[:, :], xc[:, :], sc[0][:, :], ALU.mult).then_inc(dve_xn, 1)

                def f_gated(B, fs):
                    dve.wait_ge(pe_w2, batch_done(B - 1))
                    for f in fs:
                        o, n = FCH[f]
                        dve.wait_ge(pe_up, batch_done(B, f, 3))
                        dve.wait_ge(act_gelu, batch_done(B, f, 3))
                        dve.scalar_tensor_tensor(hid[0:n, f, :], proj[1][0:n, :], b1_sb[0:n, 0, f:f + 1], gel[0:n, f % 2, :],
                                                 ALU.add, ALU.mult).then_inc(dve_hid, 1)

                def f_resid2(B, xb):
                    dve.wait_ge(pe_w2, batch_done(B))
                    dve.wait_ge(act_fin, batch_done(B, 1, 2))
                    dve.scalar_tensor_tensor(xs[:, xb, :], sc[0][:, :], vec[:, 2:3], xs[:, xb, :], ALU.add, ALU.add).then_inc(dve_x2, 1)

                def split_in(B, xb):
                    h = DIM // 2
                    dve.wait_ge(act_in, batch_done(B, 1, 2))
                    dve.tensor_tensor(in_lo[0:h, WIN:], xs[0:h, xb, :], in_hi[0:h, WIN:], ALU.subtract).then_inc(dve_in, 1)
                    dve.tensor_tensor(in_lo[h:DIM, WIN + 1:], xs[h:DIM, xb, 0:SEQ - 1], in_hi[h:DIM, WIN + 1:], ALU.subtract).then_inc(dve_in, 1)

                def step(T, s, has_a, has1, has2, ff, tail, B, xb, tail_xb):
                    def rot(c):
                        if has_a:
                            rotary(T, s, c)

                    def norm(*cs):
                        for c in cs:
                            if has_a:
                                normalise(T, s, c)

                    rot(0)
                    if has2:
                        shift_max(T - 2, s % 2, 1)
                    rot(1)
                    if tail and s in (2, 6):
                        f_resid2(B - 2, tail_xb)
                    if ff and s == 3:
                        f_centre(B - 1)
                    if tail and s in (0, 4):
                        f_scale(B - 2)
                    rot(2)
                    norm(0)
                    if tail and s in (1, 5):
                        f_gated(B - 2, (0,))
                    if has1:
                        shift_max(T - 1, (s - 1) % 2, 0)
                    rot(3)
                    if tail and s in (1, 5):
                        f_gated(B - 2, (1,))
                    norm(1)
                    if s == 3:
                        return
                    if has2:
                        sums(T - 2, s % 2)
                    norm(2)
                    if tail and s in (1, 5):
                        f_gated(B - 2, (2,))
                    if ff and s == 2:
                        norm(3)
                        f_resid1(B - 1, xb)
                    if has2:
                        out_norm(T - 2, s % 2)
                    if not (ff and s == 2):
                        norm(3)

                def leftover(B, T, started):
                    if started >= 2:
                        f_veps(B - 2)
                    if started:
                        sums(T - 3, 1)
                        normalise(T - 1, 3, 2)
                        out_norm(T - 3, 1)
                        normalise(T - 1, 3, 3)
                    if started >= 2:
                        f_diag(B - 2)

                def split_w(L, *cs):
                    for c in cs:
                        dve.wait_ge(act_whi, layer_done(L, c, 6))
                        dve.scalar_tensor_tensor(w_lo[:, c * CH:(c + 1) * CH], w_stage[:, c * CH:(c + 1) * CH], W_SCALE,
                                                 w_hi[:, c * CH:(c + 1) * CH], ALU.mult, ALU.subtract).then_inc(dve_wlo, 1)

                def body(L, B, xb, new_layer, started, prev_xb=None, tail_xb=None):
                    split_in(B, xb)
                    if new_layer:
                        split_w(L, 0, 1)
                    leftover(B, B * TILES, started)
                    if new_layer:
                        split_w(L, 2, 3, 4, 5)
                        dve.wait_ge(t_loaded, (L + 1) * (16 * T_DMAS))
                        for s in range(TILES):
                            dve.tensor_tensor(table[:, s, :, :], rope[:, s, :, :], qks[:, :, :], ALU.mult).then_inc(dve_tab, 1)
                        dve.wait_ge(dve_tab, layer_done(L, TILES - 1, TILES))
                    for s in range(4):
                        step(B * TILES + s, s, True, started or s >= 1, started or s >= 2, started >= 1, started >= 2,
                             B, prev_xb, tail_xb)

                body(L0, L0 * BATCHES, 0, True, 0)
                body(L0, L0 * BATCHES + 1, 1, False, 1, 0)
                with dve.Fori(2, BATCHES) as b:
                    body(L0, b + L0 * BATCHES, bass.ds(b, 1), False, 2, bass.ds(b - 1, 1), bass.ds(b - 2, 1))
                with dve.Fori(1, DEPTH) as l:
                    L = l + L0
                    body(L, L * BATCHES, 0, True, 2, BATCHES - 1, BATCHES - 2)
                    with dve.Fori(1, BATCHES) as b:
                        body(L, L * BATCHES + b, bass.ds(b, 1), False, 2, bass.ds(b - 1, 1), bass.ds((b + BATCHES - 2) & (BATCHES - 1), 1))
                B = (L0 + DEPTH) * BATCHES
                Te = B * TILES
                leftover(B, Te, 2)
                step(Te, 4, False, True, True, False, True, B, None, BATCHES - 2)
                step(Te + 1, 5, False, False, True, False, True, B, None, None)
                f_resid2(B - 2, BATCHES - 2)
                f_resid1(B - 1, BATCHES - 1)
                f_centre(B - 1)
                f_veps(B - 1)
                f_diag(B - 1)
                f_scale(B - 1)
                f_gated(B - 1, (0, 1, 2))
                f_resid2(B - 1, BATCHES - 1)

            def pool_program(pool):
                passed[pool] = passed_pool

                def chunk(T, c):
                    b = c % 2
                    pool.wait_ge(dve_n2, tile_done(T, c, 4))
                    wait_apart(pool, pool_r, tile_done(T - 1, 2 * c + 1, 8))
                    pool.tensor_scalar(n2f[:, c, :], n2[:, c, :], NORM_FLOOR, None, ALU.max).then_inc(pool_r, 1)
                    pool.wait_ge(pool_r, tile_done(T, 2 * c, 8))
                    pool.wait_ge(dve_qkn, tile_done(T - 1, c, 4))
                    pool.tensor_tensor(rn[:, c, :], n2f[:, c, :], half_neg[:, 0:HPC], ALU.pow).then_inc(pool_r, 1)
                    pool.wait_ge(dve_rot, tile_done(T, c, 4))
                    pool.wait_ge(dve_qkn, tile_done(T, c - 2, 4))
                    pool.tensor_tensor(rot[:, c % 2, :], t1[:, b, :], t2[:, b, :], ALU.add).then_inc(pool_add, 1)

                def carry(T, s):
                    p = s % 2
                    wait_apart(pool, pe_s, tile_done(T - 2, 1, 2))
                    if s == 0:
                        pool.memset(kT[:, p, :, 0:WIN], 0.0).then_inc(pool_carry, 1)
                    else:
                        pool.tensor_copy(kT[:, p, :, 0:WIN], kT[:, 1 - p, :, P:P + WIN]).then_inc(pool_carry, 1)

                def f_rstd(B):
                    pool.wait_ge(dve_veps, batch_done(B))
                    pool.wait_ge(dve_diag, batch_done(B - 1))
                    pool.tensor_tensor(rstd[:, :], veps[:, :], half_neg[:, 0:TILES], ALU.pow).then_inc(pool_rstd, 1)

                def body(B, first):
                    T0 = B * TILES
                    for s in range(4):
                        T = T0 + s
                        chunk(T, 0)
                        chunk(T, 1)
                        if s:
                            fills = n_half + 4 if first and s == 1 else n_half + (B - L0 * BATCHES) * 32 + (8 * s - 8)
                            pool.wait_ge(act_tr, fills + TR_LEAD)
                        carry(T, s)
                        chunk(T, 2)
                        chunk(T, 3)
                        if s == 3 and not first:
                            f_rstd(B - 1)

                n_half = half * (8 * DEPTH * LAYER_TILES)
                body(L0 * BATCHES, True)
                with pool.Fori(1, DEPTH * BATCHES) as i:
                    body(i + L0 * BATCHES, False)
                f_rstd((L0 + DEPTH) * BATCHES - 1)

            with nc.Block() as block:
                block.sync(dma_block)
                block.tensor(pe_program)
                block.scalar(act_program)
                block.vector(dve_program)
                block.gpsimd(pool_program)

        g_pe_q, g_act_hi, g_dve_st = sem("g_pe_q"), sem("g_act_hi"), sem("g_dve_st")
        g_pe_v, g_act_v, g_pe_s, g_act_sig = sem("g_pe_v"), sem("g_act_v"), sem("g_pe_s"), sem("g_act_sig")
        g_pe_o, g_act_o, g_pe_nd, g_dve_r, g_pe_wo, g_dve_x = (sem(n) for n in ("g_pe_o", "g_act_o", "g_pe_nd", "g_dve_r", "g_pe_wo", "g_dve_x"))
        g_zero, g_act_w = sem("g_zero"), sem("g_act_w")

        def global_attention():
            hi16 = qkn[:, 0, :, :].bitcast(F16)
            store = vw[:, :, :, :].rearrange("p a w c -> p (a w c)")
            n_q, n_k, n_v = GROUPS * SEQ // 2, GROUPS * HPG * SEQ // 2, TILES * GH * 32
            q_st = store[:, 0:n_q].bitcast(F16).rearrange("p (g t) -> p g t", g=GROUPS)
            k_st = store[:, n_q:n_q + n_k].bitcast(F16).rearrange("p (g i t) -> p g i t", g=GROUPS, i=HPG)
            vaug = [w_stage[:, 0:n_v].rearrange("p (t h c) -> p t h c", t=TILES, h=GH),
                    store[:, n_q + n_k:n_q + n_k + n_v].rearrange("p (t h c) -> p t h c", t=TILES, h=GH)]
            sig = oT[:, 0:8, :].rearrange("p (a b) t -> p a b t", a=4)
            og = qT[:, :, :, :].rearrange("p a n t -> p (a n t)").rearrange("p (g t) -> p g t", g=GROUPS)
            gw_qk = rot[:, 0:2, :].rearrange("p k (g i r d) -> p k g i r d", g=GROUPS, i=HPG, r=4)
            rden = t1[:, 1, :]
            den = t2[:, 0, :]
            att = t2[:, 1, :]
            UNITS = GROUPS * TILES * 2
            PER_GROUP = TILES * 2
            STAGE_AT = {16: 0, 18: 1, 20: 2, 22: 3, 24: 4, 26: 5, 30: 6, 31: 7}
            V_AT, ND_AT, WO_AT = 28, 7, 15

            def unit(n):
                b, u = divmod(n, UNITS)
                return b, u // PER_GROUP, (u // 2) % TILES, u % 2

            with nc.Block() as block:
                @block.gpsimd
                def _(pool):
                    for v in vaug:
                        pool.memset(v, 0.0)
                    pool.memset(k_st, 0.0).then_inc(g_zero, 1)
                    pool.wait_ge(g_zero, 1)
                    for v in vaug:
                        last = pool.memset(v[:, :, :, GD:GD + 1], 1.0)
                    last.then_inc(g_zero, 1)

                @block.tensor
                def _(pe):
                    def project(b, j):
                        g, k = divmod(j, 2)
                        i = 8 * b + j
                        if i >= 2:
                            pe.wait_ge(g_dve_st, i - 1)
                        if b >= 2 and j < 2:
                            pe.wait_ge(g_dve_x, b - 1)
                        if b and j == 6:
                            pe.wait_ge(g_act_v, b + 1)
                        pe.matmul(ps[6 + k][:, :], gw_qk[:, k, g, :, :, :].rearrange("p i r d -> p (i r d)"),
                                  xs[:, b, :], start=True, stop=True).then_inc(g_pe_q, 1)

                    def value(b):
                        pe.wait_ge(g_dve_st, 8 * b + (5 if b else 7))
                        for t in range(TILES):
                            last = pe.matmul(ps[6][:, t * P:(t + 1) * P], xs[:, b, t * P:(t + 1) * P], gwT[:, 2, :],
                                             start=True, stop=True)
                        last.then_inc(g_pe_v, 1)

                    def score(n):
                        b, g, t, h = unit(n)
                        pe.wait_ge(g_dve_st, 8 * b + 2 * g + 2)
                        if n >= 2:
                            pe.wait_ge(g_act_sig, n - 1)
                        for j in range(2):
                            i = 2 * h + j
                            last = pe.matmul(ps[i][:, :], k_st[:, g, i, t * P:(t + 1) * P], q_st[:, g, :], start=True, stop=True)
                        last.then_inc(g_pe_s, 1)

                    def apply(n):
                        b, g, t, h = unit(n)
                        pe.wait_ge(g_act_v, b + 1)
                        pe.wait_ge(g_act_sig, n + 1)
                        if t == 0 and h == 0 and GROUPS * b + g >= 2:
                            pe.wait_ge(g_act_o, GROUPS * b + g - 1)
                        for j in range(2):
                            i = 2 * h + j
                            last = pe.matmul(ps[4 + g % 2][32 * i:32 * i + 32, :], vaug[b % 2][:, t, HPG * g + i, :],
                                             sig[:, n % 4, j, :], start=t == 0, stop=t == TILES - 1,
                                             skip_group_check=True)
                        last.then_inc(g_pe_o, 1)

                    def gather(b):
                        pe.wait_ge(g_act_o, GROUPS * (b + 1))
                        pe.wait_ge(g_dve_st, 8 * min(b + 2, BATCHES))
                        pe.wait_ge(g_act_v, min(b + 2, BATCHES))
                        if b:
                            pe.wait_ge(g_dve_x, b)
                        for k in (1, 0):
                            for g in range(GROUPS):
                                last = pe.matmul(ps[6 + k][:, :], sel[:, k, g, :], og[:, g, :], start=g == 0, stop=g == GROUPS - 1)
                            last.then_inc(g_pe_nd, 1)

                    def output(b):
                        pe.wait_ge(g_dve_r, 3 * (b + 1))
                        pe.matmul(ps[6][:, :], gwT[:, 3, :], att, start=True, stop=True).then_inc(g_pe_wo, 1)

                    pe.wait_ge(g_zero, 2)
                    pe.wait_ge(g_act_w, 1)
                    for j in range(8):
                        project(0, j)
                    value(0)
                    total = UNITS * BATCHES
                    for n in range(total + 2):
                        if n < total:
                            score(n)
                        if n >= 2:
                            apply(n - 2)
                        if n >= total:
                            continue
                        b, u = divmod(n, UNITS)
                        if b and u == ND_AT:
                            gather(b - 1)
                        if b and u == WO_AT:
                            output(b - 1)
                        if b + 1 < BATCHES and u in STAGE_AT:
                            project(b + 1, STAGE_AT[u])
                        if b + 1 < BATCHES and u == V_AT:
                            value(b + 1)
                    gather(BATCHES - 1)
                    output(BATCHES - 1)

                @block.scalar
                def _(act):
                    def high(b, j):
                        i = 8 * b + j
                        act.wait_ge(g_pe_q, i + 1)
                        if i >= 2:
                            act.wait_ge(g_dve_st, i - 1)
                        act.activation(hi16[:, i % 2, 0:SEQ], ps[6 + i % 2][:, :], ACT.Copy).then_inc(g_act_hi, 1)

                    def value(b):
                        act.wait_ge(g_pe_v, b + 1)
                        if b >= 2:
                            act.wait_ge(g_pe_o, UNITS * (b - 1))
                        act.activation(vaug[b % 2][:, :, :, 0:GD], ps[6][:, :].rearrange("p (t h d) -> p t h d", t=TILES, h=GH),
                                       ACT.Copy).then_inc(g_act_v, 1)

                    def collect(b, g):
                        act.wait_ge(g_pe_o, UNITS * b + PER_GROUP * (g + 1))
                        if g == 0 and b:
                            act.wait_ge(g_pe_nd, 2 * b)
                        act.activation(og[:, g, :], ps[4 + g % 2][:, :], ACT.Copy).then_inc(g_act_o, 1)

                    for k in range(2):
                        for r in range(4):
                            last = act.activation(gw_qk[:, k, :, :, r, :],
                                                  gwT[:, k, :].rearrange("p (g i d) -> p g i d", g=GROUPS, i=HPG), ACT.Copy)
                    last.then_inc(g_act_w, 1)
                    act.wait_ge(g_zero, 2)
                    for j in range(8):
                        high(0, j)
                    value(0)
                    for n in range(UNITS * BATCHES):
                        b, g, t, h = unit(n)
                        act.wait_ge(g_pe_s, n + 1)
                        if n >= 4:
                            act.wait_ge(g_pe_o, n - 3)
                        for j in range(2):
                            last = act.activation(sig[:, n % 4, j, :], ps[2 * h + j][:, :], ACT.Sigmoid, scale=GD ** -0.5)
                        last.then_inc(g_act_sig, 1)
                        u = n % UNITS
                        if n > 2 and u % PER_GROUP == 2:
                            collect(*divmod(n // PER_GROUP - 1, GROUPS))
                        if u >= 1 and b + 1 < BATCHES:
                            if u - 1 in STAGE_AT:
                                high(b + 1, STAGE_AT[u - 1])
                            if u - 1 == V_AT:
                                value(b + 1)
                        if u == UNITS - 1 and b + 1 < BATCHES:
                            high(b + 1, STAGE_AT[u])
                    collect(BATCHES - 1, GROUPS - 1)

                @block.vector
                def _(dve):
                    def split(b, j):
                        g, k = divmod(j, 2)
                        i = 8 * b + j
                        dve.wait_ge(g_act_hi, i + 1)
                        if b:
                            dve.wait_ge(g_pe_s, UNITS * (b - 1) + PER_GROUP * (g + 1))
                        if k == 0:
                            dve.scalar_tensor_tensor(q_st[:, g, :], hi16[:, 0, 0:SEQ], slot[:, 0:1], ps[6][:, :],
                                                     ALU.mult, ALU.add).then_inc(g_dve_st, 1)
                        else:
                            for h in range(HPG):
                                r = slice(32 * h, 32 * h + 32)
                                last = dve.scalar_tensor_tensor(k_st[r, g, h, :], hi16[r, 1, 0:SEQ], slot[r, 1:2], ps[7][r, :],
                                                                ALU.mult, ALU.add)
                            last.then_inc(g_dve_st, 1)

                    def normalise(b):
                        dve.wait_ge(g_pe_nd, 2 * b + 1)
                        dve.tensor_scalar(den, ps[7][:, :], SIG_EPS, None, ALU.add).then_inc(g_dve_r, 1)
                        dve.wait_ge(g_dve_r, 3 * b + 1)
                        dve.reciprocal(rden, den).then_inc(g_dve_r, 1)
                        dve.wait_ge(g_dve_r, 3 * b + 2)
                        dve.wait_ge(g_pe_nd, 2 * b + 2)
                        dve.tensor_tensor(att, rden, ps[6][:, :], ALU.mult).then_inc(g_dve_r, 1)
                        dve.wait_ge(g_pe_wo, b + 1)
                        dve.tensor_tensor(resid[:, b, :], resid[:, b, :], ps[6][:, :], ALU.add).then_inc(g_dve_x, 1)

                    dve.wait_ge(g_zero, 2)
                    for j in range(8):
                        split(0, j)
                    for b in range(BATCHES):
                        if b:
                            normalise(b - 1)
                        if b + 1 < BATCHES:
                            for j in range(8):
                                split(b + 1, j)
                    normalise(BATCHES - 1)
                    dve.wait_ge(g_dve_x, BATCHES)

        norm_block(False, True)
        stack(0)
        norm_block(True, True)
        global_attention()
        norm_block(False, True)
        stack(1)
        norm_block(True, False)

        fin_pe, fin_act, stored = sem("fin_pe"), sem("fin_act"), sem("stored")
        with nc.Block() as block:
            @block.tensor
            def _(pe):
                for g in range(4):
                    if g >= 2:
                        pe.wait_ge(fin_act, g - 1)
                    for i in range(4):
                        last = pe.transpose(tr[g % 2][:, i * P:(i + 1) * P], resid[:, g, i * P:(i + 1) * P], ident[:, :])
                    last.then_inc(fin_pe, 1)

            @block.scalar
            def _(act):
                for g in range(4):
                    act.wait_ge(fin_pe, g + 1)
                    act.activation(xtok[:, 4 * g:4 * g + 4, :], tr[g % 2][:, :].rearrange("p (t d) -> p t d", d=DIM),
                                   ACT.Copy).then_inc(fin_act, 1)

            @block.sync
            def _(sp):
                for g in range(4):
                    sp.wait_ge(fin_act, g + 1)
                    sp.dma_start(out[g, :, :].rearrange("(t p) d -> p t d", p=P), xtok[:, 4 * g:4 * g + 4, :]).then_inc(stored, 16)
                sp.wait_ge(stored, 64)


def rope_tables():
    f = np.float32
    half = np.arange(0, DH, 2, dtype=f)
    inv_freq = (f(1.0) / np.power(f(10000.0), half / f(DH))).astype(f)
    t = np.arange(SEQ, dtype=f)
    ang = (t[:, None] * inv_freq[None, :]).astype(f)
    base = ((half + f(0.4 * DH)) / f(1.4 * DH)).astype(f)
    power = ((t - SEQ // 2) / f(WIN // 2)).astype(f)
    scale = np.power(base[None, :].astype(np.float64), power[:, None])
    cos, sin = np.cos(ang.astype(np.float64)), np.sin(ang.astype(np.float64))
    rows = []
    for sc, mul in ((scale, 8.0), (1.0 / scale, 1.0)):
        c, s = cos * sc * mul, sin * sc * mul
        rows += [np.concatenate([c, c], -1), np.concatenate([-s, s], -1)]
    return np.stack(rows, 1).astype(f)


def window_masks():
    i = np.arange(WIN)[:, None] + WIN
    j = np.arange(KEYS)[None, :]
    m = np.where((i < j) | (i > j + WIN), MASKED, 0.0)
    inner = np.tile(m, (WPT, 1))
    first = inner.copy()
    first[:WIN, :WIN] = MASKED
    return np.ascontiguousarray(np.stack([inner, first], 1).astype(np.float32))


def slot_signs():
    r = (np.arange(P) // GD) % 4
    return np.ascontiguousarray(np.stack([np.where(r % 2 == 1, -1.0, 0.0), np.where(r >= 2, -1.0, 0.0)], 1).astype(np.float32))


def selectors():
    s = np.zeros((P, 2, GROUPS, P), np.float32)
    for g in range(GROUPS):
        for i in range(HPG):
            for d in range(GD):
                m = (HPG * g + i) * GD + d
                s[32 * i + d, 0, g, m] = 1.0
                s[32 * i + GD, 1, g, m] = 1.0
    return s


_INS = ['L0_attn_x', 'L0_attn_Wq', 'L0_attn_Wk', 'L0_attn_Wv', 'L0_attn_Wo', 'L0_ffn_Wqkv', 'L0_ffn_q_scale',
        'L0_ffn_k_scale', 'L0_ffn_Wo', 'L0_ffn_ln_g', 'L0_ffn_ln_b', 'L0_ffn_W1', 'L0_ffn_b1', 'L0_ffn_W2', 'L0_ffn_b2']


def kernel(**inputs):
    import concourse.bacc as bacc
    from concourse.bass_utils import run_bass_kernel_spmd

    nc = bacc.Bacc("TRN2", target_bir_lowering=False, num_devices=1)
    arrays, args = {}, []
    for name in _INS:
        arrays[f"in_{name}"] = np.ascontiguousarray(inputs[name])
    for name, a in (("rope", rope_tables()), ("ident", np.eye(P, dtype=np.float32)), ("mask", window_masks()),
                    ("slot", slot_signs()), ("sel", selectors())):
        arrays[f"const_{name}"] = a
    for name, a in arrays.items():
        args.append(nc.dram_tensor(name, a.shape, mybir.dt.from_np(a.dtype), kind="ExternalInput").ap())
    args.append(nc.dram_tensor("out", (BATCHES, SEQ, DIM), F32, kind="ExternalOutput").ap())
    build(nc, *args)
    r = run_bass_kernel_spmd(nc, [arrays], core_ids=[0])
    return r.results[0]["out"]
```
